# Optimizing a Trainium2 kernel written in Bass

```python
import numpy as np
import jax
import jax.numpy as jnp

def _softmax(x, axis=-1):
    return jax.nn.softmax(x, axis=axis)

def _gelu(x):
    return jax.nn.gelu(x, approximate=True)

def _silu(x):
    return jax.nn.silu(x)

def _sigmoid(x):
    return jax.nn.sigmoid(x)

def _layernorm(x, axis=-1, eps=1e-05):
    m = jnp.mean(x, axis=axis, keepdims=True)
    v = jnp.var(x, axis=axis, keepdims=True)
    return (x - m) / jnp.sqrt(v + eps)

def _scatter_add(tgt, idx, src, axis=0):
    return tgt.at[idx].add(src)

def _segment_sum(src, seg, n):
    return jax.ops.segment_sum(src, seg, n)
kernel_name = 'mk_gnn_ffn_d2_gnn_r8_2711c7'

def setup_inputs(seed: int=0):
    np.random.seed(seed)
    _w = jnp.asarray

    def _rec_inputs():
        import jax
        import jax.numpy as jnp
        _gk = jax.random.key(seed)
        x = -0.0003713 + 1 * jax.random.normal(jax.random.fold_in(_gk, 1), (12500, 256), jnp.float32)
        _s = jax.random.randint(jax.random.fold_in(_gk, 2), (100000,), 0, 12500, jnp.int32)
        _d = jax.random.randint(jax.random.fold_in(_gk, 3), (100000,), 0, 12500, jnp.int32)
        _loop = jnp.arange(12500, dtype=jnp.int32)
        src = jnp.concatenate([_s, _d, _loop])
        dst = jnp.concatenate([_d, _s, _loop])
        _o = jnp.argsort(dst, stable=True)
        src = src[_o]
        dst = dst[_o]
        return (x, src, dst)
    x, src, dst = _rec_inputs()

    def _L0_gnn_setup():
        import jax, jax.numpy as jnp
        import numpy as np
        N_NODES = 6250
        N_EDGES = 100000
        IN_DIM = 256
        HEADS = 4
        HEAD_DIM = 64
        NEG_SLOPE = 0.2
        key = jax.random.key(seed)
        k1, k2, k3, k4, k5 = jax.random.split(key, 5)
        x = jax.random.normal(k1, (N_NODES, IN_DIM), dtype=jnp.float32)
        edge_index = jax.random.randint(k2, (2, N_EDGES), 0, N_NODES, dtype=jnp.int64)
        W = jax.random.normal(k3, (IN_DIM, HEADS * HEAD_DIM), dtype=jnp.float32) * (1.0 / np.sqrt(IN_DIM))
        att_src = jax.random.normal(k4, (HEADS, HEAD_DIM), dtype=jnp.float32) * (1.0 / np.sqrt(HEAD_DIM))
        att_dst = jax.random.normal(k5, (HEADS, HEAD_DIM), dtype=jnp.float32) * (1.0 / np.sqrt(HEAD_DIM))
        bias = jnp.zeros((HEADS * HEAD_DIM,), dtype=jnp.float32)
        return {'x': x, 'edge_index': edge_index, 'W': W, 'att_src': att_src, 'att_dst': att_dst, 'bias': bias}
    _L0_gnn_all = _L0_gnn_setup()
    _L0_gnn_in = {k: v for k, v in _L0_gnn_all.items() if k in ('W', 'att_src', 'att_dst', 'bias')}
    del _L0_gnn_all

    def _L0_ffn_setup():
        import jax, jax.numpy as jnp
        import numpy as np
        BN_EPS = 0.001

        def _bn(h, g, b, m, v):
            return g * (h - m) * jax.lax.rsqrt(v + BN_EPS) + b
        key = jax.random.key(seed)
        ks = jax.random.split(key, 8)
        B, F, Df = (256, 64, 256)
        E, H, D = (8, 256, 256)
        s1 = 1.0 / np.sqrt(Df)
        s2 = 1.0 / np.sqrt(H)
        return {'x': jax.random.normal(ks[0], (B, F, Df), jnp.float32), 'Wr': jax.random.normal(ks[1], (Df, E), jnp.float32) * s1, 'br': jnp.zeros((E,), jnp.float32), 'W1': jax.random.normal(ks[2], (E, Df, H), jnp.float32) * s1, 'b1': jnp.zeros((E, H), jnp.float32), 'g1': jnp.ones((E, H), jnp.float32), 'be1': jnp.zeros((E, H), jnp.float32), 'm1': jnp.zeros((E, H), jnp.float32), 'v1': jnp.ones((E, H), jnp.float32), 'W2': jax.random.normal(ks[3], (E, H, H), jnp.float32) * s2, 'b2': jnp.zeros((E, H), jnp.float32), 'g2': jnp.ones((E, H), jnp.float32), 'be2': jnp.zeros((E, H), jnp.float32), 'm2': jnp.zeros((E, H), jnp.float32), 'v2': jnp.ones((E, H), jnp.float32), 'Wo': jax.random.normal(ks[4], (E, H, D), jnp.float32) * s2, 'bo': jnp.zeros((E, D), jnp.float32)}
    _L0_ffn_all = _L0_ffn_setup()
    _L0_ffn_in = {k: v for k, v in _L0_ffn_all.items() if k in ('Wr', 'br', 'W1', 'b1', 'g1', 'be1', 'm1', 'v1', 'W2', 'b2', 'g2', 'be2', 'm2', 'v2', 'Wo', 'bo')}
    del _L0_ffn_all

    def _L1_gnn_setup():
        import jax, jax.numpy as jnp
        import numpy as np
        N, E = (6250, 100000)
        IN, H, C = (256, 8, 32)
        NEG_SLOPE = 0.2
        EPS = 1e-05
        key = jax.random.key(seed)
        ks = jax.random.split(key, 6)
        x = jax.random.normal(ks[0], (N, IN), jnp.float32)
        edge_index = jax.random.randint(ks[1], (2, E), 0, N, dtype=jnp.int32)
        W = jax.random.normal(ks[2], (IN, H * C), jnp.float32) / np.sqrt(IN).astype(np.float32)
        att_src = jax.random.normal(ks[3], (H, C), jnp.float32) * 0.1
        att_dst = jax.random.normal(ks[4], (H, C), jnp.float32) * 0.1
        bias = jnp.zeros((H * C,), jnp.float32)
        gamma = jnp.ones((H * C,), jnp.float32)
        beta = jnp.zeros((H * C,), jnp.float32)
        return {'x': x, 'edge_index': edge_index, 'W': W, 'att_src': att_src, 'att_dst': att_dst, 'bias': bias, 'gamma': gamma, 'beta': beta}
    _L1_gnn_all = _L1_gnn_setup()
    _L1_gnn_in = {k: v for k, v in _L1_gnn_all.items() if k in ('W', 'att_src', 'att_dst', 'bias', 'gamma', 'beta')}
    del _L1_gnn_all

    def _L1_ffn_setup():
        import jax, jax.numpy as jnp
        import numpy as np
        B, N, D = (16, 512, 256)
        NUM_EXPERTS, TOP_K, HEADS = (4, 2, 4)
        N_EDGES = 131072
        LN_EPS = 1e-05

        def _layernorm(x, g, b):
            mu = x.mean(-1, keepdims=True)
            var = ((x - mu) ** 2).mean(-1, keepdims=True)
            return (x - mu) * jax.lax.rsqrt(var + LN_EPS) * g + b

        def _forward(x, edge_index, W_gat, att_src, att_dst, b_gat, ln_gamma, ln_beta, W1, b1, W2, b2):
            Bc, Nc, Dc = x.shape
            M = Bc * Nc
            x_flat = x.reshape(M, Dc)
            h = (x_flat @ W_gat).reshape(M, HEADS, NUM_EXPERTS)
            loops = jnp.arange(M, dtype=edge_index.dtype)
            src = jnp.concatenate([edge_index[0], loops])
            dst = jnp.concatenate([edge_index[1], loops])
            a_src = (h * att_src).sum(-1)
            a_dst = (h * att_dst).sum(-1)
            e = jax.nn.leaky_relu(a_src[src] + a_dst[dst], negative_slope=0.2)
            e_max = jax.ops.segment_max(e, dst, num_segments=M)
            ee = jnp.exp(e - e_max[dst])
            denom = jax.ops.segment_sum(ee, dst, num_segments=M)
            alpha = ee / (denom[dst] + 1e-16)
            msg = h[src] * alpha[:, :, None]
            agg = jax.ops.segment_sum(msg, dst, num_segments=M).reshape(M, HEADS * NUM_EXPERTS) + b_gat
            scores = _layernorm(agg, ln_gamma, ln_beta).reshape(M, HEADS, NUM_EXPERTS).mean(1)
            scores = scores.reshape(Bc, Nc, NUM_EXPERTS)
            topk_s, topk_i = jax.lax.top_k(scores, TOP_K)
            w = jax.nn.softmax(topk_s, axis=-1)
            out = jnp.zeros_like(x)
            for ei in range(NUM_EXPERTS):
                g = jnp.where(topk_i == ei, w, 0.0).sum(-1)
                hh = jax.nn.gelu(x @ W1[ei] + b1[ei], approximate=False)
                out = out + g[..., None] * (hh @ W2[ei] + b2[ei])
            return out
        key = jax.random.key(seed)
        ks = jax.random.split(key, 8)
        s = 0.05
        return {'x': jax.random.normal(ks[0], (B, N, D), jnp.float32), 'W_gat': jax.random.normal(ks[1], (D, HEADS * NUM_EXPERTS), jnp.float32) * s, 'att_src': jax.random.normal(ks[2], (HEADS, NUM_EXPERTS), jnp.float32) * s, 'att_dst': jax.random.normal(ks[3], (HEADS, NUM_EXPERTS), jnp.float32) * s, 'b_gat': jnp.zeros((HEADS * NUM_EXPERTS,), jnp.float32), 'ln_gamma': jnp.ones((HEADS * NUM_EXPERTS,), jnp.float32), 'ln_beta': jnp.zeros((HEADS * NUM_EXPERTS,), jnp.float32), 'W1': jax.random.normal(ks[4], (NUM_EXPERTS, D, 2 * D), jnp.float32) * s, 'b1': jnp.zeros((NUM_EXPERTS, 2 * D), jnp.float32), 'W2': jax.random.normal(ks[5], (NUM_EXPERTS, 2 * D, D), jnp.float32) * s, 'b2': jnp.zeros((NUM_EXPERTS, D), jnp.float32), 'edge_index': jax.random.randint(ks[6], (2, N_EDGES), 0, B * N, jnp.int32)}
    _L1_ffn_all = _L1_ffn_setup()
    _L1_ffn_in = {k: v for k, v in _L1_ffn_all.items() if k in ('W_gat', 'att_src', 'att_dst', 'b_gat', 'ln_gamma', 'ln_beta', 'W1', 'b1', 'W2', 'b2', 'edge_index')}
    del _L1_ffn_all
    return {'x': x, 'src': src, 'dst': dst, 'L0_gnn_W': _L0_gnn_in['W'], 'L0_gnn_att_src': _L0_gnn_in['att_src'], 'L0_gnn_att_dst': _L0_gnn_in['att_dst'], 'L0_gnn_bias': _L0_gnn_in['bias'], 'L0_ffn_Wr': _L0_ffn_in['Wr'], 'L0_ffn_br': _L0_ffn_in['br'], 'L0_ffn_W1': _L0_ffn_in['W1'], 'L0_ffn_b1': _L0_ffn_in['b1'], 'L0_ffn_g1': _L0_ffn_in['g1'], 'L0_ffn_be1': _L0_ffn_in['be1'], 'L0_ffn_m1': _L0_ffn_in['m1'], 'L0_ffn_v1': _L0_ffn_in['v1'], 'L0_ffn_W2': _L0_ffn_in['W2'], 'L0_ffn_b2': _L0_ffn_in['b2'], 'L0_ffn_g2': _L0_ffn_in['g2'], 'L0_ffn_be2': _L0_ffn_in['be2'], 'L0_ffn_m2': _L0_ffn_in['m2'], 'L0_ffn_v2': _L0_ffn_in['v2'], 'L0_ffn_Wo': _L0_ffn_in['Wo'], 'L0_ffn_bo': _L0_ffn_in['bo'], 'L1_gnn_W': _L1_gnn_in['W'], 'L1_gnn_att_src': _L1_gnn_in['att_src'], 'L1_gnn_att_dst': _L1_gnn_in['att_dst'], 'L1_gnn_bias': _L1_gnn_in['bias'], 'L1_gnn_gamma': _L1_gnn_in['gamma'], 'L1_gnn_beta': _L1_gnn_in['beta'], 'L1_ffn_W_gat': _L1_ffn_in['W_gat'], 'L1_ffn_att_src': _L1_ffn_in['att_src'], 'L1_ffn_att_dst': _L1_ffn_in['att_dst'], 'L1_ffn_b_gat': _L1_ffn_in['b_gat'], 'L1_ffn_ln_gamma': _L1_ffn_in['ln_gamma'], 'L1_ffn_ln_beta': _L1_ffn_in['ln_beta'], 'L1_ffn_W1': _L1_ffn_in['W1'], 'L1_ffn_b1': _L1_ffn_in['b1'], 'L1_ffn_W2': _L1_ffn_in['W2'], 'L1_ffn_b2': _L1_ffn_in['b2'], 'L1_ffn_edge_index': _L1_ffn_in['edge_index']}

def reference(x, src, dst, L0_gnn_W, L0_gnn_att_src, L0_gnn_att_dst, L0_gnn_bias, L0_ffn_Wr, L0_ffn_br, L0_ffn_W1, L0_ffn_b1, L0_ffn_g1, L0_ffn_be1, L0_ffn_m1, L0_ffn_v1, L0_ffn_W2, L0_ffn_b2, L0_ffn_g2, L0_ffn_be2, L0_ffn_m2, L0_ffn_v2, L0_ffn_Wo, L0_ffn_bo, L1_gnn_W, L1_gnn_att_src, L1_gnn_att_dst, L1_gnn_bias, L1_gnn_gamma, L1_gnn_beta, L1_ffn_W_gat, L1_ffn_att_src, L1_ffn_att_dst, L1_ffn_b_gat, L1_ffn_ln_gamma, L1_ffn_ln_beta, L1_ffn_W1, L1_ffn_b1, L1_ffn_W2, L1_ffn_b2, L1_ffn_edge_index):
    import jax
    import jax.numpy as jnp

    def _L0_gnn_ref(x, edge_index, W, att_src, att_dst, bias):
        import jax, jax.numpy as jnp
        import numpy as np
        N_NODES = 6250
        N_EDGES = 100000
        IN_DIM = 256
        HEADS = 4
        HEAD_DIM = 64
        NEG_SLOPE = 0.2
        N = x.shape[0]
        loops = jnp.arange(N, dtype=edge_index.dtype)
        src = jnp.concatenate([edge_index[0], loops])
        dst = jnp.concatenate([edge_index[1], loops])
        h = (x @ W).reshape(N, HEADS, HEAD_DIM)
        a_src = jnp.einsum('nhd,hd->nh', h, att_src)
        a_dst = jnp.einsum('nhd,hd->nh', h, att_dst)
        e = a_src[src] + a_dst[dst]
        e = jax.nn.leaky_relu(e, NEG_SLOPE)
        m = jax.ops.segment_max(e, dst, num_segments=N)
        e = jnp.exp(e - m[dst])
        denom = jax.ops.segment_sum(e, dst, num_segments=N)
        alpha = e / denom[dst]
        msg = alpha[:, :, None] * h[src]
        out = jax.ops.segment_sum(msg, dst, num_segments=N)
        return out.reshape(N, HEADS * HEAD_DIM) + bias

    def _L0_ffn_ref(x, Wr, br, W1, b1, g1, be1, m1, v1, W2, b2, g2, be2, m2, v2, Wo, bo):
        import jax, jax.numpy as jnp
        import numpy as np
        BN_EPS = 0.001

        def _bn(h, g, b, m, v):
            return g * (h - m) * jax.lax.rsqrt(v + BN_EPS) + b
        feat = jnp.mean(x, axis=0)
        w = jax.nn.softmax(feat @ Wr + br, axis=-1)
        h = jnp.einsum('bfd,edh->bfeh', x, W1) + b1
        h = jax.nn.relu(_bn(h, g1, be1, m1, v1))
        h = jnp.einsum('bfeh,ehk->bfek', h, W2) + b2
        h = jax.nn.relu(_bn(h, g2, be2, m2, v2))
        y = jnp.einsum('bfeh,ehd->bfed', h, Wo) + bo
        return jnp.einsum('bfed,fe->bfd', y, w)

    def _L1_gnn_ref(x, edge_index, W, att_src, att_dst, bias, gamma, beta):
        import jax, jax.numpy as jnp
        import numpy as np
        N, E = (6250, 100000)
        IN, H, C = (256, 8, 32)
        NEG_SLOPE = 0.2
        EPS = 1e-05
        n = x.shape[0]
        xl = (x @ W).reshape(n, H, C)
        a_src = jnp.einsum('nhc,hc->nh', xl, att_src)
        a_dst = jnp.einsum('nhc,hc->nh', xl, att_dst)
        loops = jnp.arange(n, dtype=edge_index.dtype)
        src = jnp.concatenate([edge_index[0], loops])
        dst = jnp.concatenate([edge_index[1], loops])
        logits = jax.nn.leaky_relu(a_src[src] + a_dst[dst], NEG_SLOPE)
        seg_max = jax.ops.segment_max(logits, dst, num_segments=n)
        ex = jnp.exp(logits - seg_max[dst])
        denom = jax.ops.segment_sum(ex, dst, num_segments=n)
        alpha = ex / denom[dst]
        msgs = xl[src] * alpha[:, :, None]
        out = jax.ops.segment_sum(msgs, dst, num_segments=n).reshape(n, H * C) + bias
        mu = jnp.mean(out, axis=-1, keepdims=True)
        var = jnp.var(out, axis=-1, keepdims=True)
        return (out - mu) / jnp.sqrt(var + EPS) * gamma + beta

    def _L1_ffn_ref(x, W_gat, att_src, att_dst, b_gat, ln_gamma, ln_beta, W1, b1, W2, b2, edge_index):
        import jax, jax.numpy as jnp
        import numpy as np
        B, N, D = (16, 512, 256)
        NUM_EXPERTS, TOP_K, HEADS = (4, 2, 4)
        N_EDGES = 131072
        LN_EPS = 1e-05

        def _layernorm(x, g, b):
            mu = x.mean(-1, keepdims=True)
            var = ((x - mu) ** 2).mean(-1, keepdims=True)
            return (x - mu) * jax.lax.rsqrt(var + LN_EPS) * g + b

        def _forward(x, edge_index, W_gat, att_src, att_dst, b_gat, ln_gamma, ln_beta, W1, b1, W2, b2):
            Bc, Nc, Dc = x.shape
            M = Bc * Nc
            x_flat = x.reshape(M, Dc)
            h = (x_flat @ W_gat).reshape(M, HEADS, NUM_EXPERTS)
            loops = jnp.arange(M, dtype=edge_index.dtype)
            src = jnp.concatenate([edge_index[0], loops])
            dst = jnp.concatenate([edge_index[1], loops])
            a_src = (h * att_src).sum(-1)
            a_dst = (h * att_dst).sum(-1)
            e = jax.nn.leaky_relu(a_src[src] + a_dst[dst], negative_slope=0.2)
            e_max = jax.ops.segment_max(e, dst, num_segments=M)
            ee = jnp.exp(e - e_max[dst])
            denom = jax.ops.segment_sum(ee, dst, num_segments=M)
            alpha = ee / (denom[dst] + 1e-16)
            msg = h[src] * alpha[:, :, None]
            agg = jax.ops.segment_sum(msg, dst, num_segments=M).reshape(M, HEADS * NUM_EXPERTS) + b_gat
            scores = _layernorm(agg, ln_gamma, ln_beta).reshape(M, HEADS, NUM_EXPERTS).mean(1)
            scores = scores.reshape(Bc, Nc, NUM_EXPERTS)
            topk_s, topk_i = jax.lax.top_k(scores, TOP_K)
            w = jax.nn.softmax(topk_s, axis=-1)
            out = jnp.zeros_like(x)
            for ei in range(NUM_EXPERTS):
                g = jnp.where(topk_i == ei, w, 0.0).sum(-1)
                hh = jax.nn.gelu(x @ W1[ei] + b1[ei], approximate=False)
                out = out + g[..., None] * (hh @ W2[ei] + b2[ei])
            return out
        return _forward(x, edge_index, W_gat, att_src, att_dst, b_gat, ln_gamma, ln_beta, W1, b1, W2, b2)
    edge_index = jnp.stack([src, dst])
    x = x + _L0_gnn_ref(_layernorm(x, axis=-1), edge_index, L0_gnn_W, L0_gnn_att_src, L0_gnn_att_dst, L0_gnn_bias)
    x = x + _L0_ffn_ref(_layernorm(x, axis=-1)[None], L0_ffn_Wr, L0_ffn_br, L0_ffn_W1, L0_ffn_b1, L0_ffn_g1, L0_ffn_be1, L0_ffn_m1, L0_ffn_v1, L0_ffn_W2, L0_ffn_b2, L0_ffn_g2, L0_ffn_be2, L0_ffn_m2, L0_ffn_v2, L0_ffn_Wo, L0_ffn_bo)[0]
    x = x + _L1_gnn_ref(_layernorm(x, axis=-1), edge_index, L1_gnn_W, L1_gnn_att_src, L1_gnn_att_dst, L1_gnn_bias, L1_gnn_gamma, L1_gnn_beta)
    x = x + _L1_ffn_ref(_layernorm(x, axis=-1)[None], L1_ffn_W_gat, L1_ffn_att_src, L1_ffn_att_dst, L1_ffn_b_gat, L1_ffn_ln_gamma, L1_ffn_ln_beta, L1_ffn_W1, L1_ffn_b1, L1_ffn_W2, L1_ffn_b2, L1_ffn_edge_index)[0]
    return x

_drawn_inputs = setup_inputs


def setup_inputs(seed=0):
    import zlib

    import numpy as np

    out = dict(_drawn_inputs(seed))
    spreads = {'L0_gnn_bias': (0.0, 0.1),
     'L0_ffn_br': (0.0, 0.1),
     'L0_ffn_b1': (0.0, 0.1),
     'L0_ffn_g1': (1.0, 0.2),
     'L0_ffn_be1': (0.0, 0.1),
     'L0_ffn_m1': (0.0, 0.1),
     'L0_ffn_v1': (1.0, 0.2),
     'L0_ffn_b2': (0.0, 0.1),
     'L0_ffn_g2': (1.0, 0.2),
     'L0_ffn_be2': (0.0, 0.1),
     'L0_ffn_m2': (0.0, 0.1),
     'L0_ffn_v2': (1.0, 0.2),
     'L0_ffn_bo': (0.0, 0.1),
     'L1_gnn_bias': (0.0, 0.1),
     'L1_gnn_gamma': (1.0, 0.2),
     'L1_gnn_beta': (0.0, 0.1),
     'L1_ffn_b_gat': (0.0, 0.1),
     'L1_ffn_ln_gamma': (1.0, 0.2),
     'L1_ffn_ln_beta': (0.0, 0.1),
     'L1_ffn_b1': (0.0, 0.1),
     'L1_ffn_b2': (0.0, 0.1)}
    factors = {'L1_ffn_att_dst': 47.471, 'L1_ffn_att_src': 2.667}
    for name, (base, spread) in spreads.items():
        noise = np.random.default_rng([zlib.crc32(name.encode()), seed]).standard_normal(out[name].shape)
        drawn = base * np.exp(spread * noise) if base else spread * noise
        out[name] = jnp.asarray(drawn.astype(out[name].dtype))
    for name, factor in factors.items():
        out[name] = (out[name] * factor).astype(out[name].dtype)
    return out
```

```python
from contextlib import ExitStack

import concourse.bass as bass
from concourse import mybir

ALU = mybir.AluOpType
ACT = mybir.ActivationFunctionType
AX = mybir.AxisListType
F32 = mybir.dt.float32
BF16 = mybir.dt.bfloat16
I32 = mybir.dt.int32

P = 128
NODES, DIM = 12500, 256
NB = -(-NODES // P)
CHUNK = 4
NCH = -(-NB // CHUNK)
ROWS = NCH * CHUNK * P
KC = DIM // P
FAR = 1 << 20
LOW = -1.0e30
SLOPE = 0.2
LN_EPS = 1e-5
BN_EPS = 1e-3
HALF = 8
BODY = 2 * HALF
LOT = 4
TURN = 8 * LOT


class Ctx:

    def __init__(self, nc, stage):
        self.nc, self.stage, self.stack, self.sems = nc, stage, ExitStack(), []

    def __enter__(self):
        self.stack.__enter__()
        return self

    def __exit__(self, *e):
        if e[0] is None and self.sems:
            self.nc.all_engine_barrier()
            self.nc.clear_and_free_semaphores(self.sems)
            self.nc.all_engine_barrier()
        return self.stack.__exit__(*e)

    def sb(self, name, shape, dt=F32):
        return self.stack.enter_context(self.nc.sbuf_tensor(f"{self.stage}_{name}", list(shape), dt))

    def ps(self, name, shape, dt=F32):
        return self.stack.enter_context(self.nc.psum_tensor(f"{self.stage}_{name}", list(shape), dt))

    def sem(self, name):
        self.sems.append(self.nc.alloc_semaphore(f"{self.stage}_{name}"))
        return self.sems[-1]


class Link:

    def __init__(self, eng, sem, base=0):
        self.eng, self.sem, self.base, self.n = eng, sem, base, 0

    def on(self, eng):
        self.eng = eng
        return self

    def __call__(self, ins):
        self.n += 1
        ins.then_inc(self.sem, 1)
        self.eng.wait_ge(self.sem, self.base + self.n)


def make_constants(nc, c):
    K = {
        "ident": c.sb("ident", [P, P]), "identb": c.sb("identb", [P, P], BF16),
        "ones": c.sb("ones", [P, P]), "upper": c.sb("upper", [P, P]),
        "iota": c.sb("iota", [P, P]), "iotab": c.sb("iotab", [P, P], BF16), "iotai": c.sb("iotai", [P, P], I32),
        "low": c.sb("low", [P, 1]), "eps": c.sb("eps", [P, 1]), "bneps": c.sb("bneps", [P, 1]),
    }
    filled, shaped = c.sem("filled"), c.sem("shaped")
    with nc.Block() as block:

        @block.gpsimd
        def _(pool):
            nc.gpsimd.memset(K["ident"][:, :], 0.0).then_inc(filled, 1)
            nc.gpsimd.memset(K["ones"][:, :], 1.0).then_inc(filled, 1)
            nc.gpsimd.memset(K["low"][:, :], LOW)
            nc.gpsimd.memset(K["eps"][:, :], LN_EPS)
            nc.gpsimd.memset(K["bneps"][:, :], BN_EPS)
            nc.gpsimd.iota(K["iotai"][:, :], [[1, P]], base=0, channel_multiplier=0).then_inc(shaped, 1)
            pool.wait_ge(filled, 2)
            nc.gpsimd.affine_select(out=K["ident"][:, :], in_=K["ident"][:, :], compare_op=ALU.not_equal, fill=1.0,
                                    base=0, pattern=[[-1, P]], channel_multiplier=1).then_inc(shaped, 1)
            nc.gpsimd.affine_select(out=K["upper"][:, :], in_=K["ones"][:, :], compare_op=ALU.is_gt, fill=0.0,
                                    base=0, pattern=[[1, P]], channel_multiplier=-1).then_inc(shaped, 1)

        @block.vector
        def _(dve):
            dve.wait_ge(shaped, 3)
            nc.vector.tensor_copy(K["identb"][:, :], K["ident"][:, :])
            nc.vector.tensor_copy(K["iota"][:, :], K["iotai"][:, :])
            nc.vector.tensor_copy(K["iotab"][:, :], K["iotai"][:, :])
    return K


def sort_edges(nc, K, name, src, dst, cols, padded, start, count, pairs, blk=None):
    E = src.shape[0]
    full = E // P
    rest = E - full * P
    T = -(-E // (P * BODY)) * BODY
    N = T // HALF
    NPOS = P * cols
    with Ctx(nc, name) as c:
        srci = c.sb("srci", [P, T], I32)
        dsti = c.sb("dsti", [P, T], I32)
        part = c.sb("part", [P, T + HALF], I32)
        lo = c.sb("lo", [P, T + HALF], BF16)
        hi = c.sb("hi", [P, T + HALF], BF16)
        skip = c.sb("skip", [P, T])
        blank = c.sb("blank", [P, cols, 2], I32)
        lead = c.sb("lead", [1, 2], I32)
        ohlo = c.sb("ohlo", [P, 2, HALF, P], BF16)
        ohhi = c.sb("ohhi", [P, 2, HALF, NB], BF16)
        cleared, loaded, blanked, ch = c.sem("cleared"), c.sem("loaded"), c.sem("blanked"), c.sem("ch")
        ntr = full and (2 + 2 * (rest > 0))

        def onehots(slot, col):
            nc.vector.tensor_tensor(ohlo[:, slot, :, :], K["iotab"][:, :].unsqueeze(1).to_broadcast([P, HALF, P]),
                                    lo[:, bass.ds(col, HALF)].unsqueeze(2).to_broadcast([P, HALF, P]), ALU.is_equal)
            return nc.vector.tensor_tensor(ohhi[:, slot, :, :],
                                           K["iotab"][:, 0:NB].unsqueeze(1).to_broadcast([P, HALF, NB]),
                                           hi[:, bass.ds(col, HALF)].unsqueeze(2).to_broadcast([P, HALF, NB]),
                                           ALU.is_equal)

        with Ctx(nc, name + "h") as c2:
            countp = c2.ps("countp", [P, 512])
            totalp = c2.ps("totalp", [P, 512])
            withinp = c2.ps("withinp", [P, 512])
            tilep = c2.ps("tilep", [P, 512])
            blkp = [c2.ps(f"blkp{j}", [P, 512]) for j in range(4)] if padded else []
            sizes = c2.sb("sizes", [P, NB])
            sizei = c2.sb("sizei", [P, NB], I32)
            ends = c2.sb("ends", [P, NB])
            firsts = c2.sb("firsts", [P, P])
            zero = c2.sb("zero", [P, NB])
            onehot_ready, onehot_used = c2.sem("onehot_ready"), c2.sem("onehot_used")
            count_ready, sums_ready = c2.sem("count_ready"), c2.sem("sums_ready")
            firsts_ready, turned, reached, summed = (c2.sem(s) for s in ("firsts_ready", "turned", "reached", "summed"))
            if padded:
                tilei = c2.sb("tilei", [P, cols], I32)
                tilef = c2.sb("tilef", [P, cols])
                tcol = c2.sb("tcol", [P, 1])
                reach = c2.sb("reach", [P, cols])
                numbered = c2.sem("numbered")
            W = cols // 4
            with nc.Block() as block:

                @block.sync
                def _(sp):
                    sp.wait_ge(cleared, 3)
                    for ap, t in ((src, srci), (dst, dsti)):
                        sp.dma_start(t[:, 0:full], ap[0:full * P].rearrange("(p c) -> p c", p=P)).then_inc(loaded, 16)
                        if rest:
                            sp.dma_start(t[0:rest, full:full + 1],
                                         ap[full * P:E].rearrange("(p c) -> p c", c=1)).then_inc(loaded, 16)
                    sp.wait_ge(cleared, 6)
                    sp.dma_start(pairs[0:1, :], lead[:, :]).then_inc(blanked, 16)
                    sp.dma_start(pairs[1:1 + NPOS, :].rearrange("(p c) w -> p c w", p=P), blank[:, :, :])\
                      .then_inc(blanked, 16)
                    sp.wait_ge(blanked, 32)

                @block.vector
                def _(dve):
                    link = Link(dve, ch)
                    nc.vector.memset(srci[:, :], 0).then_inc(cleared, 1)
                    nc.vector.memset(dsti[:, :], -1).then_inc(cleared, 1)
                    nc.vector.memset(part[:, :], -1).then_inc(cleared, 1)
                    nc.vector.memset(zero[:, :], 0.0).then_inc(onehot_used, 2)
                    nc.vector.memset(blank[:, :, 0:1], 0).then_inc(cleared, 1)
                    nc.vector.memset(blank[:, :, 1:2], -1).then_inc(cleared, 1)
                    nc.vector.memset(lead[:, :], -2).then_inc(cleared, 1)
                    dve.wait_ge(loaded, 16 * ntr)
                    dve.wait_ge(cleared, 6)
                    link(nc.vector.tensor_scalar(part[:, 0:T], dsti[:, :], 127, None, ALU.bitwise_and))
                    link(nc.vector.tensor_copy(lo[:, :], part[:, :]))
                    link(nc.vector.tensor_scalar(part[:, 0:T], dsti[:, :], 7, None, ALU.arith_shift_right))
                    link(nc.vector.memset(part[:, T:T + HALF], -1))
                    link(nc.vector.tensor_copy(hi[:, :], part[:, :]))
                    link(nc.vector.tensor_scalar(skip[:, :], hi[:, 0:T], 0.0, float(FAR), ALU.is_lt, ALU.mult))
                    with dve.Fori(0, N // 2) as i:
                        for h in range(2):
                            dve.wait_ge(onehot_used, i * 2 + h + 1)
                            onehots(h, i * BODY + h * HALF).then_inc(onehot_ready, 1)
                    dve.wait_ge(onehot_used, N + 2)
                    nc.vector.tensor_copy(count[:, :], countp[:, 0:NB]).then_inc(count_ready, 1)
                    dve.wait_ge(sums_ready, 1)
                    link(nc.vector.tensor_copy(sizes[:, :], totalp[:, 0:NB]))
                    if padded:
                        link(nc.vector.tensor_scalar(sizes[:, :], sizes[:, :], float(P - 1), None, ALU.add))
                        link(nc.vector.tensor_copy(sizei[:, :], sizes[:, :]))
                        link(nc.vector.tensor_scalar(sizei[:, :], sizei[:, :], 7, None, ALU.arith_shift_right))
                        link(nc.vector.tensor_copy(sizes[:, :], sizei[:, :]))
                    link(nc.vector.tensor_tensor_scan(ends[:, :], K["ones"][:, 0:NB], sizes[:, :], 0.0,
                                                      ALU.mult, ALU.add))
                    link(nc.vector.memset(firsts[:, :], 0.0))
                    link(nc.vector.tensor_tensor(firsts[:, 0:NB], ends[:, :], sizes[:, :], ALU.subtract))
                    dve.sem_inc(firsts_ready, 1)
                    nc.vector.scalar_tensor_tensor(out=start[:, :], in0=firsts[:, 0:NB],
                                                   scalar=float(P) if padded else 1.0, in1=withinp[:, 0:NB],
                                                   op0=ALU.mult, op1=ALU.add)
                    if padded:
                        dve.wait_ge(numbered, 1)
                        link(nc.vector.tensor_copy(tilef[:, :], tilei[:, :]))
                        dve.wait_ge(turned, 1)
                        link(nc.vector.tensor_copy(tcol[:, :], tilep[:, 0:1]))
                        nc.vector.tensor_scalar(reach[:, :], tilef[:, :], tcol[:, 0:1], None, ALU.is_ge)\
                          .then_inc(reached, 1)
                        dve.wait_ge(summed, 1)
                        for j in range(4):
                            nc.vector.tensor_scalar(blk[0:1, j * W:(j + 1) * W], blkp[j][0:1, 0:W], -1.0, None, ALU.add)

                @block.gpsimd
                def _(pool):
                    if padded:
                        nc.gpsimd.iota(tilei[:, :], [[1, cols]], base=0, channel_multiplier=0).then_inc(numbered, 1)

                @block.tensor
                def _(pe):
                    pe.wait_ge(onehot_used, 2)
                    nc.tensor.matmul(countp[:, 0:NB], K["ones"][:, :], zero[:, :], start=True, stop=True)
                    with pe.Fori(0, N // 2) as i:
                        for h in range(2):
                            pe.wait_ge(onehot_ready, i * 2 + h + 1)
                            for u in range(HALF):
                                mm = nc.tensor.matmul(countp[:, 0:NB], ohlo[:, h, u, :], ohhi[:, h, u, :],
                                                      start=False, stop=True, skip_group_check=True)
                            mm.then_inc(onehot_used, 1)
                    pe.wait_ge(count_ready, 1)
                    nc.tensor.matmul(totalp[:, 0:NB], K["ones"][:, :], count[:, :], start=True, stop=True)
                    nc.tensor.matmul(withinp[:, 0:NB], K["upper"][:, :], count[:, :], start=True, stop=True)\
                      .then_inc(sums_ready, 1)
                    if padded:
                        pe.wait_ge(firsts_ready, 1)
                        nc.tensor.transpose(tilep[:, 0:P], firsts[:, :], K["ident"][:, :]).then_inc(turned, 1)
                        pe.wait_ge(reached, 1)
                        for j in range(4):
                            mm = nc.tensor.matmul(blkp[j][:, 0:W], K["ones"][0:NB, :], reach[0:NB, j * W:(j + 1) * W],
                                                  start=True, stop=True)
                        mm.then_inc(summed, 1)

        with Ctx(nc, name + "s") as c2:
            turnp = c2.ps("turnp", [P, HALF, P], BF16)
            samep = [c2.ps(f"samep{g}", [P, 4, P]) for g in range(2)]
            addp = [c2.ps(f"addp{g}", [P, 512]) for g in range(2)]
            placep = [c2.ps(f"placep{g}", [P, 512]) for g in range(2)]
            run = [c2.sb(f"run{h}", [P, HALF, NB]) for h in range(2)]
            loT = c2.sb("loT", [P, 2, HALF, P])
            loTb = c2.sb("loTb", [P, 2, HALF, P], BF16)
            same = c2.sb("same", [P, 2, HALF, P], BF16)
            prod = c2.sb("prod", [P, 2, 4, NB])
            placef = c2.sb("placef", [P, HALF])
            placei = c2.sb("placei", [P, 2, HALF], I32)
            pair = c2.sb("pair", [P, 2, HALF, 2], I32)
            s = {n: c2.sem(n) for n in ("onehot_ready", "turned", "copied", "copiedb", "same_ready", "masked", "add_ready",
                                        "run_ready", "place_ready", "place_used", "scatter_ready", "passed",
                                        "reduced")}
            landed = [c2.sem(f"landed{h}") for h in range(2)]
            slot_free = [c2.sem(f"slot_free{h}") for h in range(2)]
            quad = lambda bank: bank[:, 0:4 * NB].rearrange("p (a b) -> p a b", a=4)
            with nc.Block() as block:

                @block.vector
                def _(dve):
                    nc.vector.tensor_scalar(run[0][:, 0, :], start[:, :], 1.0, None, ALU.add)\
                      .then_inc(s["run_ready"], 1)
                    dve.sem_inc(s["masked"], 1)
                    dve.sem_inc(s["place_used"], 2)
                    for h in range(2):
                        dve.sem_inc(slot_free[h], 1)
                    onehots(0, 0).then_inc(s["onehot_ready"], 1)

                    def tables(n, h):
                        dve.wait_ge(s["add_ready"], n + 1)
                        for u in range(HALF):
                            dve.wait_ge(s["run_ready"], n * HALF + u + 1)
                            o = run[h][:, u + 1, :] if u + 1 < HALF else run[1 - h][:, 0, :]
                            nc.vector.tensor_tensor(o, run[h][:, u, :], quad(addp[u // 4])[:, u % 4, :], ALU.add)\
                              .then_inc(s["run_ready"], 1)
                        dve.wait_ge(s["same_ready"], n + 1)
                        for g in range(2):
                            mk = nc.vector.tensor_tensor(same[:, h, 4 * g:4 * g + 4, :], samep[g][:, :, :],
                                                         K["upper"][:, :].unsqueeze(1).to_broadcast([P, 4, P]),
                                                         ALU.mult)
                        mk.then_inc(s["masked"], 1)

                    def place(n, h, k, after):
                        for g in range(2):
                            dve.wait_ge(s["place_ready"], n * 2 + g + 1)
                            nc.vector.tensor_tensor(prod[:, g, :, :], quad(placep[g]),
                                                    ohhi[:, h, 4 * g:4 * g + 4, :], ALU.mult)\
                              .then_inc(s["place_used"], 1)
                        dve.wait_ge(s["place_used"], n * 2 + 4)
                        if after is not None:
                            onehots(h, after).then_inc(s["onehot_ready"], 1)
                        nc.vector.tensor_reduce(placef[:, :], prod[:, :, :, :].rearrange("p g a b -> p (g a) b"),
                                                AX.X, ALU.add).then_inc(s["reduced"], 1)
                        dve.wait_ge(slot_free[h], k + 1)
                        dve.wait_ge(s["reduced"], n + 1)
                        nc.vector.tensor_tensor(placei[:, h, :], placef[:, :], skip[:, bass.ds(n * HALF, HALF)],
                                                ALU.add)
                        nc.vector.tensor_copy(pair[:, h, :, 0], srci[:, bass.ds(n * HALF, HALF)])
                        nc.vector.tensor_copy(pair[:, h, :, 1], dsti[:, bass.ds(n * HALF, HALF)])\
                          .then_inc(s["scatter_ready"], 1)

                    tables(0, 0)
                    onehots(1, HALF).then_inc(s["onehot_ready"], 1)
                    with dve.Fori(0, N // 2 - 1) as i:
                        for j in range(2):
                            tables(i * 2 + j + 1, 1 - j)
                            place(i * 2 + j, j, i, i * BODY + (j + 2) * HALF)
                    tables(N - 1, 1)
                    place(N - 2, 0, N // 2 - 1, None)
                    place(N - 1, 1, N // 2 - 1, None)

                @block.scalar
                def _(act):
                    def copy_turned(slot, n):
                        act.wait_ge(s["turned"], n + 1)
                        nc.scalar.copy(loTb[:, slot, :, :], turnp[:, :, :]).then_inc(s["copiedb"], 1)
                        nc.scalar.copy(loT[:, slot, :, :], turnp[:, :, :]).then_inc(s["copied"], 1)

                    copy_turned(0, 0)
                    copy_turned(1, 1)
                    with act.Fori(0, N // 2 - 1) as i:
                        for h in range(2):
                            copy_turned(h, i * 2 + h + 2)

                @block.tensor
                def _(pe):
                    def turn(slot, n):
                        pe.wait_ge(s["onehot_ready"], n + 1)
                        for u in range(HALF):
                            tr = nc.tensor.transpose(turnp[:, u, :], ohlo[:, slot, u, :], K["identb"][:, :])
                        tr.then_inc(s["turned"], 1)

                    def add(n, h):
                        pe.wait_ge(s["run_ready"], n * HALF + 1)
                        for u in range(HALF):
                            mm = nc.tensor.matmul(quad(addp[u // 4])[:, u % 4, :], ohlo[:, h, u, :],
                                                  ohhi[:, h, u, :], start=True, stop=True)
                        mm.then_inc(s["add_ready"], 1)

                    def half(n, h, last):
                        pe.wait_ge(s["copiedb"], n + 1)
                        pe.wait_ge(s["masked"], n + 1)
                        for u in range(HALF):
                            mm = nc.tensor.matmul(samep[u // 4][:, u % 4, :], loTb[:, h, u, :], loTb[:, h, u, :],
                                                  start=True, stop=True)
                        mm.then_inc(s["same_ready"], 1)
                        pe.wait_ge(s["copied"], n + 1)
                        pe.wait_ge(s["masked"], n + 2)
                        for u in range(HALF):
                            g = u // 4
                            if u % 4 == 0:
                                pe.wait_ge(s["place_used"], n * 2 + g + 1)
                            nc.tensor.matmul(quad(placep[g])[:, u % 4, :], loT[:, h, u, :], run[h][:, u, :],
                                             start=True, stop=False)
                            mm = nc.tensor.matmul(quad(placep[g])[:, u % 4, :], same[:, h, u, :],
                                                  ohhi[:, h, u, :], start=False, stop=True)
                            if u % 4 == 3:
                                mm.then_inc(s["place_ready"], 1)
                            if u == 3 and not last:
                                turn(1 - h, n + 1)
                                add(n + 1, 1 - h)

                    turn(0, 0)
                    add(0, 0)
                    with pe.Fori(0, N // 2 - 1) as i:
                        for h in range(2):
                            half(i * 2 + h, h, False)
                    half(N - 2, 0, False)
                    half(N - 1, 1, True)

                @block.gpsimd
                def _(pool):
                    with pool.Fori(0, N // 2) as i:
                        for h in range(2):
                            pool.wait_ge(s["scatter_ready"], i * 2 + h + 1)
                            pool.sem_inc(s["passed"], 1)
                            for u in range(HALF):
                                nc.gpsimd.indirect_dma_start(
                                    pairs, bass.IndirectOffsetOnAxis(ap=placei[:, h, u:u + 1], axis=0),
                                    pair[:, h, u, :], None, bounds_check=NPOS, oob_is_err=False)\
                                  .then_inc(landed[h], 16)

                @block.sync
                def _(sp):
                    with sp.Fori(0, N // 2) as i:
                        for h in range(2):
                            sp.wait_ge(landed[h], i * (16 * HALF) + 16 * HALF)
                            sp.sem_inc(slot_free[h], 1)


def gather_columns(nc, name, table, width, idx, out, cols, half):
    N = cols // half
    with Ctx(nc, name) as c:
        idxs = c.sb("idxs", [P, 2, half], I32)
        rows = c.sb("rows", [P, 2, half, width])
        idx_ready, passed = c.sem("idx_ready"), c.sem("passed")
        landed = [c.sem(f"landed{h}") for h in range(2)]
        with nc.Block() as block:

            @block.scalar
            def _(act):
                def stage(h, col):
                    nc.scalar.copy(idxs[:, h, :], idx[:, bass.ds(col, half)]).then_inc(idx_ready, 1)

                def take(h, n, col):
                    act.wait_ge(landed[h], n)
                    nc.scalar.copy(out[:, bass.ds(col, half), :], rows[:, h, :, :])

                stage(0, 0)
                stage(1, half)
                with act.Fori(0, N // 2 - 1) as i:
                    for h in range(2):
                        take(h, i * (16 * half) + 16 * half, i * (2 * half) + h * half)
                        stage(h, i * (2 * half) + (h + 2) * half)
                for h in range(2):
                    take(h, N // 2 * 16 * half, (N - 2 + h) * half)

            @block.gpsimd
            def _(pool):
                with pool.Fori(0, N // 2) as i:
                    for h in range(2):
                        pool.wait_ge(idx_ready, i * 2 + h + 1)
                        pool.sem_inc(passed, 1)
                        for u in range(half):
                            nc.gpsimd.indirect_dma_start(
                                rows[:, h, u, :], None, table,
                                bass.IndirectOffsetOnAxis(ap=idxs[:, h, u:u + 1], axis=0)).then_inc(landed[h], 16)


def scatter_columns(nc, name, table, width, idx, vals, cols, half, last):
    N = cols // half
    with Ctx(nc, name) as c:
        idxs = c.sb("idxs", [P, 2, half], I32)
        rows = c.sb("rows", [P, 2, half, width])
        staged, passed = c.sem("staged"), c.sem("passed")
        landed = [c.sem(f"landed{h}") for h in range(2)]
        with nc.Block() as block:

            @block.scalar
            def _(act):
                def stage(h, col):
                    nc.scalar.copy(idxs[:, h, :], idx[:, bass.ds(col, half)])
                    nc.scalar.copy(rows[:, h, :, :], vals[:, bass.ds(col, half), :]).then_inc(staged, 1)

                stage(0, 0)
                stage(1, half)
                with act.Fori(0, N // 2 - 1) as i:
                    for h in range(2):
                        act.wait_ge(landed[h], i * (16 * half) + 16 * half)
                        act.sem_inc(passed, 1)
                        stage(h, i * (2 * half) + (h + 2) * half)
                for h in range(2):
                    act.wait_ge(landed[h], N // 2 * 16 * half)

            @block.gpsimd
            def _(pool):
                with pool.Fori(0, N // 2) as i:
                    for h in range(2):
                        pool.wait_ge(staged, i * 2 + h + 1)
                        pool.sem_inc(passed, 1)
                        for u in range(half):
                            nc.gpsimd.indirect_dma_start(
                                table, bass.IndirectOffsetOnAxis(ap=idxs[:, h, u:u + 1], axis=0),
                                rows[:, h, u, :], None, bounds_check=last, oob_is_err=False).then_inc(landed[h], 16)


def carry_over(nc, K, name, last, anyfirst, op0, op1, initial, out, width):
    with Ctx(nc, name) as c:
        lp, rp, op = (c.ps(n, [P, 512]) for n in ("lp", "rp", "op"))
        both = c.sb("both", [P, P])
        rows = c.sb("rows", [P, 2, P])
        state = c.sb("state", [P, P])
        spread, turned, scanned, back, ch = (c.sem(n) for n in ("spread", "turned", "scanned", "back", "ch"))
        with nc.Block() as block:

            @block.vector
            def _(dve):
                link = Link(dve, ch)
                nc.vector.tensor_copy(both[:, 0:width], anyfirst[:, 0:1].to_broadcast([P, width])).then_inc(spread, 1)
                dve.wait_ge(turned, 1)
                link(nc.vector.tensor_copy(rows[0:width, 0, :], lp[0:width, 0:P]))
                link(nc.vector.tensor_copy(rows[0:width, 1, :], rp[0:width, 0:P]))
                link(nc.vector.memset(state[0:width, 0:1], initial))
                nc.vector.tensor_tensor_scan(state[0:width, 1:P], rows[0:width, 1, 0:P - 1], rows[0:width, 0, 0:P - 1],
                                             initial, op0, op1).then_inc(scanned, 1)
                dve.wait_ge(back, 1)
                nc.vector.tensor_copy(out[:, 0:width], op[:, 0:width])

            @block.tensor
            def _(pe):
                nc.tensor.transpose(lp[0:width, 0:P], last[:, 0:width], K["ident"][:, :])
                pe.wait_ge(spread, 1)
                nc.tensor.transpose(rp[0:width, 0:P], both[:, 0:width], K["ident"][:, :]).then_inc(turned, 1)
                pe.wait_ge(scanned, 1)
                nc.tensor.transpose(op[:, 0:width], state[0:width, :], K["ident"][0:width, 0:width]).then_inc(back, 1)


def edge_weights(nc, K, c, name, cols, H, table, width, pairs, start, count, asn, adn, mn, scratch):
    maxd, filld, fillm = scratch
    NPOS = P * cols
    prs = c.sb("prs", [P, cols, 2], I32)
    prev = c.sb("prev", [P, 1], I32)
    rows = c.sb("rows", [P, cols, width])
    prevf = c.sb("prevf", [P, 1])
    first = c.sb("first", [P, cols])
    inner = c.sb("inner", [P, cols])
    before = c.sb("before", [P, cols]) if width > H else None
    inall = c.sb("inall", [P, 1])
    lown = c.sb("lown", [P, 1])
    starti = c.sb("starti", [P, NB], I32)
    endi = c.sb("endi", [P, NB], I32)
    tmpn = c.sb("tmpn", [P, NB])
    has = c.sb("has", [P, NB])
    last = c.sb("last", [P, 32])
    carry = c.sb("carry", [P, 32])
    with Ctx(nc, name + "e") as e:
        val = e.sb("val", [P, cols, H])
        seen = e.sb("seen", [P, cols])
        dstf = e.sb("dstf", [P, cols])
        if before is None:
            before = e.sb("before", [P, cols])
        steps = Link(None, e.sem("steps"))
        loaded, zeroed, stored = e.sem("loaded"), e.sem("zeroed"), e.sem("stored")
        places = pairs[1:1 + NPOS, :].rearrange("(p c) w -> p c w", p=P)
        onp = lambda d: d.rearrange("(p c) w -> p c w", p=P)
        with nc.Block() as block:

            @block.sync
            def _(sp):
                sp.dma_start(prs[:, :, :], places).then_inc(loaded, 16)
                with nc.allow_non_contiguous_dma("one word of each partition"):
                    sp.dma_start(prev[:, :], pairs[0:NPOS, :].rearrange("(p c) w -> p c w", p=P)[:, 0, 1:2])\
                      .then_inc(loaded, 16)
                sp.wait_ge(zeroed, 1)
                sp.dma_start(onp(filld), val[:, :, :]).then_inc(stored, 16)
                sp.dma_start(onp(fillm), val[:, :, :]).then_inc(stored, 16)
                sp.wait_ge(stored, 32)

            @block.vector
            def _(dve):
                link = steps.on(dve)
                nc.vector.memset(val[:, :, :], 0.0).then_inc(zeroed, 1)
                dve.wait_ge(loaded, 32)
                link(nc.vector.tensor_copy(dstf[:, :], prs[:, :, 1]))
                link(nc.vector.tensor_copy(prevf[:, :], prev[:, :]))
                link(nc.vector.tensor_tensor(first[:, 1:cols], dstf[:, 1:cols], dstf[:, 0:cols - 1], ALU.not_equal))
                link(nc.vector.tensor_tensor(first[:, 0:1], dstf[:, 0:1], prevf[:, :], ALU.not_equal))
                link(nc.vector.tensor_scalar(inner[:, :], first[:, :], -1.0, 1.0, ALU.mult, ALU.add))
                link(nc.vector.tensor_tensor_scan(before[:, :], inner[:, :], inner[:, :], 1.0, ALU.mult, ALU.min))
                link(nc.vector.tensor_scalar(seen[:, :], before[:, :], -LOW, LOW, ALU.mult, ALU.add))
                link(nc.vector.tensor_copy(inall[:, :], before[:, cols - 1:cols]))
                link(nc.vector.tensor_copy(lown[:, :], seen[:, cols - 1:cols]))
                link(nc.vector.tensor_scalar(has[:, :], count[:, :], 0.0, None, ALU.is_gt))
                link(nc.vector.tensor_scalar(tmpn[:, :], has[:, :], -float(FAR), float(FAR), ALU.mult, ALU.add))
                link(nc.vector.tensor_tensor(tmpn[:, :], tmpn[:, :], start[:, :], ALU.add))
                link(nc.vector.tensor_copy(starti[:, :], tmpn[:, :]))
                link(nc.vector.scalar_tensor_tensor(out=tmpn[:, :], in0=start[:, :], scalar=-1.0, in1=count[:, :],
                                                    op0=ALU.add, op1=ALU.add))
                link(nc.vector.tensor_scalar(tmpn[:, :], tmpn[:, :], 0.0, None, ALU.max))
                link(nc.vector.tensor_copy(endi[:, :], tmpn[:, :]))

        gather_columns(nc, name + "g", table, width, prs[:, :, 0], rows[:, :, :], cols, HALF)

        with nc.Block() as block:

            @block.vector
            def _(dve):
                link = steps.on(dve)
                link(nc.vector.tensor_scalar(first[:, :], first[:, :], LOW, None, ALU.mult))
                for h in range(H):
                    m = nc.vector.tensor_tensor_scan(val[:, :, h], first[:, :], rows[:, :, h], LOW, ALU.add, ALU.max)
                link(m)
                link(nc.vector.tensor_copy(last[:, 0:H], val[:, cols - 1, :]))
        carry_over(nc, K, name + "cm", last, lown, ALU.add, ALU.max, LOW, carry, H)
        with nc.Block() as block:

            @block.vector
            def _(dve):
                for h in range(H):
                    m = nc.vector.scalar_tensor_tensor(out=val[:, :, h], in0=seen[:, :], scalar=carry[:, h:h + 1],
                                                       in1=val[:, :, h], op0=ALU.add, op1=ALU.max)
                m.then_inc(zeroed, 1)

            @block.sync
            def _(sp):
                sp.wait_ge(zeroed, 2)
                sp.dma_start(onp(maxd), val[:, :, :]).then_inc(stored, 16)
                sp.wait_ge(stored, 48)
        gather_columns(nc, name + "n", maxd, H, endi[:, :], mn[:, :, :], NB, 7)
        with nc.Block() as block:

            @block.vector
            def _(dve):
                link = steps.on(dve)
                hb = has[:, :].unsqueeze(2).to_broadcast([P, NB, H])
                link(nc.vector.tensor_scalar(tmpn[:, :], has[:, :], -LOW, LOW, ALU.mult, ALU.add))
                link(nc.vector.tensor_tensor(mn[:, :, :], mn[:, :, :], hb, ALU.mult))
                link(nc.vector.tensor_tensor(mn[:, :, :], mn[:, :, :],
                                             tmpn[:, :].unsqueeze(2).to_broadcast([P, NB, H]), ALU.add))
                link(nc.vector.tensor_tensor(mn[:, :, :], mn[:, :, :], asn[:, 0:NB, :], ALU.max))
                link(nc.vector.tensor_tensor(mn[:, :, :], mn[:, :, :], adn[:, 0:NB, :], ALU.add))
                link(nc.vector.scalar_tensor_tensor(out=mn[:, :, :], in0=mn[:, :, :], scalar=SLOPE, in1=mn[:, :, :],
                                                    op0=ALU.mult, op1=ALU.max))
        scatter_columns(nc, name + "sd", filld, H, starti[:, :], adn[:, 0:NB, :], NB, 7, NPOS - 1)
        scatter_columns(nc, name + "sm", fillm, H, starti[:, :], mn[:, :, :], NB, 7, NPOS - 1)
        for q, (d, tag) in enumerate(((filld, "fd"), (fillm, "fm"))):
            with nc.Block() as block:

                @block.sync
                def _(sp):
                    sp.dma_start(val[:, :, :], onp(d)).then_inc(loaded, 16)

                @block.vector
                def _(dve):
                    link = steps.on(dve)
                    dve.wait_ge(loaded, 48 + 16 * q)
                    for h in range(H):
                        m = nc.vector.tensor_tensor_scan(val[:, :, h], inner[:, :], val[:, :, h], 0.0,
                                                         ALU.mult, ALU.add)
                    link(m)
                    link(nc.vector.tensor_copy(last[:, 0:H], val[:, cols - 1, :]))
            carry_over(nc, K, name + tag, last, inall, ALU.mult, ALU.add, 0.0, carry, H)
            with nc.Block() as block:

                @block.vector
                def _(dve):
                    link = steps.on(dve)
                    for h in range(H):
                        m = nc.vector.scalar_tensor_tensor(out=val[:, :, h], in0=before[:, :],
                                                           scalar=carry[:, h:h + 1], in1=val[:, :, h],
                                                           op0=ALU.mult, op1=ALU.add)
                    link(m)
                    if q == 0:
                        link(nc.vector.tensor_tensor(rows[:, :, 0:H], rows[:, :, 0:H], val[:, :, :], ALU.add))
                        link(nc.vector.scalar_tensor_tensor(out=rows[:, :, 0:H], in0=rows[:, :, 0:H], scalar=SLOPE,
                                                            in1=rows[:, :, 0:H], op0=ALU.mult, op1=ALU.max))
                    else:
                        link(nc.vector.tensor_tensor(rows[:, :, 0:H], rows[:, :, 0:H], val[:, :, :], ALU.subtract))
                        link(nc.vector.tensor_scalar(first[:, :], dstf[:, :], 0.0, None, ALU.is_ge))
                        nc.vector.tensor_tensor(rows[:, :, 0:H], rows[:, :, 0:H],
                                                first[:, :].unsqueeze(2).to_broadcast([P, cols, H]), ALU.mult)\
                          .then_inc(zeroed, 1)

                @block.scalar
                def _(act):
                    if q == 1:
                        act.wait_ge(zeroed, 3)
                        nc.scalar.activation(rows[:, :, 0:H], rows[:, :, 0:H], ACT.Exp)
    return {"prs": prs, "rows": rows, "first": first, "inner": inner, "before": before, "inall": inall,
            "last": last, "carry": carry, "endi": endi, "has": has}


def edge_records(nc, K, name, cols, H, ed, records):
    R = H + 2
    KB = cols // P
    rows, prs, low, srcf = ed["rows"], ed["prs"], ed["inner"], ed["first"]
    with Ctx(nc, name) as c:
        rec = c.sb("rec", [P, cols, R])
        turnp = [c.ps(f"turnp{j}", [P, 4, P]) for j in range(4)]
        ready, turned, taken, stored, ch = (c.sem(n) for n in ("ready", "turned", "taken", "stored", "ch"))
        fields = [rows[:, :, h] for h in range(H)] + [low[:, :], srcf[:, :]]
        groups = [(f, k) for f in range(R) for k in range(0, KB, 4)]
        out = rec[:, :, :].rearrange("e (p k) r -> e r k p", k=KB)
        with nc.Block() as block:

            @block.vector
            def _(dve):
                link = Link(dve, ch)
                link(nc.vector.tensor_scalar(srcf[:, :], prs[:, :, 1], 0.0, 1000.0, ALU.is_lt, ALU.mult))
                link(nc.vector.tensor_scalar(prs[:, :, 1], prs[:, :, 1], 127, None, ALU.bitwise_and))
                link(nc.vector.tensor_copy(low[:, :], prs[:, :, 1]))
                link(nc.vector.tensor_tensor(low[:, :], low[:, :], srcf[:, :], ALU.add))
                nc.vector.tensor_copy(srcf[:, :], prs[:, :, 0]).then_inc(ready, 1)
                for g, (f, k) in enumerate(groups):
                    n = min(4, KB - k)
                    dve.wait_ge(turned, g + 1)
                    o = out[:, f, k:k + n, :]
                    if f == H + 1:
                        o = rec[:, :, :].bitcast(I32).rearrange("e (p k) r -> e r k p", k=KB)[:, f, k:k + n, :]
                    nc.vector.tensor_copy(o, turnp[g % 4][:, 0:n, :]).then_inc(taken, 1)

            @block.tensor
            def _(pe):
                pe.wait_ge(ready, 1)
                for g, (f, k) in enumerate(groups):
                    if g >= 4:
                        pe.wait_ge(taken, g - 3)
                    for j in range(min(4, KB - k)):
                        mm = nc.tensor.transpose(turnp[g % 4][:, j, :], fields[f][:, (k + j) * P:(k + j + 1) * P],
                                                 K["ident"][:, :])
                    mm.then_inc(turned, 1)

            @block.sync
            def _(sp):
                sp.wait_ge(taken, len(groups))
                sp.dma_start(records, rec[:, :, :].rearrange("p t r -> p (t r)")).then_inc(stored, 16)
                sp.wait_ge(stored, 16)


def sum_messages(nc, K, name, tiles, H, htab, records, blk, acc):
    SLOTS, PAGES, BANKS = 4, TURN // LOT, 8
    R, D, W = H + 2, DIM // H, DIM + H
    L = tiles // LOT
    assert L % PAGES == 0
    with Ctx(nc, name) as c:
        rec = [c.sb(f"rec{q}", [P, LOT, R]) for q in range(PAGES)]
        hrow = [c.sb(f"hrow{q}", [P, LOT, DIM]) for q in range(SLOTS)]
        msg = [c.sb(f"msg{q}", [P, LOT, W]) for q in range(SLOTS)]
        to = [c.sb(f"to{q}", [P, LOT, P]) for q in range(SLOTS)]
        sump = [c.ps(f"sump{j}", [P, 512]) for j in range(BANKS)]
        msg_ready, summed, added, passed = (c.sem(n) for n in ("msg_ready", "summed", "added", "passed"))
        rec_in = [c.sem(f"rec_in{q}") for q in range(PAGES)]
        landed = [c.sem(f"landed{q}") for q in range(SLOTS)]
        with nc.Block() as block:

            @block.sync
            def _(sp):
                def load(q, col):
                    sp.dma_start(rec[q][:, :, :].rearrange("p t r -> p (t r)"),
                                 records[:, bass.ds(col, LOT * R)]).then_inc(rec_in[q], 16)

                for q in range(PAGES):
                    load(q, q * LOT * R)
                with sp.Fori(0, L // PAGES) as i:
                    for q in range(PAGES):
                        sp.wait_ge(msg_ready, i * TURN + q * LOT + LOT)
                        load(q, i * (TURN * R) + (q + PAGES) * LOT * R)
                for q in range(PAGES):
                    sp.wait_ge(rec_in[q], (L // PAGES + 1) * 16)

            @block.gpsimd
            def _(pool):
                def gather(q):
                    for u in range(LOT):
                        nc.gpsimd.indirect_dma_start(
                            hrow[q % SLOTS][:, u, :], None, htab,
                            bass.IndirectOffsetOnAxis(ap=rec[q][:, u, R - 1:R].bitcast(I32), axis=0))\
                          .then_inc(landed[q % SLOTS], 16)

                for q in range(SLOTS):
                    pool.wait_ge(rec_in[q], 16)
                    gather(q)
                with pool.Fori(0, L // PAGES) as i:
                    for q in range(PAGES):
                        nq = (q + SLOTS) % PAGES
                        pool.wait_ge(msg_ready, i * TURN + q * LOT + LOT)
                        pool.wait_ge(rec_in[nq], i * 16 + 16 * (1 + (q + SLOTS) // PAGES))
                        pool.sem_inc(passed, 1)
                        gather(nq)

            @block.vector
            def _(dve):
                def rows_to(q, turn, wrap):
                    s = q % SLOTS
                    per = PAGES // SLOTS
                    dve.wait_ge(rec_in[q], turn * 16 + 16 * (1 + wrap))
                    dve.wait_ge(landed[s], turn * (16 * LOT * per) + 16 * LOT * (q // SLOTS + 1 + per * wrap))
                    nc.vector.tensor_tensor(to[s][:, :, :], K["iota"][:, :].unsqueeze(1).to_broadcast([P, LOT, P]),
                                            rec[q][:, :, H:H + 1].to_broadcast([P, LOT, P]), ALU.is_equal)
                    nc.vector.tensor_copy(msg[s][:, :, DIM:W], rec[q][:, :, 0:H])

                def message(q, u):
                    s = q % SLOTS
                    nc.vector.tensor_tensor(
                        msg[s][:, u, 0:DIM].rearrange("p (a d) -> p a d", a=H),
                        hrow[s][:, u, :].rearrange("p (a d) -> p a d", a=H),
                        rec[q][:, u, 0:H].unsqueeze(2).to_broadcast([P, H, D]), ALU.mult).then_inc(msg_ready, 1)

                nc.vector.memset(acc[:, :, :], 0.0).then_inc(added, BANKS)
                rows_to(0, 0, 0)
                for u in range(LOT):
                    message(0, u)
                with dve.Fori(0, L // PAGES) as i:
                    for q in range(PAGES):
                        _, b = nc.values_load_multi_w_load_instructions(
                            blk[0:1, bass.ds(i * TURN + q * LOT, LOT)], engines=[mybir.EngineType.DVE],
                            min_val=0, max_val=NB - 1)
                        nq = (q + 1) % PAGES
                        rows_to(nq, i, (q + 1) // PAGES)
                        for u in range(LOT):
                            t = i * TURN + q * LOT + u
                            message(nq, u)
                            dve.wait_ge(summed, t + 1)
                            dve.wait_ge(added, t + BANKS)
                            a = acc[:, bass.ds(b[u], 1), :].rearrange("p a c -> p (a c)")
                            nc.vector.tensor_tensor(a, a, sump[(q * LOT + u) % BANKS][:, 0:W], ALU.add)\
                              .then_inc(added, 1)
                for s in range(SLOTS):
                    dve.wait_ge(landed[s], (L // SLOTS + 1) * 16 * LOT)

            @block.tensor
            def _(pe):
                with pe.Fori(0, L // PAGES) as i:
                    for q in range(PAGES):
                        for u in range(LOT):
                            t = i * TURN + q * LOT + u
                            pe.wait_ge(msg_ready, t + 1)
                            pe.wait_ge(added, t + 1)
                            nc.tensor.matmul(sump[(q * LOT + u) % BANKS][:, 0:W], to[q % SLOTS][:, u, :],
                                             msg[q % SLOTS][:, u, :],
                                             start=True, stop=True).then_inc(summed, 1)


def pad_rows(nc, name, x, xp, tails):
    extra = ROWS - NODES
    with Ctx(nc, name) as c:
        zero = c.sb("zero", [P, extra * DIM // 100])
        copied, cleared = c.sem("copied"), c.sem("cleared")
        with nc.Block() as block:

            @block.vector
            def _(dve):
                nc.vector.memset(zero[:, :], 0.0).then_inc(cleared, 1)

            @block.sync
            def _(sp):
                sp.dma_start(xp[0:NODES, :].rearrange("(a b) d -> a (b d)", a=100),
                             x.rearrange("(a b) d -> a (b d)", a=100)).then_inc(copied, 16)
                sp.wait_ge(cleared, 1)
                sp.dma_start(xp[NODES:ROWS, :].rearrange("(a b) d -> a (b d)", a=100), zero[0:100, :])\
                  .then_inc(copied, 16)
                for d in tails:
                    sp.dma_start(d[NB * P:ROWS, :].rearrange("(a b) d -> a (b d)", a=P),
                                 zero[:, 0:(ROWS - NB * P) * DIM // P]).then_inc(copied, 16)
                sp.wait_ge(copied, 32 + 16 * len(tails))


def node_tables(nc, K, name, xin, w, F, H, att_src, att_dst, htab, atab, asn, adn, hn):
    N = ROWS // P // 2
    D = F // H
    AW = H if hn is None else H + F
    with Ctx(nc, name) as c:
        ws = c.sb("ws", [P, KC, F])
        att = c.sb("att", [P, 2, F])
        x = [c.sb(f"x{h}", [P, 2, DIM]) for h in range(2)]
        xn = [c.sb(f"xn{h}", [P, 2, DIM]) for h in range(2)]
        xT = [c.sb(f"xT{h}", [P, KC, 2, P]) for h in range(2)]
        hs = [c.sb(f"hs{h}", [P, 2, F]) for h in range(2)]
        ab = [c.sb(f"ab{h}", [P, 2, AW]) for h in range(2)]
        stats, mv, sd, rstd = c.sb("stats", [P, 2, 6]), c.sb("mv", [P, 2, 2]), c.sb("sd", [P, 2, 1]), c.sb("rstd", [P, 2, 1])
        prod = c.sb("prod", [P, 2, 2, F])
        red = c.sb("red", [P, 2, 2, H])
        xTp = [c.ps(f"xTp{h}", [P, KC, 2, P]) for h in range(2)]
        hp = [c.ps(f"hp{h}", [P, 512]) for h in range(2)]
        (w_in, var_ready, sd_ready, xn_ready, xT_ready, xT_copied, h_ready, h_copied, ab_ready, ch) = (
            c.sem(n) for n in ("w_in", "var_ready", "sd_ready", "xn_ready", "xT_ready", "xT_copied", "h_ready",
                               "h_copied", "ab_ready", "ch"))
        x_in = [c.sem(f"x_in{h}") for h in range(2)]
        stored = [c.sem(f"stored{h}") for h in range(2)]
        slot_free, passed = c.sem("slot_free"), c.sem("passed")
        stores = 1 + (hn is None)
        xv = xin.rearrange("(b p) d -> p b d", p=P)
        av = atab.rearrange("(b p) d -> p b d", p=P)
        hv = htab.rearrange("(b p) d -> p b d", p=P) if hn is None else None
        LINKS = 8
        with nc.Block() as block:

            @block.sync
            def _(sp):
                sp.dma_start(ws[:, :, :], w.rearrange("(k p) f -> p k f", p=P)).then_inc(w_in, 16)
                sp.dma_start(att[:, 0, :], att_src.rearrange("h d -> (h d)").partition_broadcast(P)).then_inc(w_in, 16)
                sp.dma_start(att[:, 1, :], att_dst.rearrange("h d -> (h d)").partition_broadcast(P)).then_inc(w_in, 16)
                for h in range(2):
                    sp.dma_start(x[h][:, :, :], xv[:, 2 * h:2 * h + 2, :]).then_inc(x_in[h], 16)
                with sp.Fori(0, N // 2 - 1) as i:
                    for h in range(2):
                        sp.wait_ge(xn_ready, i * 2 + h + 1)
                        sp.dma_start(x[h][:, :, :], xv[:, bass.ds(i * 4 + 2 * h + 4, 2), :]).then_inc(x_in[h], 16)

            @block.scalar
            def _(act):
                act.wait_ge(w_in, 48)
                with act.Fori(0, N // 2) as i:
                    for h in range(2):
                        n = i * 2 + h
                        act.wait_ge(var_ready, n + 1)
                        nc.scalar.activation(sd[:, :, :], mv[:, :, 1:2], ACT.Sqrt, bias=K["eps"][:, 0:1])\
                          .then_inc(sd_ready, 1)
                        act.wait_ge(xT_ready, n + 1)
                        nc.scalar.copy(xT[h][:, :, :, :], xTp[h][:, :, :, :]).then_inc(xT_copied, 1)
                        act.wait_ge(h_ready, n + 1)
                        act.wait_ge(slot_free, n + 1)
                        nc.scalar.copy(hs[h][:, :, :], hp[h][:, 0:2 * F].rearrange("p (a f) -> p a f", a=2))\
                          .then_inc(h_copied, 1)

            @block.tensor
            def _(pe):
                pe.wait_ge(w_in, 48)
                with pe.Fori(0, N // 2) as i:
                    for h in range(2):
                        n = i * 2 + h
                        pe.wait_ge(xn_ready, n + 1)
                        for k in range(KC):
                            for j in range(2):
                                mm = nc.tensor.transpose(xTp[h][:, k, j, :], xn[h][:, j, k * P:(k + 1) * P],
                                                         K["ident"][:, :])
                        mm.then_inc(xT_ready, 1)
                        pe.wait_ge(xT_copied, n + 1)
                        for j in range(2):
                            for k in range(KC):
                                mm = nc.tensor.matmul(hp[h][:, j * F:(j + 1) * F], xT[h][:, k, j, :], ws[:, k, :],
                                                      start=(k == 0), stop=(k == KC - 1))
                        mm.then_inc(h_ready, 1)

            @block.vector
            def _(dve):
                dve.wait_ge(w_in, 48)
                dve.sem_inc(slot_free, 2)
                with dve.Fori(0, N // 2) as i:
                    for h in range(2):
                        n = i * 2 + h
                        link = Link(dve, ch, i * (2 * LINKS) + h * LINKS)
                        dve.wait_ge(x_in[h], i * 16 + 16)
                        for j in range(2):
                            m = nc.vector.bn_stats(stats[:, j, :], x[h][:, j, :])
                        link(m)
                        dve.sem_inc(passed, 1)
                        for j in range(2):
                            m = nc.vector.bn_aggr(mv[:, j, :], stats[:, j, :])
                        m.then_inc(var_ready, 1)
                        dve.wait_ge(sd_ready, n + 1)
                        link(nc.vector.reciprocal(rstd[:, :, :], sd[:, :, :]))
                        for j in range(2):
                            m = nc.vector.tensor_scalar(xn[h][:, j, :], x[h][:, j, :], mv[:, j, 0:1], rstd[:, j, :],
                                                        ALU.subtract, ALU.mult)
                        m.then_inc(xn_ready, 1)
                        dve.wait_ge(h_copied, n + 1)
                        for q in range(2):
                            m = nc.vector.tensor_tensor(prod[:, q, :, :], hs[h][:, :, :],
                                                        att[:, q, :].unsqueeze(1).to_broadcast([P, 2, F]), ALU.mult)
                        link(m)
                        link(nc.vector.tensor_reduce(red[:, :, :, :].rearrange("p q a h -> p (q a h)"),
                                                     prod[:, :, :, :].rearrange("p q a (h d) -> p (q a h) d", h=H),
                                                     AX.X, ALU.add))
                        link(nc.vector.tensor_tensor(asn[:, bass.ds(n * 2, 2), :], red[:, 0, :, :], red[:, 0, :, :],
                                                     ALU.max))
                        link(nc.vector.tensor_tensor(adn[:, bass.ds(n * 2, 2), :], red[:, 1, :, :], red[:, 1, :, :],
                                                     ALU.max))
                        if hn is not None:
                            link(nc.vector.tensor_tensor(hn[:, bass.ds(n * 2, 2), :], hs[h][:, :, :], hs[h][:, :, :],
                                                         ALU.max))
                            nc.vector.tensor_copy(ab[h][:, :, H:H + F], hs[h][:, :, :])
                        else:
                            link(nc.vector.tensor_copy(ab[h][:, :, 0:1], red[:, 0, :, 0:1]))
                        link(nc.vector.tensor_copy(ab[h][:, :, 0:H], red[:, 0, :, :]))
                        dve.sem_inc(ab_ready, 1)
                        assert link.n == LINKS

            @block.gpsimd
            def _(pool):
                with pool.Fori(0, N // 2) as i:
                    for h in range(2):
                        n = i * 2 + h
                        pool.wait_ge(ab_ready, n + 1)
                        pool.dma_start(av[:, bass.ds(n * 2, 2), :], ab[h][:, :, :]).then_inc(stored[h], 16)
                        if hn is None:
                            pool.dma_start(hv[:, bass.ds(n * 2, 2), :], hs[h][:, :, :]).then_inc(stored[h], 16)
                        pool.wait_ge(stored[h], i * (16 * stores) + 16 * stores)
                        pool.sem_inc(slot_free, 1)


def finish_attention(nc, K, name, acc, H, htab, asn, adn, mn, xin, xout, bias, norm):
    D, W = DIM // H, DIM + H
    LINKS = 5 if norm is None else 9
    with Ctx(nc, name) as c:
        own = c.sb("own", [P, NB, H])
        rden = c.sb("rden", [P, NB, H])
        par = c.sb("par", [P, 3, DIM])
        hr = [c.sb(f"hr{h}", [P, DIM]) for h in range(2)]
        x = [c.sb(f"x{h}", [P, DIM]) for h in range(2)]
        t = c.sb("t", [P, DIM])
        y = [c.sb(f"y{h}", [P, DIM]) for h in range(2)]
        stats, mv, sd, rstd = c.sb("stats", [P, 6]), c.sb("mv", [P, 2]), c.sb("sd", [P, 1]), c.sb("rstd", [P, 1])
        par_in, score_ready, own_ready, ch, done, var_ready, sd_ready, slot_free = (
            c.sem(n) for n in ("par_in", "score_ready", "own_ready", "ch", "done", "var_ready", "sd_ready",
                               "slot_free"))
        passed = c.sem("passed")
        x_in = [c.sem(f"x_in{h}") for h in range(2)]
        stored = [c.sem(f"stored{h}") for h in range(2)]
        blocks = lambda d: d.rearrange("(b p) d -> b p d", p=P)
        xv, hv, ov = blocks(xin), blocks(htab), blocks(xout)
        one = lambda a, b: a[:, bass.ds(b, 1), :].rearrange("p a h -> p (a h)").unsqueeze(2).to_broadcast([P, H, D])
        heads = lambda a: a.rearrange("p (h d) -> p h d", h=H)
        with nc.Block() as block:

            @block.sync
            def _(sp):
                for q, a in enumerate([bias] + list(norm or ())):
                    sp.dma_start(par[:, q, :], a.partition_broadcast(P)).then_inc(par_in, 16)

                def load(h, b):
                    sp.dma_start(x[h][:, :], xv[bass.ds(b, 1), :, :].rearrange("a p d -> p (a d)"))\
                      .then_inc(x_in[h], 16)
                    sp.dma_start(hr[h][:, :], hv[bass.ds(b, 1), :, :].rearrange("a p d -> p (a d)"))\
                      .then_inc(x_in[h], 16)

                load(0, 0)
                load(1, 1)
                with sp.Fori(0, NB // 2 - 1) as i:
                    for h in range(2):
                        sp.wait_ge(done, i * 2 + h + 1)
                        load(h, i * 2 + h + 2)

            @block.gpsimd
            def _(pool):
                with pool.Fori(0, NB // 2) as i:
                    for h in range(2):
                        pool.wait_ge(done, i * 2 + h + 1)
                        pool.dma_start(ov[bass.ds(i * 2 + h, 1), :, :].rearrange("a p d -> p (a d)"), y[h][:, :])\
                            .then_inc(stored[h], 16)
                        pool.wait_ge(stored[h], i * 16 + 16)
                        pool.sem_inc(slot_free, 1)

            @block.scalar
            def _(act):
                act.wait_ge(score_ready, 1)
                nc.scalar.activation(own[:, :, :], own[:, :, :], ACT.Exp).then_inc(own_ready, 1)
                if norm is not None:
                    with act.Fori(0, NB) as b:
                        act.wait_ge(var_ready, b + 1)
                        nc.scalar.activation(sd[:, :], mv[:, 1:2], ACT.Sqrt, bias=K["eps"][:, 0:1])\
                          .then_inc(sd_ready, 1)

            @block.vector
            def _(dve):
                link = Link(dve, ch)
                dve.sem_inc(slot_free, 2)
                link(nc.vector.tensor_tensor(own[:, :, :], asn[:, 0:NB, :], adn[:, 0:NB, :], ALU.add))
                link(nc.vector.scalar_tensor_tensor(out=own[:, :, :], in0=own[:, :, :], scalar=SLOPE,
                                                    in1=own[:, :, :], op0=ALU.mult, op1=ALU.max))
                link(nc.vector.tensor_tensor(own[:, :, :], own[:, :, :], mn[:, :, :], ALU.subtract))
                dve.sem_inc(score_ready, 1)
                dve.wait_ge(own_ready, 1)
                link(nc.vector.tensor_tensor(rden[:, :, :], own[:, :, :], acc[:, :, DIM:W], ALU.add))
                link(nc.vector.reciprocal(rden[:, :, :], rden[:, :, :]))
                dve.wait_ge(par_in, 16 * (1 + (2 if norm else 0)))
                base = link.n
                with dve.Fori(0, NB // 2) as i:
                    for h in range(2):
                        b = i * 2 + h
                        link = Link(dve, ch, i * (2 * LINKS) + h * LINKS + base)
                        dve.wait_ge(x_in[h], i * 32 + 32)
                        link(nc.vector.tensor_tensor(heads(t[:, :]), heads(hr[h][:, :]), one(own, b), ALU.mult))
                        link(nc.vector.tensor_tensor(t[:, :], t[:, :],
                                                     acc[:, bass.ds(b, 1), 0:DIM].rearrange("p a d -> p (a d)"),
                                                     ALU.add))
                        link(nc.vector.tensor_tensor(heads(t[:, :]), heads(t[:, :]), one(rden, b), ALU.mult))
                        link(nc.vector.tensor_tensor(t[:, :], t[:, :], par[:, 0, :], ALU.add))
                        if norm is not None:
                            link(nc.vector.bn_stats(stats[:, :], t[:, :]))
                            dve.sem_inc(passed, 1)
                            nc.vector.bn_aggr(mv[:, :], stats[:, :]).then_inc(var_ready, 1)
                            dve.wait_ge(sd_ready, b + 1)
                            link(nc.vector.reciprocal(rstd[:, :], sd[:, :]))
                            link(nc.vector.tensor_scalar(t[:, :], t[:, :], mv[:, 0:1], rstd[:, :],
                                                         ALU.subtract, ALU.mult))
                            nc.vector.tensor_tensor(x[h][:, :], x[h][:, :], par[:, 2, :], ALU.add)
                            link(nc.vector.tensor_tensor(t[:, :], t[:, :], par[:, 1, :], ALU.mult))
                        dve.wait_ge(slot_free, b + 1)
                        link(nc.vector.tensor_tensor(y[h][:, :], t[:, :], x[h][:, :], ALU.add))
                        dve.sem_inc(done, 1)
                        assert link.n == LINKS


def normalise(nc, K, dve, link, x, stats, mv, sd, rstd, xn, var_ready, sd_ready, passed, count):
    for j in range(CHUNK):
        m = nc.vector.bn_stats(stats[:, j, :], x[:, j, :])
    link(m)
    dve.sem_inc(passed, 1)
    for j in range(CHUNK):
        m = nc.vector.bn_aggr(mv[:, j, :], stats[:, j, :])
    m.then_inc(var_ready, 1)
    dve.wait_ge(sd_ready, count)
    link(nc.vector.reciprocal(rstd[:, :, :], sd[:, :, :]))
    for j in range(CHUNK):
        m = nc.vector.tensor_scalar(xn[:, j, :], x[:, j, :], mv[:, j, 0:1], rstd[:, j, :], ALU.subtract, ALU.mult)
    return m


def mix_experts(nc, K, name, xin, xout, wr, br, w1, b1, bn1, w2, b2, bn2, wo, bo):
    NE = w1.shape[0]
    NT = CHUNK * P
    YPC = 2 * NE + 2
    LINKS = 8
    with Ctx(nc, name) as c:
        wrs, brs = c.sb("wrs", [P, KC, NE]), c.sb("brs", [P, NE])
        w1s, w2s, wos = (c.sb(n, [P, NE, KC, DIM]) for n in ("w1s", "w2s", "wos"))
        bos = c.sb("bos", [NE, DIM])
        par = c.sb("par", [P, 2, 5, NE, KC])
        scale, shift = c.sb("scale", [P, 2, NE, KC]), c.sb("shift", [P, 2, NE, KC])
        x, xn, y = (c.sb(n, [P, CHUNK, DIM]) for n in ("x", "xn", "y"))
        ysum = c.sb("ysum", [P, CHUNK, DIM])
        xT = c.sb("xT", [P, KC, NT])
        h1s = [c.sb(f"h1s{j}", [P, KC, NT]) for j in range(2)]
        h2s = [c.sb(f"h2s{j}", [P, KC, NT]) for j in range(2)]
        stats, mv = c.sb("stats", [P, CHUNK, 6]), c.sb("mv", [P, CHUNK, 2])
        sd, rstd = c.sb("sd", [P, CHUNK, 1]), c.sb("rstd", [P, CHUNK, 1])
        wgt, top, tot = c.sb("wgt", [P, CHUNK, NE]), c.sb("top", [P, CHUNK]), c.sb("tot", [P, CHUNK])
        wT = c.sb("wT", [NE, CHUNK, P])
        h1p = [c.ps(f"h1p{m}", [P, NT]) for m in range(KC)]
        h2p = [c.ps(f"h2p{m}", [P, NT]) for m in range(KC)]
        yp = [c.ps(f"yp{m}", [P, 2, DIM]) for m in range(2)]
        tp = [c.ps(f"tp{m}", [P, CHUNK, P]) for m in range(2)]
        (w_in, par_ready, root_ready, x_in, var_ready, sd_ready, xn_ready, xT_ready, xT_copied, logits_ready,
         scores_ready, exp_ready, wgt_ready, wT_ready, wT_copied, h1_ready, h1_done, h2_ready, h2_done, y_ready,
         y_used, x_used, ysum_ready, slot_free, stored, passed, ch) = (c.sem(n) for n in (
             "w_in", "par_ready", "root_ready", "x_in", "var_ready", "sd_ready", "xn_ready", "xT_ready", "xT_copied",
             "logits_ready", "scores_ready", "exp_ready", "wgt_ready", "wT_ready", "wT_copied", "h1_ready", "h1_done",
             "h2_ready", "h2_done", "y_ready", "y_used", "x_used", "ysum_ready", "slot_free", "stored", "passed",
             "ch"))
        xv = xin.rearrange("(b p) d -> p b d", p=P)
        ov = xout.rearrange("(b p) d -> p b d", p=P)
        loads = [(wrs[:, :, :], wr.rearrange("(k p) e -> p k e", p=P)), (brs[:, :], br.partition_broadcast(P)),
                 (bos[:, :], bo)]
        for s_, d in ((w1s, w1), (w2s, w2), (wos, wo)):
            loads += [(s_[:, e, :, :], d[e].rearrange("(k p) h -> p k h", p=P)) for e in range(NE)]
        for l, ps_ in enumerate(((b1,) + bn1, (b2,) + bn2)):
            for q, a in enumerate(ps_):
                loads += [(par[:, l, q, e, :], a[e].rearrange("(k p) -> p k", p=P)) for e in range(NE)]
        with nc.Block() as block:

            @block.sync
            def _(sp):
                sp.dma_start(x[:, :, :], xv[:, 0:CHUNK, :]).then_inc(x_in, 16)
                with nc.allow_non_contiguous_dma("features of a bias go to the partitions"):
                    for o, a in loads:
                        sp.dma_start(o, a).then_inc(w_in, 16)
                with sp.Fori(0, NCH - 1) as i:
                    sp.wait_ge(x_used, i + 1)
                    sp.dma_start(x[:, :, :], xv[:, bass.ds(i * CHUNK + CHUNK, CHUNK), :]).then_inc(x_in, 16)

            @block.gpsimd
            def _(pool):
                with pool.Fori(0, NCH) as i:
                    pool.wait_ge(ysum_ready, i + 1)
                    pool.dma_start(ov[:, bass.ds(i * CHUNK, CHUNK), :], y[:, :, :]).then_inc(stored, 16)
                    pool.wait_ge(stored, i * 16 + 16)
                    pool.sem_inc(slot_free, 1)

            @block.scalar
            def _(act):
                act.wait_ge(w_in, 16 * len(loads))
                nc.scalar.activation(scale[:, :, :, :], par[:, :, 4, :, :], ACT.Sqrt, bias=K["bneps"][:, 0:1])\
                  .then_inc(root_ready, 1)
                act.wait_ge(par_ready, 1)
                with act.Fori(0, NCH) as i:
                    act.wait_ge(var_ready, i + 1)
                    nc.scalar.activation(sd[:, :, :], mv[:, :, 1:2], ACT.Sqrt, bias=K["eps"][:, 0:1])\
                      .then_inc(sd_ready, 1)
                    for k in range(KC):
                        act.wait_ge(xT_ready, i * KC + k + 1)
                        nc.scalar.copy(xT[:, k, :], tp[k][:, :, :].rearrange("p a b -> p (a b)"))\
                          .then_inc(xT_copied, 1)
                    act.wait_ge(scores_ready, i + 1)
                    nc.scalar.activation(wgt[:, :, :], wgt[:, :, :], ACT.Exp).then_inc(exp_ready, 1)
                    for e in range(NE):
                        for l, (pp, hs, ready, done) in enumerate(((h1p, h1s, h1_ready, h1_done),
                                                                   (h2p, h2s, h2_ready, h2_done))):
                            for m in range(KC):
                                act.wait_ge(ready, i * (NE * KC) + e * KC + m + 1)
                                nc.scalar.activation(hs[e % 2][:, m, :], pp[m][:, :], ACT.Relu,
                                                     bias=shift[:, l, e, m:m + 1], scale=scale[:, l, e, m:m + 1])\
                                  .then_inc(done, 1)

            @block.tensor
            def _(pe):
                pe.wait_ge(w_in, 16 * len(loads))
                with pe.Fori(0, NCH) as i:
                    pe.wait_ge(xn_ready, i + 1)
                    for k in range(KC):
                        for j in range(CHUNK):
                            mm = nc.tensor.transpose(tp[k][:, j, :], xn[:, j, k * P:(k + 1) * P], K["ident"][:, :])
                        mm.then_inc(xT_ready, 1)

                    def layer(pp, ws, e, rhs, ready):
                        for m in range(KC):
                            for k in range(KC):
                                mm = nc.tensor.matmul(pp[m][:, :], ws[:, e, k, m * P:(m + 1) * P], rhs[:, k, :],
                                                      start=(k == 0), stop=(k == KC - 1))
                            mm.then_inc(ready, 1)

                    pe.wait_ge(xT_copied, i * KC + KC)
                    for j in range(CHUNK):
                        for k in range(KC):
                            mm = nc.tensor.matmul(tp[0][:, 0, j * NE:(j + 1) * NE], xT[:, k, j * P:(j + 1) * P],
                                                  wrs[:, k, :], start=(k == 0), stop=(k == KC - 1))
                    mm.then_inc(logits_ready, 1)
                    layer(h1p, w1s, 0, xT, h1_ready)
                    pe.wait_ge(wgt_ready, i + 1)
                    for j in range(CHUNK):
                        mm = nc.tensor.transpose(tp[1][0:NE, j, :], wgt[:, j, :], K["ident"][:, :])
                    mm.then_inc(wT_ready, 1)
                    pe.wait_ge(wT_copied, i + 1)
                    for j in range(CHUNK):
                        if j % 2 == 0:
                            pe.wait_ge(y_used, i * YPC + j // 2 + 1)
                        mm = nc.tensor.matmul(yp[j // 2][:, j % 2, :], wT[:, j, :], bos[:, :], start=True, stop=True)
                        if j % 2:
                            mm.then_inc(y_ready, 1)
                    for e in range(NE):
                        pe.wait_ge(h1_done, i * (NE * KC) + (e + 1) * KC)
                        layer(h2p, w2s, e, h1s[e % 2], h2_ready)
                        if e + 1 < NE:
                            layer(h1p, w1s, e + 1, xT, h1_ready)
                        pe.wait_ge(h2_done, i * (NE * KC) + (e + 1) * KC)
                        for j in range(CHUNK):
                            if j % 2 == 0:
                                pe.wait_ge(y_used, i * YPC + 2 * (e + 1) + j // 2 + 1)
                            for k in range(KC):
                                mm = nc.tensor.matmul(yp[j // 2][:, j % 2, :], h2s[e % 2][:, k, j * P:(j + 1) * P],
                                                      wos[:, e, k, :], start=(k == 0), stop=(k == KC - 1))
                            if j % 2:
                                mm.then_inc(y_ready, 1)

            @block.vector
            def _(dve):
                link = Link(dve, ch)
                dve.sem_inc(slot_free, 1)
                dve.sem_inc(y_used, 2)
                dve.wait_ge(root_ready, 1)
                link(nc.vector.reciprocal(scale[:, :, :, :], scale[:, :, :, :]))
                for l in range(2):
                    link(nc.vector.tensor_tensor(scale[:, l, :, :], scale[:, l, :, :], par[:, l, 1, :, :], ALU.mult))
                    link(nc.vector.tensor_tensor(shift[:, l, :, :], par[:, l, 0, :, :], par[:, l, 3, :, :],
                                                 ALU.subtract))
                    link(nc.vector.tensor_tensor(shift[:, l, :, :], shift[:, l, :, :], scale[:, l, :, :], ALU.mult))
                    link(nc.vector.tensor_tensor(shift[:, l, :, :], shift[:, l, :, :], par[:, l, 2, :, :], ALU.add))
                dve.sem_inc(par_ready, 1)
                base = link.n
                with dve.Fori(0, NCH) as i:
                    link = Link(dve, ch, i * LINKS + base)
                    dve.wait_ge(x_in, i * 16 + 16)
                    normalise(nc, K, dve, link, x, stats, mv, sd, rstd, xn, var_ready, sd_ready, passed, i + 1)\
                        .then_inc(xn_ready, 1)
                    dve.wait_ge(logits_ready, i + 1)
                    link(nc.vector.tensor_tensor(wgt[:, :, :],
                                                 tp[0][:, 0, 0:CHUNK * NE].rearrange("p (j e) -> p j e", e=NE),
                                                 brs[:, :].unsqueeze(1).to_broadcast([P, CHUNK, NE]), ALU.add))
                    link(nc.vector.tensor_reduce(top[:, :], wgt[:, :, :], AX.X, ALU.max))
                    link(nc.vector.tensor_tensor(wgt[:, :, :], wgt[:, :, :],
                                                 top[:, :].unsqueeze(2).to_broadcast([P, CHUNK, NE]), ALU.subtract))
                    dve.sem_inc(scores_ready, 1)
                    dve.wait_ge(exp_ready, i + 1)
                    link(nc.vector.tensor_reduce(tot[:, :], wgt[:, :, :], AX.X, ALU.add))
                    link(nc.vector.reciprocal(tot[:, :], tot[:, :]))
                    link(nc.vector.tensor_tensor(wgt[:, :, :], wgt[:, :, :],
                                                 tot[:, :].unsqueeze(2).to_broadcast([P, CHUNK, NE]), ALU.mult))
                    dve.sem_inc(wgt_ready, 1)
                    dve.wait_ge(wT_ready, i + 1)
                    nc.vector.tensor_copy(wT[:, :, :], tp[1][0:NE, :, :]).then_inc(wT_copied, 1)
                    for q in range(2):
                        dve.wait_ge(y_ready, i * YPC + q + 1)
                        nc.vector.tensor_tensor(ysum[:, 2 * q:2 * q + 2, :], x[:, 2 * q:2 * q + 2, :], yp[q][:, :, :],
                                                ALU.add).then_inc(y_used, 1)
                    dve.sem_inc(passed, 1)
                    dve.wait_ge(y_used, i * YPC + 4)
                    dve.sem_inc(x_used, 1)
                    for e in range(NE):
                        if e == NE - 1:
                            dve.wait_ge(slot_free, i + 1)
                        dve.wait_ge(y_used, i * YPC + 2 * e + 4)
                        o = y if e == NE - 1 else ysum
                        for q in range(2):
                            dve.wait_ge(y_ready, i * YPC + 2 * (e + 1) + q + 1)
                            for j in range(2 * q, 2 * q + 2):
                                m = nc.vector.scalar_tensor_tensor(out=o[:, j, :], in0=yp[q][:, j % 2, :],
                                                                   scalar=wgt[:, j, e:e + 1], in1=ysum[:, j, :],
                                                                   op0=ALU.mult, op1=ALU.add)
                            m.then_inc(y_used, 1)
                    dve.wait_ge(y_used, (i + 1) * YPC + 2)
                    dve.sem_inc(ysum_ready, 1)
                    assert link.n == LINKS


def sum_small_messages(nc, K, name, cols, H, F, ed, table, out):
    W, D = H + F, F // H
    rows, inner, before = ed["rows"], ed["inner"], ed["before"]
    last, carry = ed["last"], ed["carry"]
    with Ctx(nc, name) as c:
        steps, summed, stored = Link(None, c.sem("steps")), c.sem("summed"), c.sem("stored")
        with nc.Block() as block:

            @block.vector
            def _(dve):
                link = steps.on(dve)
                msg = rows[:, :, H:W].rearrange("p c (h d) -> p c h d", h=H)
                for h in range(H):
                    m = nc.vector.tensor_tensor(msg[:, :, h, :], msg[:, :, h, :],
                                                rows[:, :, h:h + 1].to_broadcast([P, cols, D]), ALU.mult)
                link(m)
                for f in range(W):
                    m = nc.vector.tensor_tensor_scan(rows[:, :, f], inner[:, :], rows[:, :, f], 0.0, ALU.mult, ALU.add)
                link(m)
                link(nc.vector.tensor_copy(last[:, 0:W], rows[:, cols - 1, :]))
        carry_over(nc, K, name + "c", last, ed["inall"], ALU.mult, ALU.add, 0.0, carry, W)
        with nc.Block() as block:

            @block.vector
            def _(dve):
                for f in range(W):
                    m = nc.vector.scalar_tensor_tensor(out=rows[:, :, f], in0=before[:, :], scalar=carry[:, f:f + 1],
                                                       in1=rows[:, :, f], op0=ALU.mult, op1=ALU.add)
                m.then_inc(summed, 1)

            @block.sync
            def _(sp):
                sp.wait_ge(summed, 1)
                sp.dma_start(table.rearrange("(p c) w -> p c w", p=P), rows[:, :, :]).then_inc(stored, 16)
                sp.wait_ge(stored, 16)
        gather_columns(nc, name + "g", table, W, ed["endi"][:, :], out, NB, 7)
        with nc.Block() as block:

            @block.vector
            def _(dve):
                link = steps.on(dve)
                link(nc.vector.tensor_tensor(out, out, ed["has"][:, :].unsqueeze(2).to_broadcast([P, NB, W]),
                                             ALU.mult))


def choose_experts(nc, K, name, sums, H, NE, asn, adn, mn, hn, bias, gamma, beta, gate):
    F = H * NE
    with Ctx(nc, name) as c:
        own = c.sb("own", [P, NB, H])
        den = c.sb("den", [P, NB, H])
        agg = c.sb("agg", [P, NB, F])
        sq = c.sb("sq", [P, NB, F])
        mean, var = c.sb("mean", [P, NB, 1]), c.sb("var", [P, NB, 1])
        par = c.sb("par", [P, 3, F])
        sc = c.sb("sc", [P, NB, NE])
        beat = c.sb("beat", [P, NB, NE])
        one = c.sb("one", [P, NB, NE])
        par_in, score_ready, own_ready, var_ready, sd_ready, top_ready, exp_ready, ch = (
            c.sem(n) for n in ("par_in", "score_ready", "own_ready", "var_ready", "sd_ready", "top_ready",
                               "exp_ready", "ch"))
        with nc.Block() as block:

            @block.sync
            def _(sp):
                for q, a in enumerate((bias, gamma, beta)):
                    sp.dma_start(par[:, q, :], a.partition_broadcast(P)).then_inc(par_in, 16)

            @block.scalar
            def _(act):
                act.wait_ge(score_ready, 1)
                nc.scalar.activation(own[:, :, :], own[:, :, :], ACT.Exp).then_inc(own_ready, 1)
                act.wait_ge(var_ready, 1)
                nc.scalar.activation(var[:, :, :], var[:, :, :], ACT.Sqrt, bias=K["eps"][:, 0:1])\
                  .then_inc(sd_ready, 1)
                act.wait_ge(top_ready, 1)
                nc.scalar.activation(sc[:, :, :], sc[:, :, :], ACT.Exp).then_inc(exp_ready, 1)

            @block.vector
            def _(dve):
                link = Link(dve, ch)
                tt, stt = nc.vector.tensor_tensor, nc.vector.scalar_tensor_tensor
                wide = lambda a, n: a.to_broadcast([P, NB, n])
                param = lambda q: par[:, q, :].unsqueeze(1).to_broadcast([P, NB, F])
                link(tt(own[:, :, :], asn[:, 0:NB, :], adn[:, 0:NB, :], ALU.add))
                link(stt(out=own[:, :, :], in0=own[:, :, :], scalar=SLOPE, in1=own[:, :, :], op0=ALU.mult,
                         op1=ALU.max))
                link(tt(own[:, :, :], own[:, :, :], mn[:, :, :], ALU.subtract))
                dve.sem_inc(score_ready, 1)
                dve.wait_ge(own_ready, 1)
                link(tt(den[:, :, :], own[:, :, :], sums[:, :, 0:H], ALU.add))
                link(nc.vector.tensor_scalar(den[:, :, :], den[:, :, :], 1e-16, None, ALU.add))
                link(nc.vector.reciprocal(den[:, :, :], den[:, :, :]))
                dve.wait_ge(par_in, 48)
                for h in range(H):
                    f = slice(h * NE, (h + 1) * NE)
                    link(tt(agg[:, :, f], hn[:, 0:NB, f], wide(own[:, :, h:h + 1], NE), ALU.mult))
                    link(tt(agg[:, :, f], agg[:, :, f], sums[:, :, H + h * NE:H + (h + 1) * NE], ALU.add))
                    link(tt(agg[:, :, f], agg[:, :, f], wide(den[:, :, h:h + 1], NE), ALU.mult))
                link(tt(agg[:, :, :], agg[:, :, :], param(0), ALU.add))
                link(nc.vector.tensor_reduce(mean[:, :, 0], agg[:, :, :], AX.X, ALU.add))
                link(nc.vector.tensor_scalar(mean[:, :, :], mean[:, :, :], 1.0 / F, None, ALU.mult))
                link(tt(agg[:, :, :], agg[:, :, :], wide(mean[:, :, :], F), ALU.subtract))
                link(tt(sq[:, :, :], agg[:, :, :], agg[:, :, :], ALU.mult))
                link(nc.vector.tensor_reduce(var[:, :, 0], sq[:, :, :], AX.X, ALU.add))
                link(nc.vector.tensor_scalar(var[:, :, :], var[:, :, :], 1.0 / F, None, ALU.mult))
                dve.sem_inc(var_ready, 1)
                dve.wait_ge(sd_ready, 1)
                link(nc.vector.reciprocal(var[:, :, :], var[:, :, :]))
                link(tt(agg[:, :, :], agg[:, :, :], wide(var[:, :, :], F), ALU.mult))
                link(tt(agg[:, :, :], agg[:, :, :], param(1), ALU.mult))
                link(tt(agg[:, :, :], agg[:, :, :], param(2), ALU.add))
                link(nc.vector.tensor_reduce(sc[:, :, :], agg[:, :, :].rearrange("p b (h e) -> p b e h", h=H),
                                             AX.X, ALU.add))
                link(nc.vector.tensor_scalar(sc[:, :, :], sc[:, :, :], 1.0 / H, None, ALU.mult))
                link(nc.vector.memset(beat[:, :, :], 0.0))
                for j in range(NE):
                    if j + 1 < NE:
                        n = NE - j - 1
                        link(tt(one[:, :, j + 1:NE], sc[:, :, j + 1:NE], wide(sc[:, :, j:j + 1], n), ALU.is_le))
                        link(tt(beat[:, :, j + 1:NE], beat[:, :, j + 1:NE], one[:, :, j + 1:NE], ALU.add))
                    if j:
                        link(tt(one[:, :, 0:j], sc[:, :, 0:j], wide(sc[:, :, j:j + 1], j), ALU.is_lt))
                        link(tt(beat[:, :, 0:j], beat[:, :, 0:j], one[:, :, 0:j], ALU.add))
                link(nc.vector.tensor_scalar(beat[:, :, :], beat[:, :, :], 2.0, None, ALU.is_lt))
                link(nc.vector.tensor_reduce(mean[:, :, 0], sc[:, :, :], AX.X, ALU.max))
                link(tt(sc[:, :, :], sc[:, :, :], wide(mean[:, :, :], NE), ALU.subtract))
                dve.sem_inc(top_ready, 1)
                dve.wait_ge(exp_ready, 1)
                link(tt(sc[:, :, :], sc[:, :, :], beat[:, :, :], ALU.mult))
                link(nc.vector.tensor_reduce(mean[:, :, 0], sc[:, :, :], AX.X, ALU.add))
                link(nc.vector.reciprocal(mean[:, :, :], mean[:, :, :]))
                link(nc.vector.memset(gate[:, :, :], 0.0))
                link(tt(gate[:, 0:NB, :], sc[:, :, :], wide(mean[:, :, :], NE), ALU.mult))


def gated_experts(nc, K, name, xin, out, w1, b1, w2, b2, gate):
    NE, _, HID = w1.shape
    HC = HID // P
    NT = CHUNK * P
    YPC = 2 * NE + 2
    FULL = NODES // NT
    LINKS = 3
    with Ctx(nc, name) as c:
        w1s = c.sb("w1s", [P, NE, KC, HID])
        w2s = c.sb("w2s", [P, NE, HC, DIM])
        b1s, b2s = c.sb("b1s", [P, NE, HC]), c.sb("b2s", [NE, DIM])
        x, xn, y, ysum = (c.sb(n, [P, CHUNK, DIM]) for n in ("x", "xn", "y", "ysum"))
        xT = c.sb("xT", [P, KC, NT])
        hs = [c.sb(f"hs{j}", [P, HC, NT]) for j in range(2)]
        stats, mv = c.sb("stats", [P, CHUNK, 6]), c.sb("mv", [P, CHUNK, 2])
        sd, rstd = c.sb("sd", [P, CHUNK, 1]), c.sb("rstd", [P, CHUNK, 1])
        wgt = c.sb("wgt", [P, CHUNK, NE])
        wT = c.sb("wT", [NE, CHUNK, P])
        hp = [c.ps(f"hp{m}", [P, NT]) for m in range(HC)]
        yp = [c.ps(f"yp{m}", [P, 2, DIM]) for m in range(2)]
        tp = [c.ps(f"tp{m}", [P, CHUNK, P]) for m in range(2)]
        names = ("w_in", "x_in", "var_ready", "sd_ready", "xn_ready", "xT_ready", "xT_copied", "wgt_ready",
                 "wT_ready", "wT_copied", "h_ready", "h_done", "y_ready", "y_used", "x_used", "ysum_ready",
                 "slot_free", "stored", "passed", "ch")
        (w_in, x_in, var_ready, sd_ready, xn_ready, xT_ready, xT_copied, wgt_ready, wT_ready, wT_copied, h_ready,
         h_done, y_ready, y_used, x_used, ysum_ready, slot_free, stored, passed, ch) = (c.sem(n) for n in names)
        xv = xin.rearrange("(b p) d -> p b d", p=P)
        loads = [(b2s[:, :], b2)]
        for e in range(NE):
            loads += [(w1s[:, e, :, :], w1[e].rearrange("(k p) h -> p k h", p=P)),
                      (w2s[:, e, :, :], w2[e].rearrange("(k p) h -> p k h", p=P)),
                      (b1s[:, e, :], b1[e].rearrange("(k p) -> p k", p=P))]
        with nc.Block() as block:

            @block.sync
            def _(sp):
                sp.dma_start(x[:, :, :], xv[:, 0:CHUNK, :]).then_inc(x_in, 16)
                with nc.allow_non_contiguous_dma("features of a bias go to the partitions"):
                    for o, a in loads:
                        sp.dma_start(o, a).then_inc(w_in, 16)
                with sp.Fori(0, NCH - 1) as i:
                    sp.wait_ge(x_used, i + 1)
                    sp.dma_start(x[:, :, :], xv[:, bass.ds(i * CHUNK + CHUNK, CHUNK), :]).then_inc(x_in, 16)

            @block.gpsimd
            def _(pool):
                ov = out[0:FULL * NT, :].rearrange("(b p) d -> p b d", p=P)
                with pool.Fori(0, FULL) as i:
                    pool.wait_ge(ysum_ready, i + 1)
                    pool.dma_start(ov[:, bass.ds(i * CHUNK, CHUNK), :], y[:, :, :]).then_inc(stored, 16)
                    pool.wait_ge(stored, i * 16 + 16)
                    pool.sem_inc(slot_free, 1)
                pool.wait_ge(ysum_ready, NCH)
                rest = NODES - FULL * NT
                pool.dma_start(out[FULL * NT:FULL * NT + P, :], y[:, 0, :]).then_inc(stored, 16)
                pool.dma_start(out[FULL * NT + P:NODES, :], y[0:rest - P, 1, :]).then_inc(stored, 16)
                pool.wait_ge(stored, FULL * 16 + 32)

            @block.scalar
            def _(act):
                act.wait_ge(w_in, 16 * len(loads))
                with act.Fori(0, NCH) as i:
                    act.wait_ge(var_ready, i + 1)
                    nc.scalar.activation(sd[:, :, :], mv[:, :, 1:2], ACT.Sqrt, bias=K["eps"][:, 0:1])\
                      .then_inc(sd_ready, 1)
                    for k in range(KC):
                        act.wait_ge(xT_ready, i * KC + k + 1)
                        nc.scalar.copy(xT[:, k, :], tp[k][:, :, :].rearrange("p a b -> p (a b)"))\
                          .then_inc(xT_copied, 1)
                    for e in range(NE):
                        for m in range(HC):
                            act.wait_ge(h_ready, i * (NE * HC) + e * HC + m + 1)
                            nc.scalar.activation(hs[e % 2][:, m, :], hp[m][:, :], ACT.Gelu, bias=b1s[:, e, m:m + 1])\
                              .then_inc(h_done, 1)

            @block.tensor
            def _(pe):
                pe.wait_ge(w_in, 16 * len(loads))
                pe.wait_ge(y_used, 2)
                with pe.Fori(0, NCH) as i:
                    pe.wait_ge(xn_ready, i + 1)
                    for k in range(KC):
                        for j in range(CHUNK):
                            mm = nc.tensor.transpose(tp[k][:, j, :], xn[:, j, k * P:(k + 1) * P], K["ident"][:, :])
                        mm.then_inc(xT_ready, 1)

                    def hidden(e):
                        for m in range(HC):
                            pe.wait_ge(h_done, i * (NE * HC) + e * HC + m + 1)
                            for k in range(KC):
                                mm = nc.tensor.matmul(hp[m][:, :], w1s[:, e, k, m * P:(m + 1) * P], xT[:, k, :],
                                                      start=(k == 0), stop=(k == KC - 1))
                            mm.then_inc(h_ready, 1)

                    pe.wait_ge(xT_copied, i * KC + KC)
                    pe.wait_ge(wgt_ready, i + 1)
                    for j in range(CHUNK):
                        mm = nc.tensor.transpose(tp[1][0:NE, j, :], wgt[:, j, :], K["ident"][:, :])
                    mm.then_inc(wT_ready, 1)
                    hidden(0)
                    pe.wait_ge(wT_copied, i + 1)
                    for j in range(CHUNK):
                        if j % 2 == 0:
                            pe.wait_ge(y_used, i * YPC + j // 2 + 1)
                        mm = nc.tensor.matmul(yp[j // 2][:, j % 2, :], wT[:, j, :], b2s[:, :], start=True, stop=True)
                        if j % 2:
                            mm.then_inc(y_ready, 1)
                    for e in range(NE):
                        if e + 1 < NE:
                            hidden(e + 1)
                        pe.wait_ge(h_done, i * (NE * HC) + (e + 2) * HC)
                        for j in range(CHUNK):
                            if j % 2 == 0:
                                pe.wait_ge(y_used, i * YPC + 2 * (e + 1) + j // 2 + 1)
                            for k in range(HC):
                                mm = nc.tensor.matmul(yp[j // 2][:, j % 2, :], hs[e % 2][:, k, j * P:(j + 1) * P],
                                                      w2s[:, e, k, :], start=(k == 0), stop=(k == HC - 1))
                            if j % 2:
                                mm.then_inc(y_ready, 1)

            @block.vector
            def _(dve):
                dve.sem_inc(slot_free, 1)
                dve.sem_inc(h_done, HC)
                dve.sem_inc(y_used, 2)
                with dve.Fori(0, NCH) as i:
                    link = Link(dve, ch, i * LINKS)
                    link(nc.vector.tensor_tensor(wgt[:, :, :], gate[:, bass.ds(i * CHUNK, CHUNK), :],
                                                 gate[:, bass.ds(i * CHUNK, CHUNK), :], ALU.max))
                    dve.sem_inc(wgt_ready, 1)
                    dve.wait_ge(x_in, i * 16 + 16)
                    normalise(nc, K, dve, link, x, stats, mv, sd, rstd, xn, var_ready, sd_ready, passed, i + 1)\
                        .then_inc(xn_ready, 1)
                    dve.wait_ge(wT_ready, i + 1)
                    nc.vector.tensor_copy(wT[:, :, :], tp[1][0:NE, :, :]).then_inc(wT_copied, 1)
                    for q in range(2):
                        dve.wait_ge(y_ready, i * YPC + q + 1)
                        nc.vector.tensor_tensor(ysum[:, 2 * q:2 * q + 2, :], x[:, 2 * q:2 * q + 2, :], yp[q][:, :, :],
                                                ALU.add).then_inc(y_used, 1)
                    dve.wait_ge(y_used, i * YPC + 4)
                    dve.sem_inc(x_used, 1)
                    for e in range(NE):
                        if e == NE - 1:
                            dve.wait_ge(slot_free, i + 1)
                        dve.wait_ge(y_used, i * YPC + 2 * e + 4)
                        o = y if e == NE - 1 else ysum
                        for q in range(2):
                            dve.wait_ge(y_ready, i * YPC + 2 * (e + 1) + q + 1)
                            for j in range(2 * q, 2 * q + 2):
                                m = nc.vector.scalar_tensor_tensor(out=o[:, j, :], in0=yp[q][:, j % 2, :],
                                                                   scalar=wgt[:, j, e:e + 1], in1=ysum[:, j, :],
                                                                   op0=ALU.mult, op1=ALU.add)
                            m.then_inc(y_used, 1)
                    dve.wait_ge(y_used, (i + 1) * YPC + 2)
                    dve.sem_inc(ysum_ready, 1)
                    assert link.n == LINKS


def graph_attention(nc, K, name, H, edges, xp, xout, w, att_src, att_dst, bias, norm, tables):
    cols, tiles, pairs, start, count, blk = edges
    htab, atab, scratch, records = tables
    with Ctx(nc, name) as c:
        asn, adn = c.sb("asn", [P, NCH * CHUNK, H]), c.sb("adn", [P, NCH * CHUNK, H])
        mn = c.sb("mn", [P, NB, H])
        node_tables(nc, K, name + "nt", xp, w, DIM, H, att_src, att_dst, htab, atab, asn, adn, None)
        with Ctx(nc, name + "ed") as e:
            ed = edge_weights(nc, K, e, name + "ew", cols, H, atab, H, pairs, start, count, asn, adn, mn, scratch)
            edge_records(nc, K, name + "er", cols, H, ed, records)
        with Ctx(nc, name + "ac") as e:
            acc = e.sb("acc", [P, NB, DIM + H])
            sum_messages(nc, K, name + "sm", tiles, H, htab, records, blk, acc)
            finish_attention(nc, K, name + "fa", acc, H, htab, asn, adn, mn, xp, xout, bias, norm)


def gnn_two_layers(nc, a, out):
    def dram(name, shape, dt=F32):
        return nc.dram_tensor(name, shape, dt).ap()

    with Ctx(nc, "k") as c:
        K = make_constants(nc, c)
        xs = [dram(f"x{j}", (ROWS, DIM)) for j in range(4)]
        pad_rows(nc, "pad", a["x"], xs[0], [xs[1], xs[3]])
        with Ctx(nc, "g") as g:
            E = a["src"].shape[0]
            most = -(-E // P) + NB
            tiles = -(-most // TURN) * TURN
            cols = -(-(tiles + TURN) // P) * P
            pairs = dram("pairs", (1 + P * cols, 2), I32)
            start, count = g.sb("start", [P, NB]), g.sb("count", [P, NB])
            blk = g.sb("blk", [1, cols], I32)
            sort_edges(nc, K, "sg", a["src"], a["dst"], cols, True, start, count, pairs, blk)
            htab = dram("htab", (ROWS, DIM))
            for layer in range(2):
                H = a[f"L{layer}_gnn_att_src"].shape[0]
                tables = (htab, dram(f"atab{layer}", (ROWS, H)),
                          [dram(f"{n}{layer}", (P * cols, H)) for n in ("maxd", "filld", "fillm")],
                          dram(f"records{layer}", (P, cols * (H + 2))))
                p = f"L{layer}_gnn_"
                norm = None if layer == 0 else (a[p + "gamma"], a[p + "beta"])
                graph_attention(nc, K, f"g{layer}", H, (cols, tiles, pairs, start, count, blk), xs[2 * layer],
                                xs[2 * layer + 1], a[p + "W"], a[p + "att_src"], a[p + "att_dst"], a[p + "bias"],
                                norm, tables)
                if layer == 0:
                    f = "L0_ffn_"
                    mix_experts(nc, K, "f0", xs[1], xs[2], a[f + "Wr"], a[f + "br"], a[f + "W1"], a[f + "b1"],
                                tuple(a[f + n] for n in ("g1", "be1", "m1", "v1")), a[f + "W2"], a[f + "b2"],
                                tuple(a[f + n] for n in ("g2", "be2", "m2", "v2")), a[f + "Wo"], a[f + "bo"])
        with Ctx(nc, "r") as r:
            f = "L1_ffn_"
            E = a[f + "edge_index"].shape[1]
            H, NE = a[f + "att_src"].shape
            F = H * NE
            cols = E // P
            pairs = dram("rpairs", (1 + E, 2), I32)
            start, count = r.sb("start", [P, NB]), r.sb("count", [P, NB])
            gate = r.sb("gate", [P, NCH * CHUNK, NE])
            sort_edges(nc, K, "sr", a[f + "edge_index"][0, :], a[f + "edge_index"][1, :], cols, False, start, count,
                       pairs)
            with Ctx(nc, "rn") as n:
                asn, adn = n.sb("asn", [P, NCH * CHUNK, H]), n.sb("adn", [P, NCH * CHUNK, H])
                mn = n.sb("mn", [P, NB, H])
                hn = n.sb("hn", [P, NCH * CHUNK, F])
                sums = n.sb("sums", [P, NB, H + F])
                table = dram("rtab", (ROWS, H + F))
                node_tables(nc, K, "rt", xs[3], a[f + "W_gat"], F, H, a[f + "att_src"], a[f + "att_dst"], None, table,
                            asn, adn, hn)
                with Ctx(nc, "re") as e:
                    ed = edge_weights(nc, K, e, "rw", cols, H, table, H + F, pairs, start, count, asn, adn, mn,
                                      [dram(f"r{n_}", (E, H)) for n_ in ("maxd", "filld", "fillm")])
                    sum_small_messages(nc, K, "rs", cols, H, F, ed, dram("rsum", (E, H + F)), sums[:, :, :])
                choose_experts(nc, K, "rc", sums, H, NE, asn, adn, mn, hn, a[f + "b_gat"], a[f + "ln_gamma"],
                               a[f + "ln_beta"], gate)
            gated_experts(nc, K, "f1", xs[3], out, a[f + "W1"], a[f + "b1"], a[f + "W2"], a[f + "b2"], gate)


_INS = ['x', 'src', 'dst', 'L0_gnn_W', 'L0_gnn_att_src', 'L0_gnn_att_dst', 'L0_gnn_bias', 'L0_ffn_Wr', 'L0_ffn_br',
        'L0_ffn_W1', 'L0_ffn_b1', 'L0_ffn_g1', 'L0_ffn_be1', 'L0_ffn_m1', 'L0_ffn_v1', 'L0_ffn_W2', 'L0_ffn_b2',
        'L0_ffn_g2', 'L0_ffn_be2', 'L0_ffn_m2', 'L0_ffn_v2', 'L0_ffn_Wo', 'L0_ffn_bo', 'L1_gnn_W', 'L1_gnn_att_src',
        'L1_gnn_att_dst', 'L1_gnn_bias', 'L1_gnn_gamma', 'L1_gnn_beta', 'L1_ffn_W_gat', 'L1_ffn_att_src',
        'L1_ffn_att_dst', 'L1_ffn_b_gat', 'L1_ffn_ln_gamma', 'L1_ffn_ln_beta', 'L1_ffn_W1', 'L1_ffn_b1', 'L1_ffn_W2',
        'L1_ffn_b2', 'L1_ffn_edge_index']


def kernel(**inputs):
    import numpy as _np
    import concourse.bacc as _bacc
    from concourse import mybir as _mybir
    from concourse.bass_utils import run_bass_kernel_spmd as _run

    nc = _bacc.Bacc("TRN2", target_bir_lowering=False, num_devices=1)
    arrays, args = {}, {}
    for name in _INS:
        a = _np.ascontiguousarray(inputs[name])
        arrays[f"in_{name}_dram"] = a
        args[name] = nc.dram_tensor(f"in_{name}_dram", a.shape, _mybir.dt.from_np(a.dtype),
                                    kind="ExternalInput").ap()
    out = nc.dram_tensor("out_0_dram", (NODES, DIM), F32, kind="ExternalOutput").ap()
    gnn_two_layers(nc, args, out)
    r = _run(nc, [arrays], core_ids=[0])
    return r.results[0]["out_0_dram"]
```

```python
from contextlib import ExitStack

import concourse.bass as bass
from concourse import mybir

ALU = mybir.AluOpType
ACT = mybir.ActivationFunctionType
AX = mybir.AxisListType
F32 = mybir.dt.float32
BF16 = mybir.dt.bfloat16
I32 = mybir.dt.int32

P = 128
NODES, DIM = 12500, 256
NB = -(-NODES // P)
CHUNK = 4
NCH = -(-NB // CHUNK)
ROWS = NCH * CHUNK * P
KC = DIM // P
FAR = 1 << 20
LOW = -1.0e30
SLOPE = 0.2
LN_EPS = 1e-5
BN_EPS = 1e-3
HALF = 8
BODY = 2 * HALF
LOT = 4
TURN = 8 * LOT


class Ctx:

    def __init__(self, nc, stage):
        self.nc, self.stage, self.stack, self.sems = nc, stage, ExitStack(), []

    def __enter__(self):
        self.stack.__enter__()
        return self

    def __exit__(self, *e):
        if e[0] is None and self.sems:
            self.nc.all_engine_barrier()
            self.nc.clear_and_free_semaphores(self.sems)
            self.nc.all_engine_barrier()
        return self.stack.__exit__(*e)

    def sb(self, name, shape, dt=F32):
        return self.stack.enter_context(self.nc.sbuf_tensor(f"{self.stage}_{name}", list(shape), dt))

    def ps(self, name, shape, dt=F32):
        return self.stack.enter_context(self.nc.psum_tensor(f"{self.stage}_{name}", list(shape), dt))

    def sem(self, name):
        self.sems.append(self.nc.alloc_semaphore(f"{self.stage}_{name}"))
        return self.sems[-1]


class Link:

    def __init__(self, eng, sem, base=0):
        self.eng, self.sem, self.base, self.n = eng, sem, base, 0

    def on(self, eng):
        self.eng = eng
        return self

    def __call__(self, ins):
        self.n += 1
        ins.then_inc(self.sem, 1)
        self.eng.wait_ge(self.sem, self.base + self.n)


def make_constants(nc, c):
    K = {
        "ident": c.sb("ident", [P, P]), "identb": c.sb("identb", [P, P], BF16),
        "ones": c.sb("ones", [P, P]), "upper": c.sb("upper", [P, P]),
        "iota": c.sb("iota", [P, P]), "iotab": c.sb("iotab", [P, P], BF16), "iotai": c.sb("iotai", [P, P], I32),
        "low": c.sb("low", [P, 1]), "eps": c.sb("eps", [P, 1]), "bneps": c.sb("bneps", [P, 1]),
    }
    filled, shaped = c.sem("filled"), c.sem("shaped")
    with nc.Block() as block:

        @block.gpsimd
        def _(pool):
            nc.gpsimd.memset(K["ident"][:, :], 0.0).then_inc(filled, 1)
            nc.gpsimd.memset(K["ones"][:, :], 1.0).then_inc(filled, 1)
            nc.gpsimd.memset(K["low"][:, :], LOW)
            nc.gpsimd.memset(K["eps"][:, :], LN_EPS)
            nc.gpsimd.memset(K["bneps"][:, :], BN_EPS)
            nc.gpsimd.iota(K["iotai"][:, :], [[1, P]], base=0, channel_multiplier=0).then_inc(shaped, 1)
            pool.wait_ge(filled, 2)
            nc.gpsimd.affine_select(out=K["ident"][:, :], in_=K["ident"][:, :], compare_op=ALU.not_equal, fill=1.0,
                                    base=0, pattern=[[-1, P]], channel_multiplier=1).then_inc(shaped, 1)
            nc.gpsimd.affine_select(out=K["upper"][:, :], in_=K["ones"][:, :], compare_op=ALU.is_gt, fill=0.0,
                                    base=0, pattern=[[1, P]], channel_multiplier=-1).then_inc(shaped, 1)

        @block.vector
        def _(dve):
            dve.wait_ge(shaped, 3)
            nc.vector.tensor_copy(K["identb"][:, :], K["ident"][:, :])
            nc.vector.tensor_copy(K["iota"][:, :], K["iotai"][:, :])
            nc.vector.tensor_copy(K["iotab"][:, :], K["iotai"][:, :])
    return K


def sort_edges(nc, K, name, src, dst, cols, padded, start, count, pairs, blk=None, beside=None):
    E = src.shape[0]
    full = E // P
    rest = E - full * P
    T = -(-E // (P * BODY)) * BODY
    N = T // HALF
    NPOS = P * cols
    with Ctx(nc, name) as c:
        if beside:
            srci, dsti, places, gather = beside
            part = places
            gather = Gather(nc, c, *gather)
        else:
            srci = c.sb("srci", [P, T], I32)
            dsti = c.sb("dsti", [P, T], I32)
            part = c.sb("part", [P, T + HALF], I32)
        lo = c.sb("lo", [P, T + HALF], BF16)
        hi = c.sb("hi", [P, T + HALF], BF16)
        skip = c.sb("skip", [P, T])
        blank = c.sb("blank", [P, cols, 2], I32) if NPOS > E else None
        lead = c.sb("lead", [1, 2], I32)
        ohlo = c.sb("ohlo", [P, 2, HALF, P], BF16)
        ohhi = c.sb("ohhi", [P, 2, HALF, NB], BF16)
        cleared, loaded, blanked, ch = c.sem("cleared"), c.sem("loaded"), c.sem("blanked"), c.sem("ch")
        ntr = full and (2 + 2 * (rest > 0))

        def onehots(slot, col):
            nc.vector.tensor_tensor(ohlo[:, slot, :, :], K["iotab"][:, :].unsqueeze(1).to_broadcast([P, HALF, P]),
                                    lo[:, bass.ds(col, HALF)].unsqueeze(2).to_broadcast([P, HALF, P]), ALU.is_equal)
            return nc.vector.tensor_tensor(ohhi[:, slot, :, :],
                                           K["iotab"][:, 0:NB].unsqueeze(1).to_broadcast([P, HALF, NB]),
                                           hi[:, bass.ds(col, HALF)].unsqueeze(2).to_broadcast([P, HALF, NB]),
                                           ALU.is_equal)

        def histogram(c2, block, countp, totalp, withinp):
            tilep = c2.ps("tilep", [P, 512]) if padded else None
            blkp = [c2.ps(f"blkp{j}", [P, 512]) for j in range(4)] if padded else []
            sizes = c2.sb("sizes", [P, NB])
            sizei = c2.sb("sizei", [P, NB], I32)
            ends = c2.sb("ends", [P, NB])
            firsts = c2.sb("firsts", [P, P])
            zero = c2.sb("zero", [P, NB])
            onehot_ready, onehot_used = c2.sem("digits_ready"), c2.sem("digits_used")
            count_ready, sums_ready = c2.sem("count_ready"), c2.sem("sums_ready")
            firsts_ready, turned, reached, summed = (
                c2.sem(s) for s in ("firsts_ready", "tile_turned", "reached", "summed"))
            if padded:
                tilei = c2.sb("tilei", [P, cols], I32)
                tilef = c2.sb("tilef", [P, cols])
                tcol = c2.sb("tcol", [P, 1])
                reach = c2.sb("reach", [P, cols])
                numbered = c2.sem("numbered")
            W = cols // 4

            @block.sync
            def _(sp):
                sp.wait_ge(cleared, 3)
                for ap, t in ((src, srci), (dst, dsti)):
                    sp.dma_start(t[:, 0:full], ap[0:full * P].rearrange("(p c) -> p c", p=P)).then_inc(loaded, 16)
                    if rest:
                        sp.dma_start(t[0:rest, full:full + 1],
                                     ap[full * P:E].rearrange("(p c) -> p c", c=1)).then_inc(loaded, 16)
                sp.wait_ge(cleared, 6)
                sp.dma_start(pairs[0:1, :], lead[:, :]).then_inc(blanked, 16)
                if blank is not None:
                    sp.dma_start(pairs[1:1 + NPOS, :].rearrange("(p c) w -> p c w", p=P), blank[:, :, :])\
                      .then_inc(blanked, 16)
                sp.wait_ge(blanked, 16 * (1 + (blank is not None)))

            @block.vector
            def _(dve):
                link = Link(dve, ch)
                nc.vector.memset(srci[:, :], 0).then_inc(cleared, 1)
                nc.vector.memset(dsti[:, :], -1).then_inc(cleared, 1)
                nc.vector.memset(part[:, :], -1).then_inc(cleared, 1)
                nc.vector.memset(zero[:, :], 0.0).then_inc(onehot_used, 2)
                if blank is not None:
                    nc.vector.memset(blank[:, :, 0:1], 0).then_inc(cleared, 1)
                    nc.vector.memset(blank[:, :, 1:2], -1).then_inc(cleared, 1)
                nc.vector.memset(lead[:, :], -2).then_inc(cleared, 3 if blank is None else 1)
                dve.wait_ge(loaded, 16 * ntr)
                dve.wait_ge(cleared, 6)
                link(nc.vector.tensor_scalar(part[:, 0:T], dsti[:, 0:T], 127, None, ALU.bitwise_and))
                link(nc.vector.tensor_copy(lo[:, :], part[:, 0:T + HALF]))
                link(nc.vector.tensor_scalar(part[:, 0:T], dsti[:, 0:T], 7, None, ALU.arith_shift_right))
                link(nc.vector.memset(part[:, T:T + HALF], -1))
                link(nc.vector.tensor_copy(hi[:, :], part[:, 0:T + HALF]))
                link(nc.vector.tensor_scalar(skip[:, :], hi[:, 0:T], 0.0, float(FAR), ALU.is_lt, ALU.mult))
                with dve.Fori(0, N // 2) as i:
                    for h in range(2):
                        dve.wait_ge(onehot_used, i * 2 + h + 1)
                        onehots(h, i * BODY + h * HALF).then_inc(onehot_ready, 1)
                dve.wait_ge(onehot_used, N + 2)
                nc.vector.tensor_copy(count[:, :], countp[:, 0:NB]).then_inc(count_ready, 1)
                dve.wait_ge(sums_ready, 1)
                link(nc.vector.tensor_copy(sizes[:, :], totalp[:, 0:NB]))
                if padded:
                    link(nc.vector.tensor_scalar(sizes[:, :], sizes[:, :], float(P - 1), None, ALU.add))
                    link(nc.vector.tensor_copy(sizei[:, :], sizes[:, :]))
                    link(nc.vector.tensor_scalar(sizei[:, :], sizei[:, :], 7, None, ALU.arith_shift_right))
                    link(nc.vector.tensor_copy(sizes[:, :], sizei[:, :]))
                link(nc.vector.tensor_tensor_scan(ends[:, :], K["ones"][:, 0:NB], sizes[:, :], 0.0,
                                                  ALU.mult, ALU.add))
                link(nc.vector.memset(firsts[:, :], 0.0))
                link(nc.vector.tensor_tensor(firsts[:, 0:NB], ends[:, :], sizes[:, :], ALU.subtract))
                dve.sem_inc(firsts_ready, 1)
                link(nc.vector.scalar_tensor_tensor(out=start[:, :], in0=firsts[:, 0:NB],
                                                    scalar=float(P) if padded else 1.0, in1=withinp[:, 0:NB],
                                                    op0=ALU.mult, op1=ALU.add))
                if padded:
                    dve.wait_ge(numbered, 1)
                    link(nc.vector.tensor_copy(tilef[:, :], tilei[:, :]))
                    dve.wait_ge(turned, 1)
                    link(nc.vector.tensor_copy(tcol[:, :], tilep[:, 0:1]))
                    nc.vector.tensor_scalar(reach[:, :], tilef[:, :], tcol[:, 0:1], None, ALU.is_ge)\
                      .then_inc(reached, 1)
                    dve.wait_ge(summed, 1)
                    for j in range(4):
                        nc.vector.tensor_scalar(blk[0:1, j * W:(j + 1) * W], blkp[j][0:1, 0:W], -1.0, None, ALU.add)

            @block.gpsimd
            def _(pool):
                if padded:
                    nc.gpsimd.iota(tilei[:, :], [[1, cols]], base=0, channel_multiplier=0).then_inc(numbered, 1)

            @block.tensor
            def _(pe):
                pe.wait_ge(onehot_used, 2)
                nc.tensor.matmul(countp[:, 0:NB], K["ones"][:, :], zero[:, :], start=True, stop=True)
                with pe.Fori(0, N // 2) as i:
                    for h in range(2):
                        pe.wait_ge(onehot_ready, i * 2 + h + 1)
                        for u in range(HALF):
                            mm = nc.tensor.matmul(countp[:, 0:NB], ohlo[:, h, u, :], ohhi[:, h, u, :],
                                                  start=False, stop=True, skip_group_check=True)
                        mm.then_inc(onehot_used, 1)
                pe.wait_ge(count_ready, 1)
                nc.tensor.matmul(totalp[:, 0:NB], K["ones"][:, :], count[:, :], start=True, stop=True)
                nc.tensor.matmul(withinp[:, 0:NB], K["upper"][:, :], count[:, :], start=True, stop=True)\
                  .then_inc(sums_ready, 1)
                if padded:
                    pe.wait_ge(firsts_ready, 1)
                    nc.tensor.transpose(tilep[:, 0:P], firsts[:, :], K["ident"][:, :]).then_inc(turned, 1)
                    pe.wait_ge(reached, 1)
                    for j in range(4):
                        mm = nc.tensor.matmul(blkp[j][:, 0:W], K["ones"][0:NB, :], reach[0:NB, j * W:(j + 1) * W],
                                              start=True, stop=True)
                    mm.then_inc(summed, 1)

        def placing(c2, block, addp, placep):
            turnp = c2.ps("turnp", [P, HALF, P], BF16)
            samep = [c2.ps(f"samep{g}", [P, 4, P]) for g in range(2)]
            run = [c2.sb(f"run{h}", [P, HALF, NB]) for h in range(2)]
            loT = c2.sb("loT", [P, 2, HALF, P])
            loTb = c2.sb("loTb", [P, 2, HALF, P], BF16)
            same = c2.sb("same", [P, 2, HALF, P], BF16)
            prod = c2.sb("prod", [P, 2, 4, NB])
            placef = c2.sb("placef", [P, HALF])
            if not beside:
                placei = c2.sb("placei", [P, 2, HALF], I32)
                pair = c2.sb("pair", [P, 2, HALF, 2], I32)
            s = {n: c2.sem(n) for n in ("onehot_ready", "turned", "copied", "copiedb", "same_ready", "masked", "add_ready",
                                        "run_ready", "place_ready", "place_used", "scatter_ready", "passed",
                                        "reduced", "cleared")}
            landed = [c2.sem(f"landed{h}") for h in range(2)]
            slot_free = [c2.sem(f"slot_free{h}") for h in range(2)]
            quad = lambda bank: bank[:, 0:4 * NB].rearrange("p (a b) -> p a b", a=4)

            @block.vector
            def _(dve):
                nc.vector.tensor_scalar(run[0][:, 0, :], start[:, :], 1.0, None, ALU.add)\
                  .then_inc(s["run_ready"], 1)
                dve.sem_inc(s["masked"], 1)
                dve.sem_inc(s["place_used"], 2)
                if beside:
                    nc.vector.memset(places[:, :], FAR).then_inc(s["cleared"], 1)
                    dve.wait_ge(s["cleared"], 1)
                else:
                    for h in range(2):
                        dve.sem_inc(slot_free[h], 1)
                onehots(0, 0).then_inc(s["onehot_ready"], 1)

                def tables(n, h):
                    dve.wait_ge(s["add_ready"], n + 1)
                    for u in range(HALF):
                        dve.wait_ge(s["run_ready"], n * HALF + u + 1)
                        o = run[h][:, u + 1, :] if u + 1 < HALF else run[1 - h][:, 0, :]
                        nc.vector.tensor_tensor(o, run[h][:, u, :], quad(addp[u // 4])[:, u % 4, :], ALU.add)\
                          .then_inc(s["run_ready"], 1)
                    dve.wait_ge(s["same_ready"], n + 1)
                    for g in range(2):
                        mk = nc.vector.tensor_tensor(same[:, h, 4 * g:4 * g + 4, :], samep[g][:, :, :],
                                                     K["upper"][:, :].unsqueeze(1).to_broadcast([P, 4, P]),
                                                     ALU.mult)
                    mk.then_inc(s["masked"], 1)

                def place(n, h, k, after):
                    for g in range(2):
                        dve.wait_ge(s["place_ready"], n * 2 + g + 1)
                        nc.vector.tensor_tensor(prod[:, g, :, :], quad(placep[g]),
                                                ohhi[:, h, 4 * g:4 * g + 4, :], ALU.mult)\
                          .then_inc(s["place_used"], 1)
                    dve.wait_ge(s["place_used"], n * 2 + 4)
                    if after is not None:
                        onehots(h, after).then_inc(s["onehot_ready"], 1)
                    nc.vector.tensor_reduce(placef[:, :], prod[:, :, :, :].rearrange("p g a b -> p (g a) b"),
                                            AX.X, ALU.add).then_inc(s["reduced"], 1)
                    if beside:
                        dve.wait_ge(s["reduced"], n + 1)
                        nc.vector.tensor_tensor(places[:, bass.ds(n * HALF, HALF)], placef[:, :],
                                                skip[:, bass.ds(n * HALF, HALF)], ALU.add)
                        return
                    dve.wait_ge(slot_free[h], k + 1)
                    dve.wait_ge(s["reduced"], n + 1)
                    nc.vector.tensor_tensor(placei[:, h, :], placef[:, :], skip[:, bass.ds(n * HALF, HALF)],
                                            ALU.add)
                    nc.vector.tensor_copy(pair[:, h, :, 0], srci[:, bass.ds(n * HALF, HALF)])
                    nc.vector.tensor_copy(pair[:, h, :, 1], dsti[:, bass.ds(n * HALF, HALF)])\
                      .then_inc(s["scatter_ready"], 1)

                tables(0, 0)
                onehots(1, HALF).then_inc(s["onehot_ready"], 1)
                with dve.Fori(0, N // 2 - 1) as i:
                    for j in range(2):
                        tables(i * 2 + j + 1, 1 - j)
                        place(i * 2 + j, j, i, i * BODY + (j + 2) * HALF)
                tables(N - 1, 1)
                place(N - 2, 0, N // 2 - 1, None)
                place(N - 1, 1, N // 2 - 1, None)

            @block.scalar
            def _(act):
                def copy_turned(slot, n):
                    act.wait_ge(s["turned"], n + 1)
                    nc.scalar.copy(loTb[:, slot, :, :], turnp[:, :, :]).then_inc(s["copiedb"], 1)
                    nc.scalar.copy(loT[:, slot, :, :], turnp[:, :, :]).then_inc(s["copied"], 1)

                if not beside:
                    copy_turned(0, 0)
                    copy_turned(1, 1)
                    with act.Fori(0, N // 2 - 1) as i:
                        for h in range(2):
                            copy_turned(h, i * 2 + h + 2)
                else:
                    turns, odd = (N // 2 - 1) // 2, (N // 2 - 1) % 2
                    lead_in = gather.pairs - 1 - 3 * turns
                    assert lead_in > 0
                    for h in range(2):
                        gather.stage(h, h)
                    with act.Fori(0, lead_in) as i:
                        gather.advance(act, i)
                    copy_turned(0, 0)
                    copy_turned(1, 1)
                    with act.Fori(0, turns) as i:
                        for r in range(3):
                            gather.advance(act, i * 3 + lead_in + r)
                            if r < 2:
                                for h in range(2):
                                    copy_turned(h, i * 4 + 2 * r + h + 2)
                    if odd:
                        for h in range(2):
                            copy_turned(h, N - 2 + h)
                    for h in range(2):
                        gather.take(act, h, gather.pairs - 1)

            @block.tensor
            def _(pe):
                def turn(slot, n):
                    pe.wait_ge(s["onehot_ready"], n + 1)
                    for u in range(HALF):
                        tr = nc.tensor.transpose(turnp[:, u, :], ohlo[:, slot, u, :], K["identb"][:, :])
                    tr.then_inc(s["turned"], 1)

                def add(n, h):
                    pe.wait_ge(s["run_ready"], n * HALF + 1)
                    for u in range(HALF):
                        mm = nc.tensor.matmul(quad(addp[u // 4])[:, u % 4, :], ohlo[:, h, u, :],
                                              ohhi[:, h, u, :], start=True, stop=True)
                    mm.then_inc(s["add_ready"], 1)

                def half(n, h, last):
                    pe.wait_ge(s["copiedb"], n + 1)
                    pe.wait_ge(s["masked"], n + 1)
                    for u in range(HALF):
                        mm = nc.tensor.matmul(samep[u // 4][:, u % 4, :], loTb[:, h, u, :], loTb[:, h, u, :],
                                              start=True, stop=True)
                    mm.then_inc(s["same_ready"], 1)
                    pe.wait_ge(s["copied"], n + 1)
                    pe.wait_ge(s["masked"], n + 2)
                    for u in range(HALF):
                        g = u // 4
                        if u % 4 == 0:
                            pe.wait_ge(s["place_used"], n * 2 + g + 1)
                        nc.tensor.matmul(quad(placep[g])[:, u % 4, :], loT[:, h, u, :], run[h][:, u, :],
                                         start=True, stop=False)
                        mm = nc.tensor.matmul(quad(placep[g])[:, u % 4, :], same[:, h, u, :],
                                              ohhi[:, h, u, :], start=False, stop=True)
                        if u % 4 == 3:
                            mm.then_inc(s["place_ready"], 1)
                        if u == 3 and not last:
                            turn(1 - h, n + 1)
                            add(n + 1, 1 - h)

                turn(0, 0)
                add(0, 0)
                with pe.Fori(0, N // 2 - 1) as i:
                    for h in range(2):
                        half(i * 2 + h, h, False)
                half(N - 2, 0, False)
                half(N - 1, 1, True)

            @block.gpsimd
            def _(pool):
                if beside:
                    gather.issue(pool)
                    return
                with pool.Fori(0, N // 2) as i:
                    for h in range(2):
                        pool.wait_ge(s["scatter_ready"], i * 2 + h + 1)
                        pool.sem_inc(s["passed"], 1)
                        for u in range(HALF):
                            nc.gpsimd.indirect_dma_start(
                                pairs, bass.IndirectOffsetOnAxis(ap=placei[:, h, u:u + 1], axis=0),
                                pair[:, h, u, :], None, bounds_check=NPOS, oob_is_err=False)\
                              .then_inc(landed[h], 16)

            @block.sync
            def _(sp):
                if beside:
                    return
                with sp.Fori(0, N // 2) as i:
                    for h in range(2):
                        sp.wait_ge(landed[h], i * (16 * HALF) + 16 * HALF)
                        sp.sem_inc(slot_free[h], 1)

        banks = lambda c2, n: [c2.ps(f"{n}{g}", [P, 512]) for g in range(2)]
        if beside:
            with Ctx(nc, name + "s") as c2:
                addp, placep = banks(c2, "addp"), banks(c2, "placep")
                with nc.Block() as block:
                    histogram(c2, block, addp[0], placep[0], placep[1])
                    placing(c2, block, addp, placep)
        else:
            with Ctx(nc, name + "h") as c2:
                with nc.Block() as block:
                    histogram(c2, block, *(c2.ps(n, [P, 512]) for n in ("countp", "totalp", "withinp")))
            with Ctx(nc, name + "s") as c2:
                addp, placep = banks(c2, "addp"), banks(c2, "placep")
                with nc.Block() as block:
                    placing(c2, block, addp, placep)


class Gather:

    def __init__(self, nc, c, table, width, idx, out, cols, half):
        self.nc, self.table, self.idx, self.out, self.half = nc, table, idx, out, half
        self.pairs = cols // half // 2
        self.idxs = c.sb("idxs", [P, 2, half], I32)
        self.rows = c.sb("rows", [P, 2, half, width])
        self.idx_ready, self.issuing = c.sem("idx_ready"), c.sem("issuing")
        self.rows_landed = [c.sem(f"rows_landed{h}") for h in range(2)]

    def stage(self, h, n):
        self.nc.scalar.copy(self.idxs[:, h, :], self.idx[:, bass.ds(n * self.half, self.half)])\
            .then_inc(self.idx_ready, 1)

    def take(self, act, h, pair):
        act.wait_ge(self.rows_landed[h], pair * (16 * self.half) + 16 * self.half)
        self.nc.scalar.copy(self.out[:, bass.ds(pair * (2 * self.half) + h * self.half, self.half), :],
                            self.rows[:, h, :, :])

    def advance(self, act, pair):
        for h in range(2):
            self.take(act, h, pair)
            self.stage(h, pair * 2 + (h + 2))

    def issue(self, pool):
        with pool.Fori(0, self.pairs) as i:
            for h in range(2):
                pool.wait_ge(self.idx_ready, i * 2 + h + 1)
                pool.sem_inc(self.issuing, 1)
                for u in range(self.half):
                    self.nc.gpsimd.indirect_dma_start(
                        self.rows[:, h, u, :], None, self.table,
                        bass.IndirectOffsetOnAxis(ap=self.idxs[:, h, u:u + 1], axis=0))\
                        .then_inc(self.rows_landed[h], 16)


def gather_columns(nc, name, table, width, idx, out, cols, half):
    with Ctx(nc, name) as c:
        gather = Gather(nc, c, table, width, idx, out, cols, half)
        with nc.Block() as block:

            @block.scalar
            def _(act):
                for h in range(2):
                    gather.stage(h, h)
                with act.Fori(0, gather.pairs - 1) as i:
                    gather.advance(act, i)
                for h in range(2):
                    gather.take(act, h, gather.pairs - 1)

            @block.gpsimd
            def _(pool):
                gather.issue(pool)


def scatter_columns(nc, name, table, width, idx, vals, cols, half, last):
    N = cols // half
    with Ctx(nc, name) as c:
        idxs = c.sb("idxs", [P, 2, half], I32)
        rows = c.sb("rows", [P, 2, half, width])
        staged, passed = c.sem("staged"), c.sem("passed")
        landed = [c.sem(f"landed{h}") for h in range(2)]
        with nc.Block() as block:

            @block.scalar
            def _(act):
                def stage(h, col):
                    nc.scalar.copy(idxs[:, h, :], idx[:, bass.ds(col, half)])
                    nc.scalar.copy(rows[:, h, :, :], vals[:, bass.ds(col, half), :]).then_inc(staged, 1)

                stage(0, 0)
                stage(1, half)
                with act.Fori(0, N // 2 - 1) as i:
                    for h in range(2):
                        act.wait_ge(landed[h], i * (16 * half) + 16 * half)
                        act.sem_inc(passed, 1)
                        stage(h, i * (2 * half) + (h + 2) * half)
                for h in range(2):
                    act.wait_ge(landed[h], N // 2 * 16 * half)

            @block.gpsimd
            def _(pool):
                with pool.Fori(0, N // 2) as i:
                    for h in range(2):
                        pool.wait_ge(staged, i * 2 + h + 1)
                        pool.sem_inc(passed, 1)
                        for u in range(half):
                            nc.gpsimd.indirect_dma_start(
                                table, bass.IndirectOffsetOnAxis(ap=idxs[:, h, u:u + 1], axis=0),
                                rows[:, h, u, :], None, bounds_check=last, oob_is_err=False).then_inc(landed[h], 16)


def carry_over(nc, K, name, last, anyfirst, op0, op1, initial, out, width):
    with Ctx(nc, name) as c:
        lp, rp, op = (c.ps(n, [P, 512]) for n in ("lp", "rp", "op"))
        both = c.sb("both", [P, P])
        rows = c.sb("rows", [P, 2, P])
        state = c.sb("state", [P, P])
        spread, turned, scanned, back, ch = (c.sem(n) for n in ("spread", "turned", "scanned", "back", "ch"))
        with nc.Block() as block:

            @block.vector
            def _(dve):
                link = Link(dve, ch)
                nc.vector.tensor_copy(both[:, 0:width], anyfirst[:, 0:1].to_broadcast([P, width])).then_inc(spread, 1)
                dve.wait_ge(turned, 1)
                link(nc.vector.tensor_copy(rows[0:width, 0, :], lp[0:width, 0:P]))
                link(nc.vector.tensor_copy(rows[0:width, 1, :], rp[0:width, 0:P]))
                link(nc.vector.memset(state[0:width, 0:1], initial))
                nc.vector.tensor_tensor_scan(state[0:width, 1:P], rows[0:width, 1, 0:P - 1], rows[0:width, 0, 0:P - 1],
                                             initial, op0, op1).then_inc(scanned, 1)
                dve.wait_ge(back, 1)
                nc.vector.tensor_copy(out[:, 0:width], op[:, 0:width])

            @block.tensor
            def _(pe):
                nc.tensor.transpose(lp[0:width, 0:P], last[:, 0:width], K["ident"][:, :])
                pe.wait_ge(spread, 1)
                nc.tensor.transpose(rp[0:width, 0:P], both[:, 0:width], K["ident"][:, :]).then_inc(turned, 1)
                pe.wait_ge(scanned, 1)
                nc.tensor.transpose(op[:, 0:width], state[0:width, :], K["ident"][0:width, 0:width]).then_inc(back, 1)


def edge_tables(nc, name, places, H):
    dram = lambda n, w: nc.dram_tensor(f"{name}_{n}", (places, w), F32).ap()
    words = 15000
    if places // P * 2 * H <= words:
        return dram("maxd", H), [dram("fill", 2 * H)]
    return dram("maxd", H), [dram("filld", H), dram("fillm", H)]


def edge_weights(nc, K, c, name, cols, H, table, width, pairs, start, count, asn, adn, mn, scratch,
                 beside=None):
    maxd, fills = scratch
    FW = fills[0].shape[1]
    together = len(fills) == 1
    NPOS = P * cols
    prs = c.sb("prs", [P, cols, 2], I32)
    prev = c.sb("prev", [P, 1], I32)
    rows = c.sb("rows", [P, cols, width])
    prevf = c.sb("prevf", [P, 1])
    first = c.sb("first", [P, cols])
    inner = c.sb("inner", [P, cols])
    before = c.sb("before", [P, cols]) if width > H else None
    inall = c.sb("inall", [P, 1])
    lown = c.sb("lown", [P, 1])
    starti = c.sb("starti", [P, NB], I32)
    endi = c.sb("endi", [P, NB], I32)
    tmpn = c.sb("tmpn", [P, NB])
    has = c.sb("has", [P, NB])
    last = c.sb("last", [P, 32])
    carry = c.sb("carry", [P, 32])
    with Ctx(nc, name + "e") as e:
        seen = e.sb("seen", [P, cols])
        dstf = e.sb("dstf", [P, cols])
        if before is None:
            before = e.sb("before", [P, cols])
        steps = Link(None, e.sem("steps"))
        loaded, zeroed, stored = e.sem("loaded"), e.sem("zeroed"), e.sem("stored")
        zeros = rows[:, :, :].rearrange("p c w -> p (c w)")[:, 0:cols * H]
        flat = lambda d: d.rearrange("(p c) w -> p (c w)", p=P)
        places = pairs[1:1 + NPOS, :].rearrange("(p c) w -> p c w", p=P)
        onp = lambda d: d.rearrange("(p c) w -> p c w", p=P)
        with nc.Block() as block:

            @block.sync
            def _(sp):
                sp.dma_start(prs[:, :, :], places).then_inc(loaded, 16)
                with nc.allow_non_contiguous_dma("one word of each partition"):
                    sp.dma_start(prev[:, :], pairs[0:NPOS, :].rearrange("(p c) w -> p c w", p=P)[:, 0, 1:2])\
                      .then_inc(loaded, 16)
                sp.wait_ge(zeroed, 1)
                for f in fills:
                    for a in range(0, FW, H):
                        sp.dma_start(flat(f)[:, a * cols:(a + H) * cols], zeros).then_inc(stored, 16)
                sp.wait_ge(stored, 32)

            @block.vector
            def _(dve):
                link = steps.on(dve)
                nc.vector.memset(zeros, 0.0).then_inc(zeroed, 1)
                dve.wait_ge(loaded, 32)
                link(nc.vector.tensor_copy(dstf[:, :], prs[:, :, 1]))
                link(nc.vector.tensor_copy(prevf[:, :], prev[:, :]))
                link(nc.vector.tensor_tensor(first[:, 1:cols], dstf[:, 1:cols], dstf[:, 0:cols - 1], ALU.not_equal))
                link(nc.vector.tensor_tensor(first[:, 0:1], dstf[:, 0:1], prevf[:, :], ALU.not_equal))
                link(nc.vector.tensor_scalar(inner[:, :], first[:, :], -1.0, 1.0, ALU.mult, ALU.add))
                link(nc.vector.tensor_tensor_scan(before[:, :], inner[:, :], inner[:, :], 1.0, ALU.mult, ALU.min))
                link(nc.vector.tensor_scalar(seen[:, :], before[:, :], -LOW, LOW, ALU.mult, ALU.add))
                link(nc.vector.tensor_copy(inall[:, :], before[:, cols - 1:cols]))
                link(nc.vector.tensor_copy(lown[:, :], seen[:, cols - 1:cols]))
                link(nc.vector.tensor_scalar(has[:, :], count[:, :], 0.0, None, ALU.is_gt))
                link(nc.vector.tensor_scalar(tmpn[:, :], has[:, :], -float(FAR), float(FAR), ALU.mult, ALU.add))
                link(nc.vector.tensor_tensor(tmpn[:, :], tmpn[:, :], start[:, :], ALU.add))
                link(nc.vector.tensor_copy(starti[:, :], tmpn[:, :]))
                link(nc.vector.scalar_tensor_tensor(out=tmpn[:, :], in0=start[:, :], scalar=-1.0, in1=count[:, :],
                                                    op0=ALU.add, op1=ALU.add))
                link(nc.vector.tensor_scalar(tmpn[:, :], tmpn[:, :], 0.0, None, ALU.max))
                link(nc.vector.tensor_copy(endi[:, :], tmpn[:, :]))

        of_sources = (table, width, prs[:, :, 0], rows[:, :, :], cols, HALF)
        if beside:
            beside(of_sources)
        else:
            gather_columns(nc, name + "g", *of_sources)

        words = e.sb("words", [P, cols * FW])
        both = e.sb("both", [P, NB, 2 * H]) if together else None
        val = words[:, 0:cols * H].rearrange("p (c h) -> p c h", h=H)
        spread = words[:, :].rearrange("p (c w) -> p c w", w=FW)

        with nc.Block() as block:

            @block.vector
            def _(dve):
                link = steps.on(dve)
                link(nc.vector.tensor_scalar(first[:, :], first[:, :], LOW, None, ALU.mult))
                for h in range(H):
                    m = nc.vector.tensor_tensor_scan(val[:, :, h], first[:, :], rows[:, :, h], LOW, ALU.add, ALU.max)
                link(m)
                link(nc.vector.tensor_copy(last[:, 0:H], val[:, cols - 1, :]))
        carry_over(nc, K, name + "cm", last, lown, ALU.add, ALU.max, LOW, carry, H)
        with nc.Block() as block:

            @block.vector
            def _(dve):
                for h in range(H):
                    m = nc.vector.scalar_tensor_tensor(out=val[:, :, h], in0=seen[:, :], scalar=carry[:, h:h + 1],
                                                       in1=val[:, :, h], op0=ALU.add, op1=ALU.max)
                m.then_inc(zeroed, 1)

            @block.sync
            def _(sp):
                sp.wait_ge(zeroed, 2)
                sp.dma_start(onp(maxd), val).then_inc(stored, 16)
                sp.wait_ge(stored, 48)
        gather_columns(nc, name + "n", maxd, H, endi[:, :], mn[:, :, :], NB, 7)
        with nc.Block() as block:

            @block.vector
            def _(dve):
                link = steps.on(dve)
                hb = has[:, :].unsqueeze(2).to_broadcast([P, NB, H])
                link(nc.vector.tensor_scalar(tmpn[:, :], has[:, :], -LOW, LOW, ALU.mult, ALU.add))
                link(nc.vector.tensor_tensor(mn[:, :, :], mn[:, :, :], hb, ALU.mult))
                link(nc.vector.tensor_tensor(mn[:, :, :], mn[:, :, :],
                                             tmpn[:, :].unsqueeze(2).to_broadcast([P, NB, H]), ALU.add))
                link(nc.vector.tensor_tensor(mn[:, :, :], mn[:, :, :], asn[:, 0:NB, :], ALU.max))
                link(nc.vector.tensor_tensor(mn[:, :, :], mn[:, :, :], adn[:, 0:NB, :], ALU.add))
                link(nc.vector.scalar_tensor_tensor(out=mn[:, :, :], in0=mn[:, :, :], scalar=SLOPE, in1=mn[:, :, :],
                                                    op0=ALU.mult, op1=ALU.max))
                if together:
                    link(nc.vector.tensor_copy(both[:, :, 0:H], adn[:, 0:NB, :]))
                    link(nc.vector.tensor_copy(both[:, :, H:2 * H], mn[:, :, :]))
        sources = [both[:, :, :]] if together else [adn[:, 0:NB, :], mn[:, :, :]]
        for q, (d, v) in enumerate(zip(fills, sources)):
            scatter_columns(nc, f"{name}s{q}", d, FW, starti[:, :], v, NB, 7, NPOS - 1)
        for q, d in enumerate(fills):
            with nc.Block() as block:

                @block.sync
                def _(sp):
                    sp.dma_start(spread, onp(d)).then_inc(loaded, 16)

                @block.vector
                def _(dve):
                    link = steps.on(dve)
                    dve.wait_ge(loaded, 48 + 16 * q)
                    for f in range(FW):
                        m = nc.vector.tensor_tensor_scan(spread[:, :, f], inner[:, :], spread[:, :, f], 0.0,
                                                         ALU.mult, ALU.add)
                    link(m)
                    link(nc.vector.tensor_copy(last[:, 0:FW], spread[:, cols - 1, :]))
            carry_over(nc, K, f"{name}f{q}", last, inall, ALU.mult, ALU.add, 0.0, carry, FW)
            with nc.Block() as block:

                @block.vector
                def _(dve):
                    link = steps.on(dve)
                    for f in range(FW):
                        m = nc.vector.scalar_tensor_tensor(out=spread[:, :, f], in0=before[:, :],
                                                           scalar=carry[:, f:f + 1], in1=spread[:, :, f],
                                                           op0=ALU.mult, op1=ALU.add)
                    link(m)
                    if q == 0:
                        link(nc.vector.tensor_tensor(rows[:, :, 0:H], rows[:, :, 0:H], spread[:, :, 0:H], ALU.add))
                        link(nc.vector.scalar_tensor_tensor(out=rows[:, :, 0:H], in0=rows[:, :, 0:H], scalar=SLOPE,
                                                            in1=rows[:, :, 0:H], op0=ALU.mult, op1=ALU.max))
                    if q == len(fills) - 1:
                        link(nc.vector.tensor_tensor(rows[:, :, 0:H], rows[:, :, 0:H], spread[:, :, FW - H:FW],
                                                     ALU.subtract))
                        link(nc.vector.tensor_scalar(first[:, :], dstf[:, :], 0.0, None, ALU.is_ge))
                        nc.vector.tensor_tensor(rows[:, :, 0:H], rows[:, :, 0:H],
                                                first[:, :].unsqueeze(2).to_broadcast([P, cols, H]), ALU.mult)\
                          .then_inc(zeroed, 1)

                @block.scalar
                def _(act):
                    if q == len(fills) - 1:
                        act.wait_ge(zeroed, 3)
                        nc.scalar.activation(rows[:, :, 0:H], rows[:, :, 0:H], ACT.Exp)
    return {"prs": prs, "rows": rows, "first": first, "inner": inner, "before": before, "inall": inall,
            "last": last, "carry": carry, "endi": endi, "has": has}


def edge_records(nc, K, name, cols, H, ed, records):
    R = H + 2
    KB = cols // P
    rows, prs, low, srcf = ed["rows"], ed["prs"], ed["inner"], ed["first"]
    with Ctx(nc, name) as c:
        rec = c.sb("rec", [P, cols, R])
        turnp = [c.ps(f"turnp{j}", [P, 4, P]) for j in range(4)]
        ready, turned, taken, stored, ch = (c.sem(n) for n in ("ready", "turned", "taken", "stored", "ch"))
        fields = [rows[:, :, h] for h in range(H)] + [low[:, :], srcf[:, :]]
        groups = [(f, k) for f in range(R) for k in range(0, KB, 4)]
        out = rec[:, :, :].rearrange("e (p k) r -> e r k p", k=KB)
        with nc.Block() as block:

            @block.vector
            def _(dve):
                link = Link(dve, ch)
                link(nc.vector.tensor_scalar(srcf[:, :], prs[:, :, 1], 0.0, 1000.0, ALU.is_lt, ALU.mult))
                link(nc.vector.tensor_scalar(prs[:, :, 1], prs[:, :, 1], 127, None, ALU.bitwise_and))
                link(nc.vector.tensor_copy(low[:, :], prs[:, :, 1]))
                link(nc.vector.tensor_tensor(low[:, :], low[:, :], srcf[:, :], ALU.add))
                nc.vector.tensor_copy(srcf[:, :], prs[:, :, 0]).then_inc(ready, 1)
                for g, (f, k) in enumerate(groups):
                    n = min(4, KB - k)
                    dve.wait_ge(turned, g + 1)
                    o = out[:, f, k:k + n, :]
                    if f == H + 1:
                        o = rec[:, :, :].bitcast(I32).rearrange("e (p k) r -> e r k p", k=KB)[:, f, k:k + n, :]
                    nc.vector.tensor_copy(o, turnp[g % 4][:, 0:n, :]).then_inc(taken, 1)

            @block.tensor
            def _(pe):
                pe.wait_ge(ready, 1)
                for g, (f, k) in enumerate(groups):
                    if g >= 4:
                        pe.wait_ge(taken, g - 3)
                    for j in range(min(4, KB - k)):
                        mm = nc.tensor.transpose(turnp[g % 4][:, j, :], fields[f][:, (k + j) * P:(k + j + 1) * P],
                                                 K["ident"][:, :])
                    mm.then_inc(turned, 1)

            @block.sync
            def _(sp):
                sp.wait_ge(taken, len(groups))
                sp.dma_start(records, rec[:, :, :].rearrange("p t r -> p (t r)")).then_inc(stored, 16)
                sp.wait_ge(stored, 16)


def sum_messages(nc, K, name, tiles, H, htab, records, blk, acc):
    SLOTS, PAGES, BANKS = 4, TURN // LOT, 8
    R, D, W = H + 2, DIM // H, DIM + H
    L = tiles // LOT
    assert L % PAGES == 0
    with Ctx(nc, name) as c:
        rec = [c.sb(f"rec{q}", [P, LOT, R]) for q in range(PAGES)]
        hrow = [c.sb(f"hrow{q}", [P, LOT, DIM]) for q in range(SLOTS)]
        msg = [c.sb(f"msg{q}", [P, LOT, W]) for q in range(SLOTS)]
        to = [c.sb(f"to{q}", [P, LOT, P]) for q in range(SLOTS)]
        sump = [c.ps(f"sump{j}", [P, 512]) for j in range(BANKS)]
        msg_ready, summed, added, passed = (c.sem(n) for n in ("msg_ready", "summed", "added", "passed"))
        rec_in = [c.sem(f"rec_in{q}") for q in range(PAGES)]
        landed = [c.sem(f"landed{q}") for q in range(SLOTS)]
        with nc.Block() as block:

            @block.sync
            def _(sp):
                def load(q, col):
                    sp.dma_start(rec[q][:, :, :].rearrange("p t r -> p (t r)"),
                                 records[:, bass.ds(col, LOT * R)]).then_inc(rec_in[q], 16)

                for q in range(PAGES):
                    load(q, q * LOT * R)
                with sp.Fori(0, L // PAGES) as i:
                    for q in range(PAGES):
                        sp.wait_ge(msg_ready, i * TURN + q * LOT + LOT)
                        load(q, i * (TURN * R) + (q + PAGES) * LOT * R)
                for q in range(PAGES):
                    sp.wait_ge(rec_in[q], (L // PAGES + 1) * 16)

            @block.gpsimd
            def _(pool):
                def gather(q):
                    for u in range(LOT):
                        nc.gpsimd.indirect_dma_start(
                            hrow[q % SLOTS][:, u, :], None, htab,
                            bass.IndirectOffsetOnAxis(ap=rec[q][:, u, R - 1:R].bitcast(I32), axis=0))\
                          .then_inc(landed[q % SLOTS], 16)

                for q in range(SLOTS):
                    pool.wait_ge(rec_in[q], 16)
                    gather(q)
                with pool.Fori(0, L // PAGES) as i:
                    for q in range(PAGES):
                        nq = (q + SLOTS) % PAGES
                        pool.wait_ge(msg_ready, i * TURN + q * LOT + LOT)
                        pool.wait_ge(rec_in[nq], i * 16 + 16 * (1 + (q + SLOTS) // PAGES))
                        pool.sem_inc(passed, 1)
                        gather(nq)

            @block.vector
            def _(dve):
                def rows_to(q, turn, wrap):
                    s = q % SLOTS
                    per = PAGES // SLOTS
                    dve.wait_ge(rec_in[q], turn * 16 + 16 * (1 + wrap))
                    dve.wait_ge(landed[s], turn * (16 * LOT * per) + 16 * LOT * (q // SLOTS + 1 + per * wrap))
                    nc.vector.tensor_tensor(to[s][:, :, :], K["iota"][:, :].unsqueeze(1).to_broadcast([P, LOT, P]),
                                            rec[q][:, :, H:H + 1].to_broadcast([P, LOT, P]), ALU.is_equal)
                    nc.vector.tensor_copy(msg[s][:, :, DIM:W], rec[q][:, :, 0:H])

                def message(q, u):
                    s = q % SLOTS
                    nc.vector.tensor_tensor(
                        msg[s][:, u, 0:DIM].rearrange("p (a d) -> p a d", a=H),
                        hrow[s][:, u, :].rearrange("p (a d) -> p a d", a=H),
                        rec[q][:, u, 0:H].unsqueeze(2).to_broadcast([P, H, D]), ALU.mult).then_inc(msg_ready, 1)

                nc.vector.memset(acc[:, :, :], 0.0).then_inc(added, BANKS)
                rows_to(0, 0, 0)
                for u in range(LOT):
                    message(0, u)
                with dve.Fori(0, L // PAGES) as i:
                    for q in range(PAGES):
                        if q % 2 == 0:
                            _, blocks = nc.values_load_multi_w_load_instructions(
                                blk[0:1, bass.ds(i * TURN + q * LOT, 2 * LOT)], engines=[mybir.EngineType.DVE],
                                min_val=0, max_val=NB - 1)
                        b = blocks[q % 2 * LOT:]
                        nq = (q + 1) % PAGES
                        rows_to(nq, i, (q + 1) // PAGES)
                        for u in range(LOT):
                            t = i * TURN + q * LOT + u
                            message(nq, u)
                            dve.wait_ge(summed, t + 1)
                            dve.wait_ge(added, t + BANKS)
                            a = acc[:, bass.ds(b[u], 1), :].rearrange("p a c -> p (a c)")
                            nc.vector.tensor_tensor(a, a, sump[(q * LOT + u) % BANKS][:, 0:W], ALU.add)\
                              .then_inc(added, 1)
                for s in range(SLOTS):
                    dve.wait_ge(landed[s], (L // SLOTS + 1) * 16 * LOT)

            @block.tensor
            def _(pe):
                with pe.Fori(0, L // PAGES) as i:
                    for q in range(PAGES):
                        for u in range(LOT):
                            t = i * TURN + q * LOT + u
                            pe.wait_ge(msg_ready, t + 1)
                            pe.wait_ge(added, t + 1)
                            nc.tensor.matmul(sump[(q * LOT + u) % BANKS][:, 0:W], to[q % SLOTS][:, u, :],
                                             msg[q % SLOTS][:, u, :],
                                             start=True, stop=True).then_inc(summed, 1)


def pad_rows(nc, name, x, xp, tails):
    extra = ROWS - NODES
    with Ctx(nc, name) as c:
        zero = c.sb("zero", [P, extra * DIM // 100])
        copied, cleared = c.sem("copied"), c.sem("cleared")
        with nc.Block() as block:

            @block.vector
            def _(dve):
                nc.vector.memset(zero[:, :], 0.0).then_inc(cleared, 1)

            @block.sync
            def _(sp):
                sp.dma_start(xp[0:NODES, :].rearrange("(a b) d -> a (b d)", a=100),
                             x.rearrange("(a b) d -> a (b d)", a=100)).then_inc(copied, 16)
                sp.wait_ge(cleared, 1)
                sp.dma_start(xp[NODES:ROWS, :].rearrange("(a b) d -> a (b d)", a=100), zero[0:100, :])\
                  .then_inc(copied, 16)
                for d in tails:
                    sp.dma_start(d[NB * P:ROWS, :].rearrange("(a b) d -> a (b d)", a=P),
                                 zero[:, 0:(ROWS - NB * P) * DIM // P]).then_inc(copied, 16)
                sp.wait_ge(copied, 32 + 16 * len(tails))


def node_tables(nc, K, name, xin, w, F, H, att_src, att_dst, htab, atab, asn, adn, hn):
    N = ROWS // P // 2
    D = F // H
    with Ctx(nc, name) as c:
        ws = c.sb("ws", [P, KC, F])
        att = c.sb("att", [P, 2, F])
        x = [c.sb(f"x{h}", [P, 2, DIM]) for h in range(2)]
        xn = [c.sb(f"xn{h}", [P, 2, DIM]) for h in range(2)]
        xT = [c.sb(f"xT{h}", [P, KC, 2, P]) for h in range(2)]
        hs = [c.sb(f"hs{h}", [P, 2, F]) for h in range(2)]
        red = [c.sb(f"red{h}", [P, 2, 2, H]) for h in range(2)]
        stats, mv, sd, rstd = c.sb("stats", [P, 2, 6]), c.sb("mv", [P, 2, 2]), c.sb("sd", [P, 2, 1]), c.sb("rstd", [P, 2, 1])
        prod = c.sb("prod", [P, 2, 2, F])
        xTp = [c.ps(f"xTp{h}", [P, KC, 2, P]) for h in range(2)]
        hp = [c.ps(f"hp{h}", [P, 512]) for h in range(2)]
        (w_in, var_ready, sd_ready, xn_ready, xT_ready, xT_copied, h_ready, h_copied, a_ready, made, multiplied) = (
            c.sem(n) for n in ("w_in", "var_ready", "sd_ready", "xn_ready", "xT_ready", "xT_copied", "h_ready",
                               "h_copied", "a_ready", "made", "multiplied"))
        x_in = [c.sem(f"x_in{h}") for h in range(2)]
        stored = c.sem("stored")
        slot_free, passed = c.sem("slot_free"), c.sem("passed")
        xv = xin.rearrange("(b p) d -> p b d", p=P)
        av = atab.rearrange("(b p) d -> p b d", p=P)
        hv = htab.rearrange("(b p) d -> p b d", p=P) if hn is None else None
        XLINKS, ALINKS = 2, 2
        with nc.Block() as block:

            @block.sync
            def _(sp):
                sp.dma_start(ws[:, :, :], w.rearrange("(k p) f -> p k f", p=P)).then_inc(w_in, 16)
                sp.dma_start(att[:, 0, :], att_src.rearrange("h d -> (h d)").partition_broadcast(P)).then_inc(w_in, 16)
                sp.dma_start(att[:, 1, :], att_dst.rearrange("h d -> (h d)").partition_broadcast(P)).then_inc(w_in, 16)
                for h in range(2):
                    sp.dma_start(x[h][:, :, :], xv[:, 2 * h:2 * h + 2, :]).then_inc(x_in[h], 16)
                with sp.Fori(0, N // 2 - 1) as i:
                    for h in range(2):
                        sp.wait_ge(xn_ready, i * 2 + h + 1)
                        sp.dma_start(x[h][:, :, :], xv[:, bass.ds(i * 4 + 2 * h + 4, 2), :]).then_inc(x_in[h], 16)

            @block.scalar
            def _(act):
                def root(n):
                    act.wait_ge(var_ready, n + 1)
                    nc.scalar.activation(sd[:, :, :], mv[:, :, 1:2], ACT.Sqrt, bias=K["eps"][:, 0:1])\
                      .then_inc(sd_ready, 1)

                def copy_xT(n, h):
                    act.wait_ge(xT_ready, n + 1)
                    nc.scalar.copy(xT[h][:, :, :, :], xTp[h][:, :, :, :]).then_inc(xT_copied, 1)

                def copy_h(n, h):
                    act.wait_ge(slot_free, n + 1)
                    act.wait_ge(h_ready, n + 1)
                    act.sem_inc(passed, 1)
                    nc.scalar.copy(hs[h][:, :, :], hp[h][:, 0:2 * F].rearrange("p (a f) -> p a f", a=2))\
                      .then_inc(h_copied, 1)

                root(0)
                copy_xT(0, 0)
                with act.Fori(0, N // 2 - 1) as i:
                    for h in range(2):
                        n = i * 2 + h
                        root(n + 1)
                        copy_h(n, h)
                        copy_xT(n + 1, 1 - h)
                root(N - 1)
                copy_h(N - 2, 0)
                copy_xT(N - 1, 1)
                copy_h(N - 1, 1)

            @block.tensor
            def _(pe):
                def turn(n, h):
                    pe.wait_ge(xn_ready, n + 1)
                    for k in range(KC):
                        for j in range(2):
                            mm = nc.tensor.transpose(xTp[h][:, k, j, :], xn[h][:, j, k * P:(k + 1) * P],
                                                     K["ident"][:, :])
                    mm.then_inc(xT_ready, 1)

                def multiply(n, h):
                    pe.wait_ge(xT_copied, n + 1)
                    for j in range(2):
                        for k in range(KC):
                            mm = nc.tensor.matmul(hp[h][:, j * F:(j + 1) * F], xT[h][:, k, j, :], ws[:, k, :],
                                                  start=(k == 0), stop=(k == KC - 1))
                    mm.then_inc(h_ready, 1)

                pe.wait_ge(w_in, 48)
                turn(0, 0)
                with pe.Fori(0, N // 2 - 1) as i:
                    for h in range(2):
                        multiply(i * 2 + h, h)
                        turn(i * 2 + h + 1, 1 - h)
                multiply(N - 2, 0)
                turn(N - 1, 1)
                multiply(N - 1, 1)

            @block.vector
            def _(dve):
                def normal(n, h, turn):
                    link = Link(dve, made, n * XLINKS)
                    dve.wait_ge(x_in[h], turn * 16 + 16)
                    for j in range(2):
                        m = nc.vector.bn_stats(stats[:, j, :], x[h][:, j, :])
                    link(m)
                    dve.sem_inc(passed, 1)
                    for j in range(2):
                        m = nc.vector.bn_aggr(mv[:, j, :], stats[:, j, :])
                    m.then_inc(var_ready, 1)
                    dve.wait_ge(sd_ready, n + 1)
                    link(nc.vector.reciprocal(rstd[:, :, :], sd[:, :, :]))
                    for j in range(2):
                        m = nc.vector.tensor_scalar(xn[h][:, j, :], x[h][:, j, :], mv[:, j, 0:1], rstd[:, j, :],
                                                    ALU.subtract, ALU.mult)
                    m.then_inc(xn_ready, 1)
                    assert link.n == XLINKS

                def attend(n, h, col):
                    link = Link(dve, multiplied, n * ALINKS)
                    dve.wait_ge(h_copied, n + 1)
                    for q in range(2):
                        m = nc.vector.tensor_tensor(prod[:, q, :, :], hs[h][:, :, :],
                                                    att[:, q, :].unsqueeze(1).to_broadcast([P, 2, F]), ALU.mult)
                    link(m)
                    link(nc.vector.tensor_reduce(red[h][:, :, :, :].rearrange("p q a h -> p (q a h)"),
                                                 prod[:, :, :, :].rearrange("p q a (h d) -> p (q a h) d", h=H),
                                                 AX.X, ALU.add))
                    dve.sem_inc(a_ready, 1)
                    same = lambda o, v: nc.vector.tensor_tensor(o[:, bass.ds(col, 2), :], v, v, ALU.max)
                    same(asn, red[h][:, 0, :, :])
                    same(adn, red[h][:, 1, :, :])
                    if hn is not None:
                        same(hn, hs[h][:, :, :])
                    assert link.n == ALINKS

                dve.wait_ge(w_in, 48)
                dve.sem_inc(slot_free, 2)
                normal(0, 0, 0)
                with dve.Fori(0, N // 2 - 1) as i:
                    for h in range(2):
                        normal(i * 2 + h + 1, 1 - h, i + h)
                        attend(i * 2 + h, h, i * 4 + 2 * h)
                normal(N - 1, 1, N // 2 - 1)
                attend(N - 2, 0, 2 * N - 4)
                attend(N - 1, 1, 2 * N - 2)

            @block.gpsimd
            def _(pool):
                with pool.Fori(0, N // 2) as i:
                    for h in range(2):
                        n = i * 2 + h
                        b = bass.ds(n * 2, 2)
                        pool.wait_ge(a_ready, n + 1)
                        pool.dma_start(av[:, b, 0:H], red[h][:, 0, :, :]).then_inc(stored, 16)
                        pool.dma_start(hv[:, b, :] if hn is None else av[:, b, H:H + F], hs[h][:, :, :])\
                            .then_inc(stored, 16)
                        pool.wait_ge(stored, n * 32 + 32)
                        pool.sem_inc(slot_free, 1)


def finish_attention(nc, K, name, acc, H, htab, asn, adn, mn, xin, xout, bias, norm):
    D, W = DIM // H, DIM + H
    N, SLOTS = NB // 2, 4
    T = N // SLOTS
    assert NB % 2 == 0 and N % SLOTS == 1
    ALINKS, BLINKS = (4, 1) if norm is None else (5, 3)
    with Ctx(nc, name) as c:
        own = c.sb("own", [P, NB, H])
        rden = c.sb("rden", [P, NB, H])
        par = c.sb("par", [P, 3, DIM])
        hr = [c.sb(f"hr{s}", [P, 2, DIM]) for s in range(SLOTS)]
        x = [c.sb(f"x{s}", [P, 2, DIM]) for s in range(SLOTS)]
        t = [c.sb(f"t{h}", [P, 2, DIM]) for h in range(2)]
        y = [c.sb(f"y{h}", [P, 2, DIM]) for h in range(2)]
        stats = [c.sb(f"stats{h}", [P, 2, 6]) for h in range(2)]
        mv = [c.sb(f"mv{h}", [P, 2, 2]) for h in range(2)]
        sd = [c.sb(f"sd{h}", [P, 2, 1]) for h in range(2)]
        rstd = [c.sb(f"rstd{h}", [P, 2, 1]) for h in range(2)]
        (par_in, score_ready, own_ready, ch, combined, finished, done, var_ready, sd_ready, slot_free, stored,
         passed) = (c.sem(n) for n in ("par_in", "score_ready", "own_ready", "ch", "combined", "finished", "done",
                                       "var_ready", "sd_ready", "slot_free", "stored", "passed"))
        x_in = [c.sem(f"x_in{s}") for s in range(SLOTS)]
        blocks = lambda d: d.rearrange("(b p) d -> p b d", p=P)
        xv, hv, ov = blocks(xin), blocks(htab), blocks(xout)
        wide = lambda a, b: a[:, bass.ds(b, 2), :].unsqueeze(3).to_broadcast([P, 2, H, D])
        heads = lambda a: a.rearrange("p b (h d) -> p b h d", h=H)
        param = lambda q: par[:, q, :].unsqueeze(1).to_broadcast([P, 2, DIM])
        with nc.Block() as block:

            @block.sync
            def _(sp):
                for q, a in enumerate([bias] + list(norm or ())):
                    sp.dma_start(par[:, q, :], a.partition_broadcast(P)).then_inc(par_in, 16)

                def load(s, n):
                    b = bass.ds(n * 2, 2)
                    sp.dma_start(x[s][:, :, :], xv[:, b, :]).then_inc(x_in[s], 16)
                    sp.dma_start(hr[s][:, :, :], hv[:, b, :]).then_inc(x_in[s], 16)

                for s in range(SLOTS):
                    load(s, s)
                with sp.Fori(0, T - 1) as i:
                    for s in range(SLOTS):
                        sp.wait_ge(done, i * SLOTS + s + 1)
                        load(s, i * SLOTS + s + SLOTS)
                sp.wait_ge(done, N - SLOTS)
                load(0, N - 1)

            @block.gpsimd
            def _(pool):
                def store(n, h):
                    pool.wait_ge(done, n + 1)
                    pool.dma_start(ov[:, bass.ds(n * 2, 2), :], y[h][:, :, :]).then_inc(stored, 16)
                    pool.wait_ge(stored, n * 16 + 16)
                    pool.sem_inc(slot_free, 1)

                with pool.Fori(0, N // 2) as i:
                    for h in range(2):
                        store(i * 2 + h, h)
                store(N - 1, 0)

            @block.scalar
            def _(act):
                act.wait_ge(score_ready, 1)
                nc.scalar.activation(own[:, :, :], own[:, :, :], ACT.Exp).then_inc(own_ready, 1)
                if norm is not None:
                    def root(n, h):
                        act.wait_ge(var_ready, n + 1)
                        nc.scalar.activation(sd[h][:, :, :], mv[h][:, :, 1:2], ACT.Sqrt, bias=K["eps"][:, 0:1])\
                          .then_inc(sd_ready, 1)

                    with act.Fori(0, N // 2) as i:
                        for h in range(2):
                            root(i * 2 + h, h)
                    root(N - 1, 0)

            @block.vector
            def _(dve):
                link = Link(dve, ch)
                dve.sem_inc(slot_free, 2)
                link(nc.vector.tensor_tensor(own[:, :, :], asn[:, 0:NB, :], adn[:, 0:NB, :], ALU.add))
                link(nc.vector.scalar_tensor_tensor(out=own[:, :, :], in0=own[:, :, :], scalar=SLOPE,
                                                    in1=own[:, :, :], op0=ALU.mult, op1=ALU.max))
                link(nc.vector.tensor_tensor(own[:, :, :], own[:, :, :], mn[:, :, :], ALU.subtract))
                dve.sem_inc(score_ready, 1)
                dve.wait_ge(own_ready, 1)
                link(nc.vector.tensor_tensor(rden[:, :, :], own[:, :, :], acc[:, :, DIM:W], ALU.add))
                link(nc.vector.reciprocal(rden[:, :, :], rden[:, :, :]))
                dve.wait_ge(par_in, 16 * (1 + (2 if norm else 0)))

                def combine(n, s, turn):
                    h = s % 2
                    link = Link(dve, combined, n * ALINKS)
                    dve.wait_ge(x_in[s], turn * 32 + 32)
                    link(nc.vector.tensor_tensor(heads(t[h][:, :, :]), heads(hr[s][:, :, :]), wide(own, n * 2),
                                                 ALU.mult))
                    link(nc.vector.tensor_tensor(t[h][:, :, :], t[h][:, :, :], acc[:, bass.ds(n * 2, 2), 0:DIM],
                                                 ALU.add))
                    link(nc.vector.tensor_tensor(heads(t[h][:, :, :]), heads(t[h][:, :, :]), wide(rden, n * 2),
                                                 ALU.mult))
                    link(nc.vector.tensor_tensor(t[h][:, :, :], t[h][:, :, :], param(0), ALU.add))
                    if norm is not None:
                        for j in range(2):
                            m = nc.vector.bn_stats(stats[h][:, j, :], t[h][:, j, :])
                        link(m)
                        dve.sem_inc(passed, 1)
                        for j in range(2):
                            m = nc.vector.bn_aggr(mv[h][:, j, :], stats[h][:, j, :])
                        m.then_inc(var_ready, 1)
                    assert link.n == ALINKS

                def finish(n, s):
                    h = s % 2
                    link = Link(dve, finished, n * BLINKS)
                    if norm is not None:
                        nc.vector.tensor_tensor(x[s][:, :, :], x[s][:, :, :], param(2), ALU.add)
                        dve.wait_ge(sd_ready, n + 1)
                        link(nc.vector.reciprocal(rstd[h][:, :, :], sd[h][:, :, :]))
                        for j in range(2):
                            m = nc.vector.scalar_tensor_tensor(out=t[h][:, j, :], in0=t[h][:, j, :],
                                                               scalar=mv[h][:, j, 0:1], in1=par[:, 1, :],
                                                               op0=ALU.subtract, op1=ALU.mult)
                        link(m)
                    dve.wait_ge(slot_free, n + 1)
                    if norm is not None:
                        for j in range(2):
                            m = nc.vector.scalar_tensor_tensor(out=y[h][:, j, :], in0=t[h][:, j, :],
                                                               scalar=rstd[h][:, j, :], in1=x[s][:, j, :],
                                                               op0=ALU.mult, op1=ALU.add)
                        link(m)
                    else:
                        link(nc.vector.tensor_tensor(y[h][:, :, :], t[h][:, :, :], x[s][:, :, :], ALU.add))
                    dve.sem_inc(done, 1)
                    assert link.n == BLINKS

                combine(0, 0, 0)
                with dve.Fori(0, T) as i:
                    for s in range(SLOTS):
                        combine(i * SLOTS + s + 1, (s + 1) % SLOTS, i + (s + 1) // SLOTS)
                        finish(i * SLOTS + s, s)
                finish(N - 1, 0)


def normalise(nc, K, dve, link, x, stats, mv, sd, rstd, xn, var_ready, sd_ready, passed, count):
    for j in range(CHUNK):
        m = nc.vector.bn_stats(stats[:, j, :], x[:, j, :])
    link(m)
    dve.sem_inc(passed, 1)
    for j in range(CHUNK):
        m = nc.vector.bn_aggr(mv[:, j, :], stats[:, j, :])
    m.then_inc(var_ready, 1)
    dve.wait_ge(sd_ready, count)
    link(nc.vector.reciprocal(rstd[:, :, :], sd[:, :, :]))
    for j in range(CHUNK):
        m = nc.vector.tensor_scalar(xn[:, j, :], x[:, j, :], mv[:, j, 0:1], rstd[:, j, :], ALU.subtract, ALU.mult)
    return m


def places_per_step(tiles):
    return -(-tiles // NCH)


def mix_experts(nc, K, name, xin, xout, wr, br, w1, b1, bn1, w2, b2, bn2, wo, bo, scatter):
    srci, dsti, places, pairs, last = scatter
    PER = places_per_step(srci.shape[1])
    NE = w1.shape[0]
    NT = CHUNK * P
    YPC = 2 * NE + 2
    LINKS, XLINKS = 6, 2
    with Ctx(nc, name) as c:
        wrs, brs = c.sb("wrs", [P, KC, NE]), c.sb("brs", [P, NE])
        w1s, w2s, wos = (c.sb(n, [P, NE, KC, DIM]) for n in ("w1s", "w2s", "wos"))
        bos = c.sb("bos", [NE, DIM])
        par = c.sb("par", [P, 2, 5, NE, KC])
        scale, shift = c.sb("scale", [P, 2, NE, KC]), c.sb("shift", [P, 2, NE, KC])
        x, xn, y = (c.sb(n, [P, CHUNK, DIM]) for n in ("x", "xn", "y"))
        ysum = c.sb("ysum", [P, CHUNK, DIM])
        xT = c.sb("xT", [P, KC, NT])
        h1s = [c.sb(f"h1s{j}", [P, KC, NT]) for j in range(2)]
        h2s = [c.sb(f"h2s{j}", [P, KC, NT]) for j in range(2)]
        stats, mv = c.sb("stats", [P, CHUNK, 6]), c.sb("mv", [P, CHUNK, 2])
        sd, rstd = c.sb("sd", [P, CHUNK, 1]), c.sb("rstd", [P, CHUNK, 1])
        wgt, top, tot = c.sb("wgt", [P, CHUNK, NE]), c.sb("top", [P, CHUNK]), c.sb("tot", [P, CHUNK])
        wT = c.sb("wT", [NE, CHUNK, P])
        pair, place = c.sb("pair", [P, PER, 2], I32), c.sb("place", [P, PER], I32)
        pair_ready, scattered, pair_free, passed_pool = (
            c.sem(n) for n in ("pair_ready", "scattered", "pair_free", "passed_pool"))
        h1p = [c.ps(f"h1p{m}", [P, NT]) for m in range(KC)]
        h2p = [c.ps(f"h2p{m}", [P, NT]) for m in range(KC)]
        yp = [c.ps(f"yp{m}", [P, 2, DIM]) for m in range(2)]
        tp = [c.ps(f"tp{m}", [P, CHUNK, P]) for m in range(2)]
        (w_in, par_ready, root_ready, x_in, var_ready, sd_ready, xn_ready, xT_ready, xT_copied, logits_ready,
         scores_ready, exp_ready, wgt_ready, wT_ready, wT_copied, h1_ready, h1_done, h2_ready, h2_done, y_ready,
         y_used, x_used, ysum_ready, slot_free, stored, passed, ch, normalised) = (c.sem(n) for n in (
             "w_in", "par_ready", "root_ready", "x_in", "var_ready", "sd_ready", "xn_ready", "xT_ready", "xT_copied",
             "logits_ready", "scores_ready", "exp_ready", "wgt_ready", "wT_ready", "wT_copied", "h1_ready", "h1_done",
             "h2_ready", "h2_done", "y_ready", "y_used", "x_used", "ysum_ready", "slot_free", "stored", "passed",
             "ch", "normalised"))
        xv = xin.rearrange("(b p) d -> p b d", p=P)
        ov = xout.rearrange("(b p) d -> p b d", p=P)
        loads = [(wrs[:, :, :], wr.rearrange("(k p) e -> p k e", p=P)), (brs[:, :], br.partition_broadcast(P)),
                 (bos[:, :], bo)]
        for s_, d in ((w1s, w1), (w2s, w2), (wos, wo)):
            loads += [(s_[:, e, :, :], d[e].rearrange("(k p) h -> p k h", p=P)) for e in range(NE)]
        for l, ps_ in enumerate(((b1,) + bn1, (b2,) + bn2)):
            for q, a in enumerate(ps_):
                loads += [(par[:, l, q, e, :], a[e].rearrange("(k p) -> p k", p=P)) for e in range(NE)]
        with nc.Block() as block:

            @block.sync
            def _(sp):
                sp.dma_start(x[:, :, :], xv[:, 0:CHUNK, :]).then_inc(x_in, 16)
                with nc.allow_non_contiguous_dma("features of a bias go to the partitions"):
                    for o, a in loads:
                        sp.dma_start(o, a).then_inc(w_in, 16)
                with sp.Fori(0, NCH - 1) as i:
                    sp.wait_ge(x_used, i + 1)
                    sp.dma_start(x[:, :, :], xv[:, bass.ds(i * CHUNK + CHUNK, CHUNK), :]).then_inc(x_in, 16)

            @block.gpsimd
            def _(pool):
                with pool.Fori(0, NCH) as i:
                    pool.wait_ge(pair_ready, i + 1)
                    pool.sem_inc(passed_pool, 1)
                    for u in range(PER):
                        nc.gpsimd.indirect_dma_start(
                            pairs, bass.IndirectOffsetOnAxis(ap=place[:, u:u + 1], axis=0), pair[:, u, :], None,
                            bounds_check=last, oob_is_err=False).then_inc(scattered, 16)
                    pool.wait_ge(scattered, i * (16 * PER) + 16 * PER)
                    pool.sem_inc(pair_free, 1)
                    pool.wait_ge(ysum_ready, i + 1)
                    pool.dma_start(ov[:, bass.ds(i * CHUNK, CHUNK), :], y[:, :, :]).then_inc(stored, 16)
                    pool.wait_ge(stored, i * 16 + 16)
                    pool.sem_inc(slot_free, 1)

            @block.scalar
            def _(act):
                act.wait_ge(w_in, 16 * len(loads))
                nc.scalar.activation(scale[:, :, :, :], par[:, :, 4, :, :], ACT.Sqrt, bias=K["bneps"][:, 0:1])\
                  .then_inc(root_ready, 1)
                act.wait_ge(par_ready, 1)

                def root(i):
                    act.wait_ge(var_ready, i + 1)
                    nc.scalar.activation(sd[:, :, :], mv[:, :, 1:2], ACT.Sqrt, bias=K["eps"][:, 0:1])\
                      .then_inc(sd_ready, 1)

                def copy_xT(i):
                    for k in range(KC):
                        act.wait_ge(xT_ready, i * KC + k + 1)
                        nc.scalar.copy(xT[:, k, :], tp[k][:, :, :].rearrange("p a b -> p (a b)"))\
                          .then_inc(xT_copied, 1)

                def step(i, last):
                    act.wait_ge(pair_free, i + 1)
                    at = bass.ds(i * PER, PER)
                    nc.scalar.copy(place[:, :], places[:, at])
                    nc.scalar.copy(pair[:, :, 0], srci[:, at])
                    nc.scalar.copy(pair[:, :, 1], dsti[:, at]).then_inc(pair_ready, 1)
                    act.wait_ge(scores_ready, i + 1)
                    nc.scalar.activation(wgt[:, :, :], wgt[:, :, :], ACT.Exp).then_inc(exp_ready, 1)
                    for e in range(NE):
                        for l, (pp, hs, ready, done) in enumerate(((h1p, h1s, h1_ready, h1_done),
                                                                   (h2p, h2s, h2_ready, h2_done))):
                            for m in range(KC):
                                act.wait_ge(ready, i * (NE * KC) + e * KC + m + 1)
                                nc.scalar.activation(hs[e % 2][:, m, :], pp[m][:, :], ACT.Relu,
                                                     bias=shift[:, l, e, m:m + 1], scale=scale[:, l, e, m:m + 1])\
                                  .then_inc(done, 1)
                        if e == 1 and not last:
                            root(i + 1)
                    if not last:
                        copy_xT(i + 1)

                root(0)
                copy_xT(0)
                with act.Fori(0, NCH - 1) as i:
                    step(i, False)
                step(NCH - 1, True)

            @block.tensor
            def _(pe):
                pe.wait_ge(w_in, 16 * len(loads))
                def turn(i):
                    pe.wait_ge(xn_ready, i + 1)
                    for k in range(KC):
                        for j in range(CHUNK):
                            mm = nc.tensor.transpose(tp[k][:, j, :], xn[:, j, k * P:(k + 1) * P], K["ident"][:, :])
                        mm.then_inc(xT_ready, 1)

                def layer(pp, ws, e, rhs, ready):
                    for m in range(KC):
                        for k in range(KC):
                            mm = nc.tensor.matmul(pp[m][:, :], ws[:, e, k, m * P:(m + 1) * P], rhs[:, k, :],
                                                  start=(k == 0), stop=(k == KC - 1))
                        mm.then_inc(ready, 1)

                def step(i, last):
                    pe.wait_ge(xT_copied, i * KC + KC)
                    for j in range(CHUNK):
                        for k in range(KC):
                            mm = nc.tensor.matmul(tp[0][:, 0, j * NE:(j + 1) * NE], xT[:, k, j * P:(j + 1) * P],
                                                  wrs[:, k, :], start=(k == 0), stop=(k == KC - 1))
                    mm.then_inc(logits_ready, 1)
                    layer(h1p, w1s, 0, xT, h1_ready)
                    pe.wait_ge(wgt_ready, i + 1)
                    for j in range(CHUNK):
                        mm = nc.tensor.transpose(tp[1][0:NE, j, :], wgt[:, j, :], K["ident"][:, :])
                    mm.then_inc(wT_ready, 1)
                    pe.wait_ge(wT_copied, i + 1)
                    for j in range(CHUNK):
                        if j % 2 == 0:
                            pe.wait_ge(y_used, i * YPC + j // 2 + 1)
                        mm = nc.tensor.matmul(yp[j // 2][:, j % 2, :], wT[:, j, :], bos[:, :], start=True, stop=True)
                        if j % 2:
                            mm.then_inc(y_ready, 1)
                    for e in range(NE):
                        pe.wait_ge(h1_done, i * (NE * KC) + (e + 1) * KC)
                        layer(h2p, w2s, e, h1s[e % 2], h2_ready)
                        if e + 1 < NE:
                            layer(h1p, w1s, e + 1, xT, h1_ready)
                        elif not last:
                            turn(i + 1)
                        pe.wait_ge(h2_done, i * (NE * KC) + (e + 1) * KC)
                        for j in range(CHUNK):
                            if j % 2 == 0:
                                pe.wait_ge(y_used, i * YPC + 2 * (e + 1) + j // 2 + 1)
                            for k in range(KC):
                                mm = nc.tensor.matmul(yp[j // 2][:, j % 2, :], h2s[e % 2][:, k, j * P:(j + 1) * P],
                                                      wos[:, e, k, :], start=(k == 0), stop=(k == KC - 1))
                            if j % 2:
                                mm.then_inc(y_ready, 1)

                turn(0)
                with pe.Fori(0, NCH - 1) as i:
                    step(i, False)
                step(NCH - 1, True)

            @block.vector
            def _(dve):
                link = Link(dve, ch)
                dve.sem_inc(slot_free, 1)
                dve.sem_inc(pair_free, 1)
                dve.sem_inc(y_used, 2)
                dve.wait_ge(root_ready, 1)
                link(nc.vector.reciprocal(scale[:, :, :, :], scale[:, :, :, :]))
                for l in range(2):
                    link(nc.vector.tensor_tensor(scale[:, l, :, :], scale[:, l, :, :], par[:, l, 1, :, :], ALU.mult))
                    link(nc.vector.tensor_tensor(shift[:, l, :, :], par[:, l, 0, :, :], par[:, l, 3, :, :],
                                                 ALU.subtract))
                    link(nc.vector.tensor_tensor(shift[:, l, :, :], shift[:, l, :, :], scale[:, l, :, :], ALU.mult))
                    link(nc.vector.tensor_tensor(shift[:, l, :, :], shift[:, l, :, :], par[:, l, 2, :, :], ALU.add))
                dve.sem_inc(par_ready, 1)
                base = link.n

                def normal(i):
                    link = Link(dve, normalised, i * XLINKS)
                    dve.wait_ge(x_in, i * 16 + 16)
                    normalise(nc, K, dve, link, x, stats, mv, sd, rstd, xn, var_ready, sd_ready, passed, i + 1)\
                        .then_inc(xn_ready, 1)
                    assert link.n == XLINKS

                def step(i, last):
                    link = Link(dve, ch, i * LINKS + base)
                    dve.wait_ge(logits_ready, i + 1)
                    link(nc.vector.tensor_tensor(wgt[:, :, :],
                                                 tp[0][:, 0, 0:CHUNK * NE].rearrange("p (j e) -> p j e", e=NE),
                                                 brs[:, :].unsqueeze(1).to_broadcast([P, CHUNK, NE]), ALU.add))
                    link(nc.vector.tensor_reduce(top[:, :], wgt[:, :, :], AX.X, ALU.max))
                    link(nc.vector.tensor_tensor(wgt[:, :, :], wgt[:, :, :],
                                                 top[:, :].unsqueeze(2).to_broadcast([P, CHUNK, NE]), ALU.subtract))
                    dve.sem_inc(scores_ready, 1)
                    dve.wait_ge(exp_ready, i + 1)
                    link(nc.vector.tensor_reduce(tot[:, :], wgt[:, :, :], AX.X, ALU.add))
                    link(nc.vector.reciprocal(tot[:, :], tot[:, :]))
                    link(nc.vector.tensor_tensor(wgt[:, :, :], wgt[:, :, :],
                                                 tot[:, :].unsqueeze(2).to_broadcast([P, CHUNK, NE]), ALU.mult))
                    dve.sem_inc(wgt_ready, 1)
                    dve.wait_ge(wT_ready, i + 1)
                    nc.vector.tensor_copy(wT[:, :, :], tp[1][0:NE, :, :]).then_inc(wT_copied, 1)
                    for q in range(2):
                        dve.wait_ge(y_ready, i * YPC + q + 1)
                        nc.vector.tensor_tensor(ysum[:, 2 * q:2 * q + 2, :], x[:, 2 * q:2 * q + 2, :], yp[q][:, :, :],
                                                ALU.add).then_inc(y_used, 1)
                    dve.sem_inc(passed, 1)
                    dve.wait_ge(y_used, i * YPC + 4)
                    dve.sem_inc(x_used, 1)
                    for e in range(NE):
                        if e == NE - 1:
                            dve.wait_ge(slot_free, i + 1)
                        dve.wait_ge(y_used, i * YPC + 2 * e + 4)
                        o = y if e == NE - 1 else ysum
                        for q in range(2):
                            dve.wait_ge(y_ready, i * YPC + 2 * (e + 1) + q + 1)
                            for j in range(2 * q, 2 * q + 2):
                                m = nc.vector.scalar_tensor_tensor(out=o[:, j, :], in0=yp[q][:, j % 2, :],
                                                                   scalar=wgt[:, j, e:e + 1], in1=ysum[:, j, :],
                                                                   op0=ALU.mult, op1=ALU.add)
                            m.then_inc(y_used, 1)
                        if e == 0 and not last:
                            normal(i + 1)
                    dve.wait_ge(y_used, (i + 1) * YPC + 2)
                    dve.sem_inc(ysum_ready, 1)
                    assert link.n == LINKS

                normal(0)
                with dve.Fori(0, NCH - 1) as i:
                    step(i, False)
                step(NCH - 1, True)


def sum_small_messages(nc, K, name, cols, H, F, ed, table, out):
    W, D = H + F, F // H
    rows, inner, before = ed["rows"], ed["inner"], ed["before"]
    last, carry = ed["last"], ed["carry"]
    with Ctx(nc, name) as c:
        steps, summed, stored = Link(None, c.sem("steps")), c.sem("summed"), c.sem("stored")
        with nc.Block() as block:

            @block.vector
            def _(dve):
                link = steps.on(dve)
                msg = rows[:, :, H:W].rearrange("p c (h d) -> p c h d", h=H)
                for h in range(H):
                    m = nc.vector.tensor_tensor(msg[:, :, h, :], msg[:, :, h, :],
                                                rows[:, :, h:h + 1].to_broadcast([P, cols, D]), ALU.mult)
                link(m)
                for f in range(W):
                    m = nc.vector.tensor_tensor_scan(rows[:, :, f], inner[:, :], rows[:, :, f], 0.0, ALU.mult, ALU.add)
                link(m)
                link(nc.vector.tensor_copy(last[:, 0:W], rows[:, cols - 1, :]))
        carry_over(nc, K, name + "c", last, ed["inall"], ALU.mult, ALU.add, 0.0, carry, W)
        with nc.Block() as block:

            @block.vector
            def _(dve):
                for f in range(W):
                    m = nc.vector.scalar_tensor_tensor(out=rows[:, :, f], in0=before[:, :], scalar=carry[:, f:f + 1],
                                                       in1=rows[:, :, f], op0=ALU.mult, op1=ALU.add)
                m.then_inc(summed, 1)

            @block.sync
            def _(sp):
                sp.wait_ge(summed, 1)
                sp.dma_start(table.rearrange("(p c) w -> p c w", p=P), rows[:, :, :]).then_inc(stored, 16)
                sp.wait_ge(stored, 16)
        gather_columns(nc, name + "g", table, W, ed["endi"][:, :], out, NB, 7)
        with nc.Block() as block:

            @block.vector
            def _(dve):
                link = steps.on(dve)
                link(nc.vector.tensor_tensor(out, out, ed["has"][:, :].unsqueeze(2).to_broadcast([P, NB, W]),
                                             ALU.mult))


def choose_experts(nc, K, name, sums, H, NE, asn, adn, mn, hn, bias, gamma, beta, gate):
    F = H * NE
    with Ctx(nc, name) as c:
        own = c.sb("own", [P, NB, H])
        den = c.sb("den", [P, NB, H])
        agg = c.sb("agg", [P, NB, F])
        sq = c.sb("sq", [P, NB, F])
        mean, var = c.sb("mean", [P, NB, 1]), c.sb("var", [P, NB, 1])
        par = c.sb("par", [P, 3, F])
        sc = c.sb("sc", [P, NB, NE])
        beat = c.sb("beat", [P, NB, NE])
        one = c.sb("one", [P, NB, NE])
        par_in, score_ready, own_ready, var_ready, sd_ready, top_ready, exp_ready, ch = (
            c.sem(n) for n in ("par_in", "score_ready", "own_ready", "var_ready", "sd_ready", "top_ready",
                               "exp_ready", "ch"))
        with nc.Block() as block:

            @block.sync
            def _(sp):
                for q, a in enumerate((bias, gamma, beta)):
                    sp.dma_start(par[:, q, :], a.partition_broadcast(P)).then_inc(par_in, 16)

            @block.scalar
            def _(act):
                act.wait_ge(score_ready, 1)
                nc.scalar.activation(own[:, :, :], own[:, :, :], ACT.Exp).then_inc(own_ready, 1)
                act.wait_ge(var_ready, 1)
                nc.scalar.activation(var[:, :, :], var[:, :, :], ACT.Sqrt, bias=K["eps"][:, 0:1])\
                  .then_inc(sd_ready, 1)
                act.wait_ge(top_ready, 1)
                nc.scalar.activation(sc[:, :, :], sc[:, :, :], ACT.Exp).then_inc(exp_ready, 1)

            @block.vector
            def _(dve):
                link = Link(dve, ch)
                tt, stt = nc.vector.tensor_tensor, nc.vector.scalar_tensor_tensor
                wide = lambda a, n: a.to_broadcast([P, NB, n])
                param = lambda q: par[:, q, :].unsqueeze(1).to_broadcast([P, NB, F])
                link(tt(own[:, :, :], asn[:, 0:NB, :], adn[:, 0:NB, :], ALU.add))
                link(stt(out=own[:, :, :], in0=own[:, :, :], scalar=SLOPE, in1=own[:, :, :], op0=ALU.mult,
                         op1=ALU.max))
                link(tt(own[:, :, :], own[:, :, :], mn[:, :, :], ALU.subtract))
                dve.sem_inc(score_ready, 1)
                dve.wait_ge(own_ready, 1)
                link(tt(den[:, :, :], own[:, :, :], sums[:, :, 0:H], ALU.add))
                link(nc.vector.tensor_scalar(den[:, :, :], den[:, :, :], 1e-16, None, ALU.add))
                link(nc.vector.reciprocal(den[:, :, :], den[:, :, :]))
                dve.wait_ge(par_in, 48)
                for h in range(H):
                    f = slice(h * NE, (h + 1) * NE)
                    link(tt(agg[:, :, f], hn[:, 0:NB, f], wide(own[:, :, h:h + 1], NE), ALU.mult))
                    link(tt(agg[:, :, f], agg[:, :, f], sums[:, :, H + h * NE:H + (h + 1) * NE], ALU.add))
                    link(tt(agg[:, :, f], agg[:, :, f], wide(den[:, :, h:h + 1], NE), ALU.mult))
                link(tt(agg[:, :, :], agg[:, :, :], param(0), ALU.add))
                link(nc.vector.tensor_reduce(mean[:, :, 0], agg[:, :, :], AX.X, ALU.add))
                link(nc.vector.tensor_scalar(mean[:, :, :], mean[:, :, :], 1.0 / F, None, ALU.mult))
                link(tt(agg[:, :, :], agg[:, :, :], wide(mean[:, :, :], F), ALU.subtract))
                link(tt(sq[:, :, :], agg[:, :, :], agg[:, :, :], ALU.mult))
                link(nc.vector.tensor_reduce(var[:, :, 0], sq[:, :, :], AX.X, ALU.add))
                link(nc.vector.tensor_scalar(var[:, :, :], var[:, :, :], 1.0 / F, None, ALU.mult))
                dve.sem_inc(var_ready, 1)
                dve.wait_ge(sd_ready, 1)
                link(nc.vector.reciprocal(var[:, :, :], var[:, :, :]))
                link(tt(agg[:, :, :], agg[:, :, :], wide(var[:, :, :], F), ALU.mult))
                link(tt(agg[:, :, :], agg[:, :, :], param(1), ALU.mult))
                link(tt(agg[:, :, :], agg[:, :, :], param(2), ALU.add))
                link(nc.vector.tensor_reduce(sc[:, :, :], agg[:, :, :].rearrange("p b (h e) -> p b e h", h=H),
                                             AX.X, ALU.add))
                link(nc.vector.tensor_scalar(sc[:, :, :], sc[:, :, :], 1.0 / H, None, ALU.mult))
                link(nc.vector.memset(beat[:, :, :], 0.0))
                for j in range(NE):
                    if j + 1 < NE:
                        n = NE - j - 1
                        link(tt(one[:, :, j + 1:NE], sc[:, :, j + 1:NE], wide(sc[:, :, j:j + 1], n), ALU.is_le))
                        link(tt(beat[:, :, j + 1:NE], beat[:, :, j + 1:NE], one[:, :, j + 1:NE], ALU.add))
                    if j:
                        link(tt(one[:, :, 0:j], sc[:, :, 0:j], wide(sc[:, :, j:j + 1], j), ALU.is_lt))
                        link(tt(beat[:, :, 0:j], beat[:, :, 0:j], one[:, :, 0:j], ALU.add))
                link(nc.vector.tensor_scalar(beat[:, :, :], beat[:, :, :], 2.0, None, ALU.is_lt))
                link(nc.vector.tensor_reduce(mean[:, :, 0], sc[:, :, :], AX.X, ALU.max))
                link(tt(sc[:, :, :], sc[:, :, :], wide(mean[:, :, :], NE), ALU.subtract))
                dve.sem_inc(top_ready, 1)
                dve.wait_ge(exp_ready, 1)
                link(tt(sc[:, :, :], sc[:, :, :], beat[:, :, :], ALU.mult))
                link(nc.vector.tensor_reduce(mean[:, :, 0], sc[:, :, :], AX.X, ALU.add))
                link(nc.vector.reciprocal(mean[:, :, :], mean[:, :, :]))
                link(nc.vector.memset(gate[:, :, :], 0.0))
                link(tt(gate[:, 0:NB, :], sc[:, :, :], wide(mean[:, :, :], NE), ALU.mult))


def expert_outputs(nc, K, name, xin, z, w1, b1, w2, b2, gather):
    NE, _, HID = w1.shape
    HC = HID // P
    NT = CHUNK * P
    LINKS = 2
    with Ctx(nc, name) as c:
        gather = Gather(nc, c, *gather)
        AHEAD = -(-(gather.pairs - 1) // NCH)
        GSTEPS = (gather.pairs - 1) // AHEAD
        assert AHEAD <= NE and GSTEPS < NCH
        w1s = c.sb("w1s", [P, NE, KC, HID])
        w2s = c.sb("w2s", [P, NE, HC, DIM])
        b1s, b2s = c.sb("b1s", [P, NE, HC]), c.sb("b2s", [P, NE, DIM])
        x, xn = (c.sb(n, [P, CHUNK, DIM]) for n in ("x", "xn"))
        zs = [c.sb(f"zs{j}", [P, CHUNK, DIM]) for j in range(2)]
        xT = c.sb("xT", [P, KC, NT])
        hs = [c.sb(f"hs{j}", [P, HC, NT]) for j in range(2)]
        stats, mv = c.sb("stats", [P, CHUNK, 6]), c.sb("mv", [P, CHUNK, 2])
        sd, rstd = c.sb("sd", [P, CHUNK, 1]), c.sb("rstd", [P, CHUNK, 1])
        hp = [c.ps(f"hp{m}", [P, NT]) for m in range(HC)]
        yp = [c.ps(f"yp{m}", [P, 2, DIM]) for m in range(2)]
        tp = [c.ps(f"tp{m}", [P, CHUNK, P]) for m in range(2)]
        names = ("w_in", "x_in", "var_ready", "sd_ready", "xn_ready", "xT_ready", "xT_copied", "h_ready", "h_done",
                 "y_ready", "y_used", "z_ready", "z_free", "stored", "passed", "ch")
        (w_in, x_in, var_ready, sd_ready, xn_ready, xT_ready, xT_copied, h_ready, h_done, y_ready, y_used, z_ready,
         z_free, stored, passed, ch) = (c.sem(n) for n in names)
        xv = xin.rearrange("(b p) d -> p b d", p=P)
        zv = z.rearrange("(b p) f -> p b f", p=P)
        loads = [(b2s[:, :, :].rearrange("p e d -> p (e d)"), b2.rearrange("e d -> (e d)").partition_broadcast(P))]
        for e in range(NE):
            loads += [(w1s[:, e, :, :], w1[e].rearrange("(k p) h -> p k h", p=P)),
                      (w2s[:, e, :, :], w2[e].rearrange("(k p) h -> p k h", p=P)),
                      (b1s[:, e, :], b1[e].rearrange("(k p) -> p k", p=P))]
        with nc.Block() as block:

            @block.sync
            def _(sp):
                sp.dma_start(x[:, :, :], xv[:, 0:CHUNK, :]).then_inc(x_in, 16)
                with nc.allow_non_contiguous_dma("features of a bias go to the partitions"):
                    for o, a in loads:
                        sp.dma_start(o, a).then_inc(w_in, 16)

                def step(i, last):
                    if not last:
                        sp.wait_ge(xn_ready, i + 1)
                        sp.dma_start(x[:, :, :], xv[:, bass.ds(i * CHUNK + CHUNK, CHUNK), :]).then_inc(x_in, 16)
                    for e in range(NE):
                        sp.wait_ge(z_ready, i * NE + e + 1)
                        sp.dma_start(zv[:, bass.ds(i * CHUNK, CHUNK), e * DIM:(e + 1) * DIM], zs[e % 2][:, :, :])\
                          .then_inc(stored, 16)
                        sp.wait_ge(stored, i * (16 * NE) + 16 * (e + 1))
                        sp.sem_inc(z_free, 1)

                with sp.Fori(0, NCH - 1) as i:
                    step(i, False)
                step(NCH - 1, True)

            @block.gpsimd
            def _(pool):
                gather.issue(pool)

            @block.scalar
            def _(act):
                def root(i):
                    act.wait_ge(var_ready, i + 1)
                    nc.scalar.activation(sd[:, :, :], mv[:, :, 1:2], ACT.Sqrt, bias=K["eps"][:, 0:1])\
                      .then_inc(sd_ready, 1)

                def copy_xT(i):
                    for k in range(KC):
                        act.wait_ge(xT_ready, i * KC + k + 1)
                        nc.scalar.copy(xT[:, k, :], tp[k][:, :, :].rearrange("p a b -> p (a b)"))\
                          .then_inc(xT_copied, 1)

                def step(i, advances, last):
                    for e in range(NE):
                        for m in range(HC):
                            act.wait_ge(h_ready, i * (NE * HC) + e * HC + m + 1)
                            nc.scalar.activation(hs[e % 2][:, m, :], hp[m][:, :], ACT.Gelu, bias=b1s[:, e, m:m + 1])\
                              .then_inc(h_done, 1)
                        if e < advances:
                            gather.advance(act, i * AHEAD + e)
                        if e == 1 and not last:
                            root(i + 1)
                    if not last:
                        copy_xT(i + 1)

                for h in range(2):
                    gather.stage(h, h)
                act.wait_ge(w_in, 16 * len(loads))
                root(0)
                copy_xT(0)
                with act.Fori(0, GSTEPS) as i:
                    step(i, AHEAD, False)
                left = gather.pairs - 1 - GSTEPS * AHEAD
                step(GSTEPS, left, GSTEPS == NCH - 1)
                if GSTEPS + 1 < NCH - 1:
                    with act.Fori(GSTEPS + 1, NCH - 1) as i:
                        step(i, 0, False)
                if GSTEPS < NCH - 1:
                    step(NCH - 1, 0, True)
                for h in range(2):
                    gather.take(act, h, gather.pairs - 1)

            @block.tensor
            def _(pe):
                def turn(i):
                    pe.wait_ge(xn_ready, i + 1)
                    for k in range(KC):
                        for j in range(CHUNK):
                            mm = nc.tensor.transpose(tp[k][:, j, :], xn[:, j, k * P:(k + 1) * P], K["ident"][:, :])
                        mm.then_inc(xT_ready, 1)

                def hidden(i, e):
                    for m in range(HC):
                        pe.wait_ge(h_done, i * (NE * HC) + e * HC + m + 1)
                        for k in range(KC):
                            mm = nc.tensor.matmul(hp[m][:, :], w1s[:, e, k, m * P:(m + 1) * P], xT[:, k, :],
                                                  start=(k == 0), stop=(k == KC - 1))
                        mm.then_inc(h_ready, 1)

                def step(i, last):
                    pe.wait_ge(xT_copied, i * KC + KC)
                    hidden(i, 0)
                    for e in range(NE):
                        if e + 1 < NE:
                            hidden(i, e + 1)
                        elif not last:
                            turn(i + 1)
                        pe.wait_ge(h_done, i * (NE * HC) + (e + 2) * HC)
                        for j in range(CHUNK):
                            if j % 2 == 0:
                                pe.wait_ge(y_used, i * (2 * NE) + 2 * e + j // 2 + 1)
                            for k in range(HC):
                                mm = nc.tensor.matmul(yp[j // 2][:, j % 2, :], hs[e % 2][:, k, j * P:(j + 1) * P],
                                                      w2s[:, e, k, :], start=(k == 0), stop=(k == HC - 1))
                            if j % 2:
                                mm.then_inc(y_ready, 1)

                pe.wait_ge(w_in, 16 * len(loads))
                turn(0)
                with pe.Fori(0, NCH - 1) as i:
                    step(i, False)
                step(NCH - 1, True)

            @block.vector
            def _(dve):
                dve.sem_inc(h_done, HC)
                dve.sem_inc(y_used, 2)
                dve.sem_inc(z_free, 2)
                dve.wait_ge(w_in, 16 * len(loads))

                def normal(i):
                    link = Link(dve, ch, i * LINKS)
                    dve.wait_ge(x_in, i * 16 + 16)
                    normalise(nc, K, dve, link, x, stats, mv, sd, rstd, xn, var_ready, sd_ready, passed, i + 1)\
                        .then_inc(xn_ready, 1)
                    assert link.n == LINKS

                def step(i, last):
                    for e in range(NE):
                        dve.wait_ge(z_free, i * NE + e + 1)
                        for q in range(2):
                            dve.wait_ge(y_ready, i * (2 * NE) + 2 * e + q + 1)
                            nc.vector.tensor_tensor(zs[e % 2][:, 2 * q:2 * q + 2, :], yp[q][:, :, :],
                                                    b2s[:, e, :].unsqueeze(1).to_broadcast([P, 2, DIM]), ALU.add)\
                              .then_inc(y_used, 1)
                        dve.wait_ge(y_used, i * (2 * NE) + 2 * e + 4)
                        dve.sem_inc(z_ready, 1)
                        if e == 0 and not last:
                            normal(i + 1)

                normal(0)
                with dve.Fori(0, NCH - 1) as i:
                    step(i, False)
                step(NCH - 1, True)


def gated_sum(nc, K, name, xin, z, NE, gate, out):
    N, SLOTS = NB // 2, 4
    T = N // SLOTS
    REST = NODES - (NB - 1) * P
    assert NB % 2 == 0 and N % SLOTS == 1 and REST > 0
    LINKS = 1 + NE
    with Ctx(nc, name) as c:
        x = [c.sb(f"x{s}", [P, 2, DIM]) for s in range(SLOTS)]
        zs = [c.sb(f"zs{s}", [P, 2, NE * DIM]) for s in range(SLOTS)]
        y = [c.sb(f"y{h}", [P, 2, DIM]) for h in range(2)]
        wgt = c.sb("wgt", [P, 2, NE])
        ysum = c.sb("ysum", [P, 2, DIM])
        done, slot_free, stored, ch = (c.sem(n) for n in ("done", "slot_free", "stored", "ch"))
        x_in = [c.sem(f"x_in{s}") for s in range(SLOTS)]
        xv, zv = xin.rearrange("(b p) d -> p b d", p=P), z.rearrange("(b p) f -> p b f", p=P)
        ov = out[0:(NB - 2) * P, :].rearrange("(b p) d -> p b d", p=P)
        with nc.Block() as block:

            @block.sync
            def _(sp):
                def load(s, n):
                    b = bass.ds(n * 2, 2)
                    sp.dma_start(x[s][:, :, :], xv[:, b, :]).then_inc(x_in[s], 16)
                    sp.dma_start(zs[s][:, :, :], zv[:, b, :]).then_inc(x_in[s], 16)

                for s in range(SLOTS):
                    load(s, s)
                with sp.Fori(0, T - 1) as i:
                    for s in range(SLOTS):
                        sp.wait_ge(done, i * SLOTS + s + 1)
                        load(s, i * SLOTS + s + SLOTS)
                sp.wait_ge(done, N - SLOTS)
                load(0, N - 1)

            @block.gpsimd
            def _(pool):
                with pool.Fori(0, N // 2) as i:
                    for h in range(2):
                        n = i * 2 + h
                        pool.wait_ge(done, n + 1)
                        pool.dma_start(ov[:, bass.ds(n * 2, 2), :], y[h][:, :, :]).then_inc(stored, 16)
                        pool.wait_ge(stored, n * 16 + 16)
                        pool.sem_inc(slot_free, 1)
                pool.wait_ge(done, N)
                pool.dma_start(out[(NB - 2) * P:(NB - 1) * P, :], y[0][:, 0, :]).then_inc(stored, 16)
                pool.dma_start(out[(NB - 1) * P:NODES, :], y[0][0:REST, 1, :]).then_inc(stored, 16)
                pool.wait_ge(stored, N * 16 + 16)

            @block.vector
            def _(dve):
                dve.sem_inc(slot_free, 2)

                def add(n, s, turn):
                    link = Link(dve, ch, n * LINKS)
                    dve.wait_ge(x_in[s], turn * 32 + 32)
                    at = gate[:, bass.ds(n * 2, 2), :]
                    link(nc.vector.tensor_tensor(wgt[:, :, :], at, at, ALU.max))
                    dve.wait_ge(slot_free, n + 1)
                    for e in range(NE):
                        for j in range(2):
                            before = x[s] if e == 0 else ysum
                            o = y[s % 2] if e == NE - 1 else ysum
                            m = nc.vector.scalar_tensor_tensor(out=o[:, j, :], in0=zs[s][:, j, e * DIM:(e + 1) * DIM],
                                                               scalar=wgt[:, j, e:e + 1], in1=before[:, j, :],
                                                               op0=ALU.mult, op1=ALU.add)
                        link(m)
                    dve.sem_inc(done, 1)
                    assert link.n == LINKS

                with dve.Fori(0, T) as i:
                    for s in range(SLOTS):
                        add(i * SLOTS + s, s, i)
                add(N - 1, 0, T)


def graph_attention(nc, K, name, H, edges, xp, xout, w, att_src, att_dst, bias, norm, tables,
                    beside=None):
    cols, tiles, pairs, start, count, blk = edges
    htab, atab, scratch, records = tables
    with Ctx(nc, name) as c:
        asn, adn = c.sb("asn", [P, NCH * CHUNK, H]), c.sb("adn", [P, NCH * CHUNK, H])
        mn = c.sb("mn", [P, NB, H])
        node_tables(nc, K, name + "nt", xp, w, DIM, H, att_src, att_dst, htab, atab, asn, adn, None)
        with Ctx(nc, name + "ed") as e:
            ed = edge_weights(nc, K, e, name + "ew", cols, H, atab, H, pairs, start, count, asn, adn, mn, scratch,
                              beside)
            edge_records(nc, K, name + "er", cols, H, ed, records)
        with Ctx(nc, name + "ac") as e:
            acc = e.sb("acc", [P, NB, DIM + H])
            sum_messages(nc, K, name + "sm", tiles, H, htab, records, blk, acc)
            finish_attention(nc, K, name + "fa", acc, H, htab, asn, adn, mn, xp, xout, bias, norm)


def gnn_two_layers(nc, a, out):
    def dram(name, shape, dt=F32):
        return nc.dram_tensor(name, shape, dt).ap()

    with Ctx(nc, "k") as c:
        K = make_constants(nc, c)
        xs = [dram(f"x{j}", (ROWS, DIM)) for j in range(4)]
        pad_rows(nc, "pad", a["x"], xs[0], [xs[1], xs[3]])
        router = a["L1_ffn_edge_index"]
        RE = router.shape[1]
        rtiles = -(-RE // (P * BODY)) * BODY
        rcols = RE // P
        assert RE == P * rcols
        rpairs = dram("rpairs", (1 + RE, 2), I32)
        rstart, rcount = c.sb("rstart", [P, NB]), c.sb("rcount", [P, NB])
        with Ctx(nc, "g") as g:
            E = a["src"].shape[0]
            most = -(-E // P) + NB
            tiles = -(-most // TURN) * TURN
            cols = -(-(tiles + TURN) // P) * P
            pairs = dram("pairs", (1 + P * cols, 2), I32)
            start, count = g.sb("start", [P, NB]), g.sb("count", [P, NB])
            blk = g.sb("blk", [1, cols], I32)
            sort_edges(nc, K, "sg", a["src"], a["dst"], cols, True, start, count, pairs, blk)
            htab = dram("htab", (ROWS, DIM))

            def attend(layer, norm, beside):
                H = a[f"L{layer}_gnn_att_src"].shape[0]
                tables = (htab, dram(f"atab{layer}", (ROWS, H)),
                          edge_tables(nc, f"edges{layer}", P * cols, H),
                          dram(f"records{layer}", (P, cols * (H + 2))))
                p = f"L{layer}_gnn_"
                graph_attention(nc, K, f"g{layer}", H, (cols, tiles, pairs, start, count, blk), xs[2 * layer],
                                xs[2 * layer + 1], a[p + "W"], a[p + "att_src"], a[p + "att_dst"], a[p + "bias"],
                                norm, tables, beside)

            with Ctx(nc, "q") as q:
                per = places_per_step(rtiles)
                srci, dsti = q.sb("srci", [P, per * NCH], I32), q.sb("dsti", [P, per * NCH], I32)
                places = q.sb("places", [P, max(per * NCH, rtiles + HALF)], I32)
                attend(0, None, lambda gather: sort_edges(
                    nc, K, "sr", router[0, :], router[1, :], rcols, False, rstart, rcount, rpairs,
                    beside=(srci, dsti, places, gather)))
                f = "L0_ffn_"
                mix_experts(nc, K, "f0", xs[1], xs[2], a[f + "Wr"], a[f + "br"], a[f + "W1"], a[f + "b1"],
                            tuple(a[f + n] for n in ("g1", "be1", "m1", "v1")), a[f + "W2"], a[f + "b2"],
                            tuple(a[f + n] for n in ("g2", "be2", "m2", "v2")), a[f + "Wo"], a[f + "bo"],
                            (srci, dsti, places, rpairs, RE))
            attend(1, (a["L1_gnn_gamma"], a["L1_gnn_beta"]), None)
        with Ctx(nc, "r") as r:
            f = "L1_ffn_"
            H, NE = a[f + "att_src"].shape
            F = H * NE
            z = dram("z", (ROWS, NE * DIM))
            gate = r.sb("gate", [P, NCH * CHUNK, NE])
            with Ctx(nc, "rn") as n:
                asn, adn = n.sb("asn", [P, NCH * CHUNK, H]), n.sb("adn", [P, NCH * CHUNK, H])
                mn = n.sb("mn", [P, NB, H])
                hn = n.sb("hn", [P, NCH * CHUNK, F])
                sums = n.sb("sums", [P, NB, H + F])
                table = dram("rtab", (ROWS, H + F))
                node_tables(nc, K, "rt", xs[3], a[f + "W_gat"], F, H, a[f + "att_src"], a[f + "att_dst"], None, table,
                            asn, adn, hn)
                with Ctx(nc, "re") as e:
                    ed = edge_weights(nc, K, e, "rw", rcols, H, table, H + F, rpairs, rstart, rcount, asn, adn, mn,
                                      edge_tables(nc, "redges", RE, H),
                                      lambda gather: expert_outputs(nc, K, "f1", xs[3], z, a[f + "W1"], a[f + "b1"],
                                                                    a[f + "W2"], a[f + "b2"], gather))
                    sum_small_messages(nc, K, "rs", rcols, H, F, ed, dram("rsum", (RE, H + F)), sums[:, :, :])
                choose_experts(nc, K, "rc", sums, H, NE, asn, adn, mn, hn, a[f + "b_gat"], a[f + "ln_gamma"],
                               a[f + "ln_beta"], gate)
            gated_sum(nc, K, "gs", xs[3], z, NE, gate, out)


_INS = ['x', 'src', 'dst', 'L0_gnn_W', 'L0_gnn_att_src', 'L0_gnn_att_dst', 'L0_gnn_bias', 'L0_ffn_Wr', 'L0_ffn_br',
        'L0_ffn_W1', 'L0_ffn_b1', 'L0_ffn_g1', 'L0_ffn_be1', 'L0_ffn_m1', 'L0_ffn_v1', 'L0_ffn_W2', 'L0_ffn_b2',
        'L0_ffn_g2', 'L0_ffn_be2', 'L0_ffn_m2', 'L0_ffn_v2', 'L0_ffn_Wo', 'L0_ffn_bo', 'L1_gnn_W', 'L1_gnn_att_src',
        'L1_gnn_att_dst', 'L1_gnn_bias', 'L1_gnn_gamma', 'L1_gnn_beta', 'L1_ffn_W_gat', 'L1_ffn_att_src',
        'L1_ffn_att_dst', 'L1_ffn_b_gat', 'L1_ffn_ln_gamma', 'L1_ffn_ln_beta', 'L1_ffn_W1', 'L1_ffn_b1', 'L1_ffn_W2',
        'L1_ffn_b2', 'L1_ffn_edge_index']


def kernel(**inputs):
    import numpy as _np
    import concourse.bacc as _bacc
    from concourse import mybir as _mybir
    from concourse.bass_utils import run_bass_kernel_spmd as _run

    nc = _bacc.Bacc("TRN2", target_bir_lowering=False, num_devices=1)
    arrays, args = {}, {}
    for name in _INS:
        a = _np.ascontiguousarray(inputs[name])
        arrays[f"in_{name}_dram"] = a
        args[name] = nc.dram_tensor(f"in_{name}_dram", a.shape, _mybir.dt.from_np(a.dtype),
                                    kind="ExternalInput").ap()
    out = nc.dram_tensor("out_0_dram", (NODES, DIM), F32, kind="ExternalOutput").ap()
    gnn_two_layers(nc, args, out)
    r = _run(nc, [arrays], core_ids=[0])
    return r.results[0]["out_0_dram"]
```
